# Optimizing a Trainium2 kernel written in Bass

```python
import numpy as np
import jax
import jax.numpy as jnp

def _softmax(x, axis=-1):
    return jax.nn.softmax(x, axis=axis)

def _gelu(x):
    return jax.nn.gelu(x, approximate=True)

def _silu(x):
    return jax.nn.silu(x)

def _sigmoid(x):
    return jax.nn.sigmoid(x)

def _layernorm(x, axis=-1, eps=1e-05):
    m = jnp.mean(x, axis=axis, keepdims=True)
    v = jnp.var(x, axis=axis, keepdims=True)
    return (x - m) / jnp.sqrt(v + eps)

def _scatter_add(tgt, idx, src, axis=0):
    return tgt.at[idx].add(src)

def _segment_sum(src, seg, n):
    return jax.ops.segment_sum(src, seg, n)
kernel_name = 'mk_gnn_resnorm_d4_gnn_r32_5e09a2'

def setup_inputs(seed: int=0):
    np.random.seed(seed)
    _w = jnp.asarray

    def _rec_inputs():
        import jax
        import jax.numpy as jnp
        _gk = jax.random.key(seed)
        x = -0.0005121 + 1.001 * jax.random.normal(jax.random.fold_in(_gk, 1), (3125, 128), jnp.float32)
        src = jax.random.randint(jax.random.fold_in(_gk, 2), (50000,), 0, 3125, jnp.int32)
        dst = jax.random.randint(jax.random.fold_in(_gk, 3), (50000,), 0, 3125, jnp.int32)
        _o = jnp.argsort(dst, stable=True)
        src = src[_o]
        dst = dst[_o]
        edge_attr_128 = 0.000189758 + 1.00013 * jax.random.normal(jax.random.fold_in(_gk, 13), (50000, 128), jnp.float32)
        return (x, src, dst, edge_attr_128)
    x, src, dst, edge_attr_128 = _rec_inputs()

    def _L0_gnn_setup():
        import jax, jax.numpy as jnp
        import numpy as np
        HIDDEN = 256

        def _segment_mean(src, seg_ids, num_segments):
            s = jax.ops.segment_sum(src, seg_ids, num_segments=num_segments)
            cnt = jax.ops.segment_sum(jnp.ones((src.shape[0],), src.dtype), seg_ids, num_segments=num_segments)
            return s / jnp.maximum(cnt, 1.0)[:, None]
        key = jax.random.key(seed)
        ks = jax.random.split(key, 12)
        N, E = (25000, 12500)
        F_NODE, F_EDGE, F_OUT = (128, 128, 128)
        x = jax.random.normal(ks[0], (N, F_NODE), jnp.float32)
        edge_index = jax.random.randint(ks[1], (2, E), 0, N, jnp.int64)
        edge_attr = jax.random.normal(ks[2], (E, F_EDGE), jnp.float32)
        u = jax.random.normal(ks[3], (1, 64), jnp.float32)
        batch = jnp.zeros((N,), jnp.int64)
        s1 = 1.0 / np.sqrt(F_NODE + F_EDGE)
        s2 = 1.0 / np.sqrt(HIDDEN)
        s3 = 1.0 / np.sqrt(F_NODE + HIDDEN)
        W1a = jax.random.uniform(ks[4], (F_NODE + F_EDGE, HIDDEN), jnp.float32, -s1, s1)
        b1a = jax.random.uniform(ks[5], (HIDDEN,), jnp.float32, -s1, s1)
        W1b = jax.random.uniform(ks[6], (HIDDEN, HIDDEN), jnp.float32, -s2, s2)
        b1b = jax.random.uniform(ks[7], (HIDDEN,), jnp.float32, -s2, s2)
        W2a = jax.random.uniform(ks[8], (F_NODE + HIDDEN, HIDDEN), jnp.float32, -s3, s3)
        b2a = jax.random.uniform(ks[9], (HIDDEN,), jnp.float32, -s3, s3)
        W2b = jax.random.uniform(ks[10], (HIDDEN, F_OUT), jnp.float32, -s2, s2)
        b2b = jax.random.uniform(ks[11], (F_OUT,), jnp.float32, -s2, s2)
        return {'x': x, 'edge_index': edge_index, 'edge_attr': edge_attr, 'u': u, 'batch': batch, 'W1a': W1a, 'b1a': b1a, 'W1b': W1b, 'b1b': b1b, 'W2a': W2a, 'b2a': b2a, 'W2b': W2b, 'b2b': b2b}
    _L0_gnn_all = _L0_gnn_setup()
    _L0_gnn_in = {k: v for k, v in _L0_gnn_all.items() if k in ('u', 'W1a', 'b1a', 'W1b', 'b1b', 'W2a', 'b2a', 'W2b', 'b2b')}
    del _L0_gnn_all

    def _L1_gnn_setup():
        import jax, jax.numpy as jnp
        import numpy as np
        N = 50000
        E = 25000
        IN_C = 128
        HID = 128
        HEADS = 4
        NEG_SLOPE = 0.2

        def _gat_conv(x, src, dst, W, att_src, att_dst, bias, heads, out_c):
            n = x.shape[0]
            h = (x @ W).reshape(n, heads, out_c)
            a_src = jnp.einsum('nhc,hc->nh', h, att_src)
            a_dst = jnp.einsum('nhc,hc->nh', h, att_dst)
            e = jax.nn.leaky_relu(a_src[src] + a_dst[dst], NEG_SLOPE)
            m = jax.ops.segment_max(e, dst, num_segments=n)
            p = jnp.exp(e - m[dst])
            denom = jax.ops.segment_sum(p, dst, num_segments=n)
            alpha = p / (denom[dst] + 1e-16)
            msg = h[src] * alpha[:, :, None]
            out = jax.ops.segment_sum(msg, dst, num_segments=n)
            return out.reshape(n, heads * out_c) + bias
        key = jax.random.key(seed)
        ks = jax.random.split(key, 10)
        out_c = HID // HEADS
        glorot = lambda k, shape: jax.random.normal(k, shape, jnp.float32) * np.sqrt(2.0 / (shape[0] + shape[-1]))
        return {'x': jax.random.normal(ks[0], (N, IN_C), jnp.float32), 'edge_index': jax.random.randint(ks[1], (2, E), 0, N, jnp.int64), 'W1': glorot(ks[2], (IN_C, HEADS * out_c)), 'att_src1': glorot(ks[3], (HEADS, out_c)), 'att_dst1': glorot(ks[4], (HEADS, out_c)), 'b1': jnp.zeros((HID,), jnp.float32), 'W2': glorot(ks[5], (HID, HID)), 'att_src2': glorot(ks[6], (1, HID)), 'att_dst2': glorot(ks[7], (1, HID)), 'b2': jnp.zeros((HID,), jnp.float32)}
    _L1_gnn_all = _L1_gnn_setup()
    _L1_gnn_in = {k: v for k, v in _L1_gnn_all.items() if k in ('W1', 'att_src1', 'att_dst1', 'b1', 'W2', 'att_src2', 'att_dst2', 'b2')}
    del _L1_gnn_all

    def _L2_gnn_setup():
        import jax, jax.numpy as jnp
        import numpy as np
        N_NODES = 50000
        N_EDGES = 25000
        D_IN, D_HID, D_OUT = (128, 256, 128)
        key = jax.random.key(seed)
        ks = jax.random.split(key, 12)
        inp = {'x': jax.random.normal(ks[0], (N_NODES, D_IN), dtype=jnp.float32), 'edge_src': jax.random.randint(ks[1], (N_EDGES,), 0, N_NODES, dtype=jnp.int32), 'edge_dst': jax.random.randint(ks[2], (N_EDGES,), 0, N_NODES, dtype=jnp.int32)}

        def lin(k, fi, fo):
            return jax.random.normal(k, (fi, fo), dtype=jnp.float32) * (1.0 / np.sqrt(fi))
        inp['Ws0'] = lin(ks[3], D_IN, D_HID)
        inp['Wn0'] = lin(ks[4], D_IN, D_HID)
        inp['b0'] = jnp.zeros((D_HID,), jnp.float32)
        inp['Ws1'] = lin(ks[5], D_HID, D_HID)
        inp['Wn1'] = lin(ks[6], D_HID, D_HID)
        inp['b1'] = jnp.zeros((D_HID,), jnp.float32)
        inp['Ws2'] = lin(ks[7], D_HID, D_OUT)
        inp['Wn2'] = lin(ks[8], D_HID, D_OUT)
        inp['b2'] = jnp.zeros((D_OUT,), jnp.float32)
        return inp
    _L2_gnn_all = _L2_gnn_setup()
    _L2_gnn_in = {k: v for k, v in _L2_gnn_all.items() if k in ('Ws0', 'Wn0', 'b0', 'Ws1', 'Wn1', 'b1', 'Ws2', 'Wn2', 'b2')}
    del _L2_gnn_all

    def _L3_gnn_setup():
        import jax, jax.numpy as jnp
        import numpy as np
        N_NODES = 50000
        N_EDGES = 18750
        D = 128
        key = jax.random.key(seed)
        k1, k2, k3, k4, k5 = jax.random.split(key, 5)
        node_feats = jax.random.normal(k1, (N_NODES, D), dtype=jnp.float32)
        edge_feats = jax.random.normal(k2, (N_EDGES, D), dtype=jnp.float32)
        mlp_w = jax.random.normal(k3, (D, D), dtype=jnp.float32) * (1.0 / np.sqrt(D))
        mlp_b = jnp.zeros((D,), dtype=jnp.float32)
        scale = jnp.ones((D,), dtype=jnp.float32) * 0.1
        src = jax.random.randint(k4, (N_EDGES,), 0, N_NODES, dtype=jnp.int64)
        dst = jax.random.randint(k5, (N_EDGES,), 0, N_NODES, dtype=jnp.int64)
        return {'node_feats': node_feats, 'edge_feats': edge_feats, 'mlp_w': mlp_w, 'mlp_b': mlp_b, 'scale': scale, 'src': src, 'dst': dst}
    _L3_gnn_all = _L3_gnn_setup()
    _L3_gnn_in = {k: v for k, v in _L3_gnn_all.items() if k in ('mlp_w', 'mlp_b', 'scale')}
    del _L3_gnn_all
    return {'x': x, 'src': src, 'dst': dst, 'edge_attr_128': edge_attr_128, 'L0_gnn_u': _L0_gnn_in['u'], 'L0_gnn_W1a': _L0_gnn_in['W1a'], 'L0_gnn_b1a': _L0_gnn_in['b1a'], 'L0_gnn_W1b': _L0_gnn_in['W1b'], 'L0_gnn_b1b': _L0_gnn_in['b1b'], 'L0_gnn_W2a': _L0_gnn_in['W2a'], 'L0_gnn_b2a': _L0_gnn_in['b2a'], 'L0_gnn_W2b': _L0_gnn_in['W2b'], 'L0_gnn_b2b': _L0_gnn_in['b2b'], 'L1_gnn_W1': _L1_gnn_in['W1'], 'L1_gnn_att_src1': _L1_gnn_in['att_src1'], 'L1_gnn_att_dst1': _L1_gnn_in['att_dst1'], 'L1_gnn_b1': _L1_gnn_in['b1'], 'L1_gnn_W2': _L1_gnn_in['W2'], 'L1_gnn_att_src2': _L1_gnn_in['att_src2'], 'L1_gnn_att_dst2': _L1_gnn_in['att_dst2'], 'L1_gnn_b2': _L1_gnn_in['b2'], 'L2_gnn_Ws0': _L2_gnn_in['Ws0'], 'L2_gnn_Wn0': _L2_gnn_in['Wn0'], 'L2_gnn_b0': _L2_gnn_in['b0'], 'L2_gnn_Ws1': _L2_gnn_in['Ws1'], 'L2_gnn_Wn1': _L2_gnn_in['Wn1'], 'L2_gnn_b1': _L2_gnn_in['b1'], 'L2_gnn_Ws2': _L2_gnn_in['Ws2'], 'L2_gnn_Wn2': _L2_gnn_in['Wn2'], 'L2_gnn_b2': _L2_gnn_in['b2'], 'L3_gnn_mlp_w': _L3_gnn_in['mlp_w'], 'L3_gnn_mlp_b': _L3_gnn_in['mlp_b'], 'L3_gnn_scale': _L3_gnn_in['scale']}

def reference(x, src, dst, edge_attr_128, L0_gnn_u, L0_gnn_W1a, L0_gnn_b1a, L0_gnn_W1b, L0_gnn_b1b, L0_gnn_W2a, L0_gnn_b2a, L0_gnn_W2b, L0_gnn_b2b, L1_gnn_W1, L1_gnn_att_src1, L1_gnn_att_dst1, L1_gnn_b1, L1_gnn_W2, L1_gnn_att_src2, L1_gnn_att_dst2, L1_gnn_b2, L2_gnn_Ws0, L2_gnn_Wn0, L2_gnn_b0, L2_gnn_Ws1, L2_gnn_Wn1, L2_gnn_b1, L2_gnn_Ws2, L2_gnn_Wn2, L2_gnn_b2, L3_gnn_mlp_w, L3_gnn_mlp_b, L3_gnn_scale):
    import jax
    import jax.numpy as jnp

    def _L0_gnn_ref(x, edge_index, edge_attr, u, batch, W1a, b1a, W1b, b1b, W2a, b2a, W2b, b2b):
        import jax, jax.numpy as jnp
        import numpy as np
        HIDDEN = 256

        def _segment_mean(src, seg_ids, num_segments):
            s = jax.ops.segment_sum(src, seg_ids, num_segments=num_segments)
            cnt = jax.ops.segment_sum(jnp.ones((src.shape[0],), src.dtype), seg_ids, num_segments=num_segments)
            return s / jnp.maximum(cnt, 1.0)[:, None]
        row, col = (edge_index[0], edge_index[1])
        h = jnp.concatenate([x[row], edge_attr], axis=1)
        h = jax.nn.elu(h @ W1a + b1a) @ W1b + b1b
        agg = _segment_mean(h, col, x.shape[0])
        z = jnp.concatenate([x, agg], axis=1)
        return jax.nn.elu(z @ W2a + b2a) @ W2b + b2b

    def _L1_gnn_ref(x, edge_index, W1, att_src1, att_dst1, b1, W2, att_src2, att_dst2, b2):
        import jax, jax.numpy as jnp
        import numpy as np
        N = 50000
        E = 25000
        IN_C = 128
        HID = 128
        HEADS = 4
        NEG_SLOPE = 0.2

        def _gat_conv(x, src, dst, W, att_src, att_dst, bias, heads, out_c):
            n = x.shape[0]
            h = (x @ W).reshape(n, heads, out_c)
            a_src = jnp.einsum('nhc,hc->nh', h, att_src)
            a_dst = jnp.einsum('nhc,hc->nh', h, att_dst)
            e = jax.nn.leaky_relu(a_src[src] + a_dst[dst], NEG_SLOPE)
            m = jax.ops.segment_max(e, dst, num_segments=n)
            p = jnp.exp(e - m[dst])
            denom = jax.ops.segment_sum(p, dst, num_segments=n)
            alpha = p / (denom[dst] + 1e-16)
            msg = h[src] * alpha[:, :, None]
            out = jax.ops.segment_sum(msg, dst, num_segments=n)
            return out.reshape(n, heads * out_c) + bias
        n = x.shape[0]
        loop = jnp.arange(n, dtype=edge_index.dtype)
        src = jnp.concatenate([edge_index[0], loop])
        dst = jnp.concatenate([edge_index[1], loop])
        out_c = HID // HEADS
        h = _gat_conv(x, src, dst, W1, att_src1, att_dst1, b1, HEADS, out_c)
        h = jax.nn.elu(h)
        out = _gat_conv(h, src, dst, W2, att_src2, att_dst2, b2, 1, HID)
        return out

    def _L2_gnn_ref(x, edge_src, edge_dst, Ws0, Wn0, b0, Ws1, Wn1, b1, Ws2, Wn2, b2):
        import jax, jax.numpy as jnp
        import numpy as np
        N_NODES = 50000
        N_EDGES = 25000
        D_IN, D_HID, D_OUT = (128, 256, 128)
        n = x.shape[0]
        deg = jax.ops.segment_sum(jnp.ones(edge_dst.shape, x.dtype), edge_dst, num_segments=n)
        inv_deg = jnp.where(deg > 0, 1.0 / jnp.maximum(deg, 1.0), 0.0)[:, None]

        def sage_conv(h, Ws, Wn, b):
            agg = jax.ops.segment_sum(h[edge_src], edge_dst, num_segments=n)
            h_neigh = agg * inv_deg
            return h @ Ws + h_neigh @ Wn + b
        h = jax.nn.relu(sage_conv(x, Ws0, Wn0, b0))
        h = jax.nn.relu(sage_conv(h, Ws1, Wn1, b1))
        h = jax.nn.relu(sage_conv(h, Ws2, Wn2, b2))
        return h

    def _L3_gnn_ref(node_feats, edge_feats, mlp_w, mlp_b, scale, src, dst):
        import jax, jax.numpy as jnp
        import numpy as np
        N_NODES = 50000
        N_EDGES = 18750
        D = 128
        n = node_feats.shape[0]
        m = node_feats[src] + edge_feats
        mx = jax.ops.segment_max(m, dst, num_segments=n)
        ex = jnp.exp(m - mx[dst])
        denom = jax.ops.segment_sum(ex, dst, num_segments=n)
        a = ex / denom[dst]
        agg = jax.ops.segment_sum(m * a, dst, num_segments=n)
        h = jax.nn.relu(agg @ mlp_w.T + mlp_b)
        return h * scale + node_feats
    edge_index = jnp.stack([src, dst])
    batch0 = jnp.zeros((3125,), jnp.int32)
    x = _layernorm(x + _L0_gnn_ref(x, edge_index, edge_attr_128, L0_gnn_u, batch0, L0_gnn_W1a, L0_gnn_b1a, L0_gnn_W1b, L0_gnn_b1b, L0_gnn_W2a, L0_gnn_b2a, L0_gnn_W2b, L0_gnn_b2b), axis=-1)
    x = _layernorm(x + _L1_gnn_ref(x, edge_index, L1_gnn_W1, L1_gnn_att_src1, L1_gnn_att_dst1, L1_gnn_b1, L1_gnn_W2, L1_gnn_att_src2, L1_gnn_att_dst2, L1_gnn_b2), axis=-1)
    x = _layernorm(x + _L2_gnn_ref(x, src, dst, L2_gnn_Ws0, L2_gnn_Wn0, L2_gnn_b0, L2_gnn_Ws1, L2_gnn_Wn1, L2_gnn_b1, L2_gnn_Ws2, L2_gnn_Wn2, L2_gnn_b2), axis=-1)
    x = _layernorm(x + _L3_gnn_ref(x, edge_attr_128, L3_gnn_mlp_w, L3_gnn_mlp_b, L3_gnn_scale, src, dst), axis=-1)
    return x

_drawn_inputs = setup_inputs


def setup_inputs(seed=0):
    import zlib

    import numpy as np

    out = dict(_drawn_inputs(seed))
    spreads = {'L1_gnn_b1': (0.0, 0.1),
     'L1_gnn_b2': (0.0, 0.1),
     'L2_gnn_b0': (0.0, 0.1),
     'L2_gnn_b1': (0.0, 0.1),
     'L2_gnn_b2': (0.0, 0.1),
     'L3_gnn_mlp_b': (0.0, 0.8),
     'L3_gnn_scale': (0.10000000149011612, 0.6)}
    factors = {'L0_gnn_W1a': 3.301,
     'L0_gnn_b1a': 8.0,
     'L0_gnn_b1b': 4.486,
     'L1_gnn_att_dst1': 2.692,
     'L1_gnn_att_dst2': 4.327}
    for name, (base, spread) in spreads.items():
        noise = np.random.default_rng([zlib.crc32(name.encode()), seed]).standard_normal(out[name].shape)
        drawn = base * np.exp(spread * noise) if base else spread * noise
        out[name] = jnp.asarray(drawn.astype(out[name].dtype))
    for name, factor in factors.items():
        out[name] = (out[name] * factor).astype(out[name].dtype)
    return out
```

```python
from contextlib import ExitStack

import concourse.bass as bass
from concourse import mybir

F32 = mybir.dt.float32
BF16 = mybir.dt.bfloat16
I32 = mybir.dt.int32
ALU = mybir.AluOpType
ACT = mybir.ActivationFunctionType
AX_X = mybir.AxisListType.X

P = 128
N_NODES, N_EDGES, D = 3125, 50000, 128
NB = -(-N_EDGES // P)
NT = 26
NODES = NT * P
S = NB + NT - 1
G = 4
NG = S // G
CH = 98
NCH = 4
BCH = S // 4
COLS = 416
NCOL = NODES // COLS
PAD_NODE = NODES - 1
NEG = -3.0e38
EPS = 1e-5
HEADS = 4
assert S % (2 * G) == 0 and NCH * CH >= NB and NCOL * COLS == NODES and S <= 512 and NT * P > N_NODES + 1

WEIGHTS = {"W1a": (2, 256), "W1b": (2, 256), "W2a": (3, 256), "W2b": (2, 128), "gW1": (1, 128), "gW2": (1, 128),
           "Ws0": (1, 256), "Wn0": (1, 256), "Ws1": (2, 256), "Wn1": (2, 256), "Ws2": (2, 128), "Wn2": (2, 128),
           "mlpT": (1, 128), "b2a": (1, 2), "sb0": (1, 2), "sb1": (1, 2)}
BIAS_ROWS = {"b1a": 256, "b1b": 256, "b2b": 128, "sb2": 128, "mlp_b": 128}
SPREAD_ROWS = {"as1": 128, "ad1": 128, "gb1": 128, "as2": 128, "ad2": 128, "gb2": 128, "scale": 128}


def offsets(sizes):
    at, out = 0, {}
    for name, n in sizes.items():
        out[name] = at
        at += n
    return out, at


W_AT, W_COLS = offsets({k: c * n for k, (c, n) in WEIGHTS.items()})
B_AT, B_COLS = offsets(BIAS_ROWS)
R_AT, R_COLS = offsets(SPREAD_ROWS)

PASSES = ["mlp", "gat1", "gat2", "sage0", "sage1", "sage2", "pool"]
ROW = {"mlp": 256, "gat1": D + HEADS, "gat2": D + 1, "sage0": 128, "sage1": 256, "sage2": 128, "pool": 128}
SUMS = {"mlp": 3 * P, "gat1": D + 2 * HEADS, "gat2": D + 2, "sage0": P, "sage1": 2 * P, "sage2": P, "pool": 2 * D}
SOFTMAX = {"gat1": (0, HEADS), "gat2": (1, 1), "pool": (2, 0)}

STAGES = [("tab0", 13, "act"), ("agg0", 16, "dve"), ("hid0", 16, "act"), ("out0", 7, "dve"), ("deg", 1, "dve"),
          ("x1T", 7, "act"), ("h1", 7, "act"), ("gT", 7, "act"), ("h2", 7, "act"), ("x2T", 7, "act"),
          ("sh0", 16, "act"), ("p1", 13, "act"), ("sh1", 16, "act"), ("p2", 7, "act"), ("out2", 7, "dve"),
          ("aT", 7, "act"), ("mo", 7, "act")]
FILLS = [(name, u, who) for name, n, who in STAGES for u in range(n)]
FIRST_FILL = {name: [f[0] for f in FILLS].index(name) for name, _, _ in STAGES}
RING = 4
TERMS = 448


def fills_read(upto, who):
    return sum(f[2] == who for f in FILLS[:upto])


def packs(per):
    return [list(range(a, min(a + per, NT))) for a in range(0, NT, per)]


def program(nc, edges_i, ea_blocks, x_rows, xT_in, wpack, bpack, rpack, out):
    with ExitStack() as ctx:
        def sb(name, shape, dt=F32):
            return ctx.enter_context(nc.sbuf_tensor(name, shape, dt))

        def sem(name):
            return ctx.enter_context(nc.semaphore(name))

        table = {k: nc.dram_tensor(f"table_{k}", (NODES, ROW[k]), F32, kind="Internal").ap() for k in PASSES}
        neg_rows = nc.dram_tensor("neg_rows", (S, P), BF16, kind="Internal").ap()
        rel_rows = nc.dram_tensor("rel_rows", (S, P), BF16, kind="Internal").ap()

        ps = ctx.enter_context(nc.psum_tensor("ps", [P, 8, 512], F32))
        big = sb("big", [P, 5, NODES])
        x_sb = sb("x_sb", [P, NT, D])
        xT = sb("xT", [P, NODES])
        h_sb = sb("h_sb", [P, NT, D + HEADS])
        inv_T = sb("inv_T", [P, NODES])
        y_sb = sb("y_sb", [P, NT, D])
        w_sb = sb("w_sb", [P, W_COLS])
        b_sb = sb("b_sb", [1, B_COLS])
        r_sb = sb("r_sb", [P, R_COLS])
        ident = sb("ident", [P, P])
        ones = sb("ones", [P, P])
        iota_i = sb("iota_i", [P, S], I32)
        iota = sb("iota", [P, S])
        part_i = sb("part_i", [P, 1], I32)
        part = sb("part", [P, 1])
        src_idx = sb("src_idx", [P, S + 2 * G], I32)
        dst_rel = sb("dst_rel", [P, S])
        last_rel = sb("last_rel", [P, S])
        tile_i = sb("tile_i", [1, S], I32)
        block_i = sb("block_i", [1, S], I32)
        adst = sb("adst", [P, NT, HEADS])
        small = sb("small", [P, 8, NT * HEADS])
        stat = sb("stat", [P, 3, NT])
        inv_row = sb("inv_row", [P, NT])
        leaks = sb("leaks", [P, 2, 2, G * HEADS])
        idx_stage = sb("idx_stage", [P, 2, 2 * G], I32)
        rows = sb("rows", [P, 2, G, 256])
        onehot = sb("onehot", [P, 2, G, P])
        ea_sb = sb("ea_sb", [P, 2, G, P])
        hp = sb("hp", [P, 2, G * P])
        s_run = sb("s_run", [P, 2, G * P])
        w_run = sb("w_run", [P, 2, G * P])
        turned = sb("turned", [P, 2, G, 256])

        flat = big[:, :, :].rearrange("p a n -> p (a n)")

        def part_of_big(at, n):
            return flat[:, at:at + n]

        lo = 3 * NODES
        pre = part_of_big(lo, 2048).rearrange("p (b g f) -> p b g f", b=2, g=G)
        neg_part = part_of_big(lo + 2048, 2048).rearrange("p (b g f) -> p b g f", b=2, g=G)
        pos_part = part_of_big(lo + 4096, 2048).rearrange("p (b g f) -> p b g f", b=2, g=G)
        rel_T = part_of_big(lo, 1024).rearrange("p (b n) -> p b n", b=2)
        logit = part_of_big(lo + 1024, 1024).rearrange("p (b n) -> p b n", b=2)
        max_run = part_of_big(lo + 2048, 1028).rearrange("p (b n) -> p b n", b=2)
        gaps = part_of_big(lo + 3080, 2048).rearrange("p (b k n) -> p b k n", b=2, k=2)
        neg_b = part_of_big(lo + 5128, 512).bitcast(BF16).rearrange("p (b n) -> p b n", b=2)
        rel_b = part_of_big(lo + 5640, 512).bitcast(BF16).rearrange("p (b n) -> p b n", b=2)
        assert 5640 + 512 <= 2 * NODES

        edges_in = part_of_big(0, 2048).bitcast(I32)
        edges_f = part_of_big(2048, 2048).rearrange("p (k c e) -> p k c e", k=4, c=NCH)
        sel = part_of_big(4096, NCH * S).rearrange("p (c s) -> p c s", c=NCH)
        moved = part_of_big(5760, S)
        tile_f = part_of_big(6176, S)
        block_f = part_of_big(6592, S)
        ends = part_of_big(7008, NT)
        below = part_of_big(7040, NCH * NT).rearrange("p (c t) -> p c t", c=NCH)
        chunk_part = part_of_big(7150, NCH)
        key = part_of_big(7155, 1)
        last_f = part_of_big(7160, S)
        tile_col = part_of_big(7580, 4)
        row_f = part_of_big(7600, 4 * 2 * P).rearrange("p (q k e) -> p q k e", q=4, k=2)
        moved_last = part_of_big(9160, S)
        row_b = part_of_big(8640, 4 * 2 * P // 2).bitcast(BF16).rearrange("p (q k e) -> p q k e", q=4, k=2)

        sum_T = big[:, 0:3, :]

        def sum_rows(k):
            at = lo if k == "sage2" else 0
            return part_of_big(at, NT * SUMS[k]).rearrange("p (t f) -> p t f", t=NT)

        spare = big[:, 2, :]

        def neg_node(m):
            return s_run[:, m, 0:COLS]

        def pos_node(m):
            return w_run[:, m, 0:COLS]

        def weight(name, c, m0=0, m=None):
            n = WEIGHTS[name][1]
            at = W_AT[name] + c * n + m0
            return w_sb[:, at:at + (n - m0 if m is None else m)]

        def bias_row(name, m0=0, m=None):
            at = B_AT[name] + m0
            return b_sb[0:1, at:at + (BIAS_ROWS[name] - m0 if m is None else m)]

        def spread(name):
            return r_sb[:, R_AT[name]:R_AT[name] + SPREAD_ROWS[name]]

        def over_tiles(row):
            return row.unsqueeze(1).to_broadcast([P, NT, D])

        def pick(t):
            return slice(t * P, (t + 1) * P)

        edges_loaded, weights_loaded, x_loaded = sem("edges_loaded"), sem("weights_loaded"), sem("x_loaded")
        iotas_ready, consts_ready = sem("iotas_ready"), sem("consts_ready")
        below_ready, keys_summed, moved_ready, tiles_spread = (
            sem("below_ready"), sem("keys_summed"), sem("moved_ready"), sem("tiles_spread"))
        rows_ready_parts = sem("rows_ready_parts")
        leak_scaled, leak_ready = sem("leak_scaled"), sem("leak_ready")
        hp_ready, carry_ready, old_max_ready = sem("hp_ready"), sem("carry_ready"), sem("old_max_ready")
        sel_ready, cols_moved, rows_moved, tables_ready, rows_ready, rows_stored = (
            sem("sel_ready"), sem("cols_moved"), sem("rows_moved"), sem("tables_ready"), sem("rows_ready"),
            sem("rows_stored"))
        dve_link, act_link = sem("dve_link"), sem("act_link")
        fill_done, read_by = sem("fill_done"), {"act": sem("read_by_act"), "dve": sem("read_by_dve")}
        table_ready = {k: sem(f"table_ready_{k}") for k in PASSES}
        table_written = sem("table_written")
        acc_zeroed = sem("acc_zeroed")
        deg_summed = sem("deg_summed")
        agg0_ready, hid0_ready, hid0_parts, x1_ready = (
            sem("agg0_ready"), sem("hid0_ready"), sem("hid0_parts"), sem("x1_ready"))
        h_ready = sem("h_ready")
        gaps_in, gaps_out = sem("node_gaps"), sem("node_gaps_exp")
        g_ready, g_low = sem("g_ready"), sem("g_low")
        g1_ready = sem("g1_ready")
        centered, squared, var_ready, rooted = sem("centered"), sem("squared"), sem("var_ready"), sem("rooted")
        x_ready = sem("x_ready")
        agg_scaled = sem("agg_scaled")
        mo_ready, agg3_ready = sem("mo_ready"), sem("agg3_ready")
        out_written = sem("out_written")
        gathered = [sem("gathered0"), sem("gathered1")]
        idx_staged, pool_tick = sem("idx_staged"), sem("pool_tick")
        onehot_ready, summed, accumulated = sem("onehot_ready"), sem("summed"), sem("accumulated")
        ea_loaded = [sem("ea_loaded0"), sem("ea_loaded1")]
        edge_product, pre_ready, parts_ready, elu_ready = (
            sem("edge_product"), sem("pre_ready"), sem("parts_ready"), sem("elu_ready"))
        neg_loaded = [sem("neg_loaded0"), sem("neg_loaded1")]
        rel_ready, taken, logit_ready, logit_turned = (
            sem("rel_ready"), sem("taken"), sem("logit_ready"), sem("logit_turned"))
        max_ready, gaps_ready, exp_ready, run_ready = (
            sem("max_ready"), sem("gaps_ready"), sem("exp_ready"), sem("run_ready"))
        turn_done, turned_ready = sem("turn_done"), sem("turned_ready")

        def has(g, back=0):
            return not isinstance(g, int) or 0 <= g - back < NG

        def early(x, n):
            return isinstance(x, int) and x < n

        def slots(eng, slot, tail, head=2):
            for g in range(head):
                slot(g, g % 2)
            with eng.Fori(head // 2, NG // 2) as i:
                slot(i * 2, 0)
                slot(i * 2 + 1, 1)
            for g in range(NG, NG + tail):
                slot(g, g % 2)

        def half(g, b):
            return g // 2 if isinstance(g, int) else (g - b) // 2

        base = {k: NG * n for n, k in enumerate(PASSES)}
        ea_base = {"mlp": 0, "pool": NG}

        block = ctx.enter_context(nc.Block())

        @block.sync
        def _(sp):
            sp.dma_start(edges_in[0:CH, :], edges_i).then_inc(edges_loaded, 16)
            sp.dma_start(xT[:, :], xT_in).then_inc(x_loaded, 16)
            sp.dma_start(x_sb[:, :, :], x_rows.rearrange("(t p) f -> p t f", p=P)).then_inc(x_loaded, 16)
            sp.wait_ge(rows_ready, 1)
            for q in range(4):
                sp.dma_start(neg_rows[q * BCH:(q + 1) * BCH, :], row_b[0:BCH, q, 0, :]).then_inc(rows_stored, 16)
                sp.dma_start(rel_rows[q * BCH:(q + 1) * BCH, :], row_b[0:BCH, q, 1, :]).then_inc(rows_stored, 16)

            def write_table(k, rows_sb):
                sp.wait_ge(table_ready[k], 1)
                sp.dma_start(table[k].rearrange("(t p) f -> p t f", p=P), rows_sb).then_inc(table_written, 16)

            def load_ea(g, b, freed, at):
                if not early(g, 2):
                    sp.wait_ge(freed, at + g - 1)
                for j in range(G):
                    blk = sp.value_load(block_i[0:1, bass.ds(g * G + j, 1)], min_val=0, max_val=NB - 1)
                    sp.dma_start(ea_sb[:, b, j, :], ea_blocks[bass.ds(blk, 1), :, :].rearrange("o p e -> p (o e)"))\
                      .then_inc(ea_loaded[b], 16)

            def load_step_rows(g, b, at, heads):
                if not early(g, 2):
                    sp.wait_ge(gaps_ready, at + g - 1)
                sp.dma_start(neg_b[:, b, :],
                             neg_rows[bass.ds(g * G, G), :].rearrange("s e -> (s e)").partition_broadcast(P))\
                  .then_inc(neg_loaded[b], 16)
                if heads:
                    sp.dma_start(rel_b[:, b, :],
                                 rel_rows[bass.ds(g * G, G), :].rearrange("s e -> (s e)").partition_broadcast(P))\
                      .then_inc(neg_loaded[b], 16)

            wide = big[:, 3:5, :].rearrange("p a n -> p (a n)").rearrange("p (t f) -> p t f", t=NT)
            low = big[:, 0:2, :].rearrange("p a n -> p (a n)").rearrange("p (t f) -> p t f", t=NT)
            write_table("mlp", wide)
            sp.wait_ge(tables_ready, 1)
            slots(sp, lambda g, b: load_ea(g, b, edge_product, 0), 0)

            def softmax_rows(k):
                n, heads = SOFTMAX[k]
                sp.wait_ge(rows_stored, 128)
                sp.wait_ge(acc_zeroed, PASSES.index(k) + 1)

                def slot(g, b):
                    load_step_rows(g, b, n * NG, heads)
                    if not heads:
                        load_ea(g, b, front_ea, n * NG)
                slots(sp, slot, 0)

            front_ea = max_ready
            write_table("gat1", h_sb[:, :, 0:ROW["gat1"]])
            softmax_rows("gat1")
            write_table("gat2", h_sb[:, :, 0:ROW["gat2"]])
            softmax_rows("gat2")
            write_table("sage0", x_sb[:, :, :])
            write_table("sage1", low)
            write_table("sage2", h_sb[:, :, 0:D])
            write_table("pool", x_sb[:, :, :])
            softmax_rows("pool")
            sp.wait_ge(x_ready, 4)
            full = N_NODES // P
            sp.dma_start(out[0:full * P, :].rearrange("(t p) f -> p t f", p=P), x_sb[:, 0:full, :])\
              .then_inc(out_written, 16)
            sp.dma_start(out[full * P:N_NODES, :], x_sb[0:N_NODES - full * P, full, :]).then_inc(out_written, 16)
            sp.wait_ge(out_written, 32)

        @block.gpsimd
        def _(pool):
            pool.iota(iota_i[:, :], pattern=[[1, S]], base=0, channel_multiplier=0).then_inc(iotas_ready, 1)
            pool.iota(part_i[:, :], pattern=[[0, 1]], base=0, channel_multiplier=1).then_inc(iotas_ready, 1)
            pool.wait_ge(tables_ready, 1)

            def gather_pass(k, freed, freed_at):
                first = base[k] // 2

                def stage(pair, to):
                    pool.tensor_copy(idx_stage[:, to, :], src_idx[:, bass.ds(pair * 2 * G, 2 * G)])\
                        .then_inc(idx_staged, 1)

                def pair(p, par, peeled):
                    for b in range(2):
                        if not (peeled and p == 0):
                            pool.wait_ge(freed, freed_at + p * 2 + b - 1)
                        if b == 0:
                            pool.wait_ge(idx_staged, PASSES.index(k) * (NG // 2 + 1) + p + 1)
                            pool.sem_inc(pool_tick, 1)
                        else:
                            stage(p + 1, 1 - par)
                        for j in range(G):
                            pool.indirect_dma_start(
                                rows[:, b, j, 0:ROW[k]], None, table[k],
                                bass.IndirectOffsetOnAxis(idx_stage[:, par, b * G + j:b * G + j + 1], 0))\
                                .then_inc(gathered[b], 16)

                pool.wait_ge(table_written, 16 * (PASSES.index(k) + 1))
                if first:
                    pool.wait_ge(idx_staged, PASSES.index(k) * (NG // 2 + 1))
                stage(0, 0)
                pair(0, 0, True)
                pair(1, 1, True)
                with pool.Fori(1, NG // 4) as i:
                    pair(i * 2, 0, False)
                    pair(i * 2 + 1, 1, False)

            gather_pass("mlp", pre_ready, 0)
            gather_pass("gat1", taken, 0)
            gather_pass("gat2", taken, NG)
            gather_pass("sage0", summed, base["sage0"])
            gather_pass("sage1", summed, base["sage1"])
            gather_pass("sage2", summed, base["sage2"])
            gather_pass("pool", taken, 2 * NG)

        @block.tensor
        def _(pe):
            pe.wait_ge(below_ready, 1)
            for c in range(NCH):
                mm = pe.matmul(ps[0:NT - 1, 0, 0:1], below[0:CH, c, 0:NT - 1], ones[0:CH, 0:1],
                               start=(c == 0), stop=(c == NCH - 1))
            mm.then_inc(keys_summed, 1)
            pe.wait_ge(moved_ready, 1)
            pe.matmul(ps[:, 1, 0:S], ones[0:NT - 1, :], moved[0:NT - 1, :], start=True, stop=True)\
              .then_inc(tiles_spread, 1)
            pe.wait_ge(sel_ready, 1)
            for n, k in enumerate((0, 1, 3)):
                for c in range(NCH):
                    mm = pe.matmul(ps[:, 2 + n, 0:S], edges_f[0:CH, k, c, :], sel[0:CH, c, :],
                                   start=(c == 0), stop=(c == NCH - 1))
                mm.then_inc(cols_moved, 1)
            for q in range(4):
                at = slice(q * BCH, (q + 1) * BCH)
                for n, k in enumerate((1, 2)):
                    for c in range(NCH):
                        pe.matmul(ps[0:BCH, 5 + q % 2, n * P:(n + 1) * P], sel[0:CH, c, at], edges_f[0:CH, k, c, :],
                                  start=(c == 0), stop=(c == NCH - 1))
                mm = pe.matmul(ps[0:BCH, 5 + q % 2, 2 * P:2 * P + 1], moved[0:NT - 1, at], ones[0:NT - 1, 0:1],
                               start=True, stop=True)
                mm.then_inc(rows_moved, 1)
                if 1 <= q < 3:
                    pe.wait_ge(rows_ready_parts, q)

            def fill(name, u):
                n = FIRST_FILL[name] + u
                if n >= RING:
                    who = FILLS[n - RING][2]
                    pe.wait_ge(read_by[who], fills_read(n - RING + 1, who))
                return ps[:, n % RING, :]

            def row_products(name, per, width, terms, bias):
                for u, tiles in enumerate(packs(per)):
                    bank = fill(name, u)
                    for i, t in enumerate(tiles):
                        to = bank[:, i * width:(i + 1) * width]
                        for n, (act, w) in enumerate(terms):
                            mm = pe.matmul(to, act[:, pick(t)], w, start=(n == 0),
                                           stop=(n == len(terms) - 1 and bias is None))
                        if bias is not None:
                            mm = pe.matmul(to, ones[0:1, :], bias, start=False, stop=True)
                    mm.then_inc(fill_done, 1)

            def column_products(name, terms_of):
                for c in range(NCOL):
                    at = slice(c * COLS, (c + 1) * COLS)
                    for m in range(2):
                        bank = fill(name, 2 * c + m)
                        terms = terms_of(m)
                        for n, (w, act) in enumerate(terms):
                            mm = pe.matmul(bank[:, 0:COLS], w, act[:, at], start=(n == 0), stop=(n == len(terms) - 1))
                        mm.then_inc(fill_done, 1)

            def turn_rows(name, of):
                for u, tiles in enumerate(packs(4)):
                    bank = fill(name, u)
                    for i, t in enumerate(tiles):
                        mm = pe.transpose(bank[:, i * P:(i + 1) * P], of(t), ident[:, :])
                    mm.then_inc(fill_done, 1)

            pe.wait_ge(weights_loaded, 48)
            pe.wait_ge(x_loaded, 32)
            pe.wait_ge(rows_ready, 1)
            row_products("tab0", 2, 256, [(xT, weight("W1a", 0))], bias_row("b1a"))

            def mlp_slot(g, b):
                if has(g):
                    if not early(g, 2):
                        pe.wait_ge(pre_ready, g - 1)
                    pe.wait_ge(ea_loaded[b], 16 * G * (half(g, b) + 1))
                    for j in range(G):
                        mm = pe.matmul(ps[:, 2 * b + j // 2, (j % 2) * 256:(j % 2) * 256 + 256], ea_sb[:, b, j, :],
                                       weight("W1a", 1), start=True, stop=True)
                    mm.then_inc(edge_product, 1)
                if has(g, 1):
                    pe.wait_ge(elu_ready, g)
                    pe.wait_ge(onehot_ready, g)
                    if has(g, 2):
                        pe.wait_ge(accumulated, G * (g - 1))
                    q = 1 - b
                    for j in range(G):
                        for c in range(2):
                            pe.matmul(ps[:, 4 + j, c * P:(c + 1) * P], pos_part[:, q, j, c * P:(c + 1) * P],
                                      onehot[:, q, j, :], start=True, stop=True)
                        mm = pe.matmul(ps[:, 4 + j, 2 * P:3 * P], ones[:, :], onehot[:, q, j, :],
                                       start=True, stop=True)
                    mm.then_inc(summed, 1)

            pe.wait_ge(read_by["act"], fills_read(FIRST_FILL["agg0"], "act"))
            slots(pe, mlp_slot, 1)

            pe.wait_ge(deg_summed, 1)
            column_products("agg0", lambda m: [(weight("W1b", 0, m * P, P), sum_T[:, 0, :]),
                                               (weight("W1b", 1, m * P, P), sum_T[:, 1, :]),
                                               (bias_row("b1b", m * P, P), sum_T[0:1, 2, :])])
            pe.wait_ge(agg0_ready, 2 * NCOL)
            column_products("hid0", lambda m: [(weight("W2a", 0, m * P, P), xT),
                                               (weight("W2a", 1, m * P, P), big[:, 3, :]),
                                               (weight("W2a", 2, m * P, P), big[:, 4, :])])
            pe.wait_ge(hid0_ready, 2 * NCOL)
            row_products("out0", 4, D, [(big[:, 0, :], weight("W2b", 0)), (big[:, 1, :], weight("W2b", 1))],
                         bias_row("b2b"))
            bank = fill("deg", 0)
            for t in range(NT):
                mm = pe.matmul(bank[:, t:t + 1], big[0:1, 2, pick(t)], ones[0:1, 0:1], start=True, stop=True)
            mm.then_inc(fill_done, 1)
            pe.wait_ge(x_ready, 1)
            turn_rows("x1T", lambda t: x_sb[:, t, :])
            pe.wait_ge(read_by["act"], fills_read(FIRST_FILL["h1"], "act"))
            row_products("h1", 4, D, [(xT, weight("gW1", 0))], None)

            def softmax_pass(k):
                n, heads = SOFTMAX[k]
                at, all_at = n * NG, base[k]
                width = SUMS[k]

                def take(x, b):
                    pe.wait_ge(gathered[b], 16 * G * (all_at // 2 + half(x, b) + 1))
                    if heads:
                        if not early(x, 2):
                            pe.wait_ge(run_ready, at + x - 1)
                        for j in range(G):
                            pe.transpose(ps[:, 2 + b, j * P:(j + 1) * P], rows[:, b, j, 0:D], ident[:, :])
                    else:
                        if not early(x, 2):
                            pe.wait_ge(logit_ready, at + x - 1)
                        for j in range(G):
                            mm = pe.transpose(ps[:, b, j * P:(j + 1) * P], rows[:, b, j, 0:D], ident[:, :])
                        mm.then_inc(taken, 1)

                def add_terms(x, b):
                    pe.wait_ge(rel_ready, at + x + 1)
                    if not early(x, 2):
                        pe.wait_ge(leak_ready, at + x - 1)
                    if not early(x, 4):
                        pe.wait_ge(accumulated, G * (all_at + x - 3))
                    for j in range(G):
                        t = pe.value_load(tile_i[0:1, bass.ds(x * G + j, 1)], min_val=0, max_val=NT - 1)
                        to = ps[:, 7, TERMS + (b * G + j) * heads:TERMS + (b * G + j + 1) * heads]
                        pe.matmul(to, ident[:, :], rows[:, b, j, D:D + heads], start=True, stop=False)
                        mm = pe.matmul(to, rel_T[:, b, j * P:(j + 1) * P],
                                       adst[:, bass.ds(t, 1), 0:heads].rearrange("p o h -> p (o h)"),
                                       start=False, stop=True)
                    mm.then_inc(taken, 1)

                def spread_logits(x, b):
                    pe.wait_ge(logit_ready, at + x + 1)
                    if not early(x, 2):
                        pe.wait_ge(gaps_ready, at + x - 1)
                    for j in range(G):
                        mm = pe.transpose(ps[:, b, j * P:(j + 1) * P], logit[:, b, j * P:(j + 1) * P], ident[:, :])
                    mm.then_inc(logit_turned, 1)

                def turn(x, b):
                    pe.wait_ge(run_ready, at + x + 1)
                    if not early(x, 1):
                        pe.wait_ge(turned_ready, at + x)
                    for j in range(G):
                        cols = slice(j * P, (j + 1) * P)
                        mm = pe.transpose(ps[:, 4, cols], w_run[:, b, cols], ident[:, :])
                        if heads:
                            picks = ident[:, 0:P:D // heads] if heads > 1 else ident[:, 0:1]
                            pe.matmul(ps[:, 5, j * 2 * heads:j * 2 * heads + heads], s_run[:, b, cols], picks,
                                      start=True, stop=True)
                            mm = pe.matmul(ps[:, 5, j * 2 * heads + heads:(j + 1) * 2 * heads],
                                           max_run[:, b, 1 + j * P:1 + (j + 1) * P], picks, start=True, stop=True)
                        else:
                            mm = pe.transpose(ps[:, 5, cols], s_run[:, b, cols], ident[:, :])
                    mm.then_inc(turn_done, 1)

                def finish(x, b):
                    pe.wait_ge(turned_ready, at + x + 1)
                    pe.wait_ge(onehot_ready, all_at + x + 1)
                    if not early(x, 1):
                        pe.wait_ge(accumulated, G * (all_at + x))
                    for j in range(G):
                        mm = pe.matmul(ps[:, 6 + j // 2, (j % 2) * 256:(j % 2) * 256 + width], onehot[:, b, j, :],
                                       turned[:, b, j, 0:width], start=True, stop=True)
                    mm.then_inc(summed, 1)

                def slot(g, b):
                    if has(g, 1) and heads:
                        spread_logits(g - 1, 1 - b)
                    if has(g):
                        take(g, b)
                    if has(g, 3):
                        finish(g - 3, 1 - b)
                    if has(g) and heads:
                        add_terms(g, b)
                    if has(g, 2):
                        turn(g - 2, b)
                slots(pe, slot, 3, head=4)

            pe.wait_ge(read_by["act"], fills_read(FIRST_FILL["gT"], "act"))
            softmax_pass("gat1")
            pe.wait_ge(g1_ready, 1)
            turn_rows("gT", lambda t: y_sb[:, t, :])
            pe.wait_ge(read_by["act"], fills_read(FIRST_FILL["h2"], "act"))
            row_products("h2", 4, D, [(big[:, 3, :], weight("gW2", 0))], None)
            pe.wait_ge(read_by["act"], fills_read(FIRST_FILL["x2T"], "act"))
            softmax_pass("gat2")
            pe.wait_ge(x_ready, 2)
            turn_rows("x2T", lambda t: x_sb[:, t, :])

            def sum_pass(k, by_row):
                all_at = base[k]
                chunks = ROW[k] // P

                def slot(g, b):
                    pe.wait_ge(gathered[b], 16 * G * (all_at // 2 + half(g, b) + 1))
                    pe.wait_ge(onehot_ready, all_at + g + 1)
                    if not early(g, 2):
                        pe.wait_ge(accumulated, G * (all_at + g - 1))
                    for j in range(G):
                        to = ps[:, 4 + 2 * b + j // 2, (j % 2) * 256:(j % 2) * 256 + 256]
                        if by_row:
                            mm = pe.matmul(to[:, 0:P], onehot[:, b, j, :], rows[:, b, j, 0:P], start=True, stop=True)
                        else:
                            for c in range(chunks):
                                mm = pe.matmul(to[:, c * P:(c + 1) * P], rows[:, b, j, c * P:(c + 1) * P],
                                               onehot[:, b, j, :], start=True, stop=True)
                    mm.then_inc(summed, 1)
                slots(pe, slot, 0)

            sum_pass("sage0", False)
            pe.wait_ge(agg_scaled, 1)
            pe.wait_ge(read_by["act"], fills_read(FIRST_FILL["sh0"], "act"))
            column_products("sh0", lambda m: [(weight("Ws0", 0, m * P, P), xT),
                                              (weight("Wn0", 0, m * P, P), sum_T[:, 0, :])])
            pe.wait_ge(read_by["act"], fills_read(FIRST_FILL["p1"], "act"))
            row_products("p1", 2, 256, [(big[:, 3, :], weight("Wn1", 0)), (big[:, 4, :], weight("Wn1", 1))], None)
            sum_pass("sage1", False)
            pe.wait_ge(agg_scaled, 2)
            column_products("sh1", lambda m: [(weight("Ws1", 0, m * P, P), big[:, 3, :]),
                                              (weight("Ws1", 1, m * P, P), big[:, 4, :]),
                                              (ident[:, :], sum_T[:, m, :])])
            pe.wait_ge(read_by["act"], fills_read(FIRST_FILL["p2"], "act"))
            row_products("p2", 4, D, [(big[:, 0, :], weight("Wn2", 0)), (big[:, 1, :], weight("Wn2", 1))], None)
            sum_pass("sage2", True)
            row_products("out2", 4, D, [(big[:, 0, :], weight("Ws2", 0)), (big[:, 1, :], weight("Ws2", 1))],
                         bias_row("sb2"))
            pe.wait_ge(read_by["dve"], fills_read(FIRST_FILL["aT"], "dve"))
            softmax_pass("pool")
            pe.wait_ge(agg3_ready, 1)
            turn_rows("aT", lambda t: y_sb[:, t, :])
            pe.wait_ge(read_by["act"], fills_read(FIRST_FILL["mo"], "act"))
            row_products("mo", 4, D, [(xT, weight("mlpT", 0))], bias_row("mlp_b"))

        @block.scalar
        def _(act):
            links = [0]

            def link(ins):
                links[0] += 1
                ins.then_inc(act_link, 1)
                act.wait_ge(act_link, links[0])

            act.dma_start(w_sb[:, :], wpack).then_inc(weights_loaded, 16)
            act.dma_start(b_sb[:, :], bpack).then_inc(weights_loaded, 16)
            act.dma_start(r_sb[:, :], rpack.rearrange("o n -> (o n)").partition_broadcast(P)).then_inc(weights_loaded, 16)

            fills = [0]

            def filled(name, u):
                n = FIRST_FILL[name] + u
                act.wait_ge(fill_done, n + 1)
                return ps[:, n % RING, :]

            def copy_rows(name, per, width, to, func=ACT.Copy):
                for u, tiles in enumerate(packs(per)):
                    bank = filled(name, u)[:, 0:len(tiles) * width].rearrange("p (t f) -> p t f", f=width)
                    act.activation(to[:, tiles[0]:tiles[-1] + 1, 0:width], bank, func).then_inc(read_by["act"], 1)

            def copy_turned(name, to):
                for u, tiles in enumerate(packs(4)):
                    bank = filled(name, u)
                    act.activation(to[:, tiles[0] * P:(tiles[-1] + 1) * P], bank[:, 0:len(tiles) * P], ACT.Copy)\
                       .then_inc(read_by["act"], 1)

            low = big[:, 0:2, :].rearrange("p a n -> p (a n)").rearrange("p (t f) -> p t f", t=NT)
            wide = big[:, 3:5, :].rearrange("p a n -> p (a n)").rearrange("p (t f) -> p t f", t=NT)
            copy_rows("tab0", 2, 256, wide)
            act.wait_ge(read_by["act"], fills_read(FIRST_FILL["agg0"], "act"))
            act.sem_inc(table_ready["mlp"], 1)

            def mlp_slot(g, b):
                act.wait_ge(pre_ready, g + 1)
                if not early(g, 2):
                    act.wait_ge(summed, g - 1)
                act.activation(neg_part[:, b], pre[:, b], ACT.Relu, scale=-1.0).then_inc(parts_ready, 1)
                act.activation(pos_part[:, b], pre[:, b], ACT.Relu).then_inc(parts_ready, 1)
                act.wait_ge(parts_ready, 3 * g + 2)
                act.activation(neg_part[:, b], neg_part[:, b], ACT.Exp, scale=-1.0).then_inc(parts_ready, 1)
            slots(act, mlp_slot, 0)

            low_bias = small[:, 0, 0:2]
            link(act.mul(low_bias, weight("b2a", 0), -1.0))
            for c in range(NCOL):
                for m in range(2):
                    u = 2 * c + m
                    bank = filled("hid0", u)
                    at = slice(c * COLS, (c + 1) * COLS)
                    if u >= 2:
                        act.wait_ge(hid0_ready, u - 1)
                    link(act.activation(neg_node(m), bank[:, 0:COLS], ACT.Relu, bias=low_bias[:, m:m + 1], scale=-1.0))
                    act.activation(pos_node(m), bank[:, 0:COLS], ACT.Relu, bias=weight("b2a", 0)[:, m:m + 1])\
                       .then_inc(read_by["act"], 1)
                    act.activation(neg_node(m), neg_node(m), ACT.Exp, scale=-1.0).then_inc(hid0_parts, 1)

            def norm(n):
                act.wait_ge(centered, n)
                act.activation(spare, y_sb[:, :, :].rearrange("p t f -> p (t f)"), ACT.Square).then_inc(squared, 1)
                act.wait_ge(var_ready, n)
                act.activation(stat[:, 1, :], stat[:, 2, :], ACT.Sqrt).then_inc(rooted, 1)

            norm(1)
            copy_turned("x1T", xT)
            copy_rows("h1", 4, D, h_sb)

            def softmax_pass(k):
                n, heads = SOFTMAX[k]
                at = n * NG
                if heads:
                    act.wait_ge(h_ready, n + 1)

                extra = 2 * heads if heads else D

                def make_logits(x, b):
                    act.wait_ge(leak_ready, at + x + 1)
                    if not early(x, 2):
                        act.wait_ge(logit_turned, at + x - 1)
                    terms = leaks[:, b, 1, 0:G * heads].unsqueeze(2).to_broadcast([P, G * heads, D // heads])
                    act.activation(logit[:, b, :].rearrange("p (h f) -> p h f", f=D // heads), terms, ACT.Copy)\
                       .then_inc(logit_ready, 1)

                def copy_turned_sums(x, b):
                    act.wait_ge(turn_done, at + x + 1)
                    if not early(x, 2):
                        act.wait_ge(summed, base[k] + x - 1)
                    act.activation(turned[:, b, :, 0:D], ps[:, 4, :].rearrange("p (g f) -> p g f", g=G), ACT.Copy)
                    act.activation(turned[:, b, :, D:D + extra],
                                   ps[:, 5, 0:G * extra].rearrange("p (g f) -> p g f", g=G), ACT.Copy)\
                       .then_inc(turned_ready, 1)

                def exponentials(x, b):
                    act.wait_ge(gaps_ready, at + x + 1)
                    act.activation(gaps[:, b], gaps[:, b], ACT.Exp).then_inc(exp_ready, 1)

                def slot(g, b):
                    if has(g, 2):
                        copy_turned_sums(g - 2, b)
                    if has(g, 1):
                        exponentials(g - 1, 1 - b)
                    if has(g) and heads:
                        make_logits(g, b)
                slots(act, slot, 2, head=4)
                if heads:
                    act.wait_ge(gaps_in, n + 1)
                    m = NT * heads
                    act.activation(small[:, 3:5, 0:m], small[:, 3:5, 0:m], ACT.Exp).then_inc(gaps_out, 1)

            softmax_pass("gat1")
            act.wait_ge(g_ready, 1)
            y_flat = y_sb[:, :, :].rearrange("p t f -> p (t f)")
            link(act.activation(spare, y_flat, ACT.Relu, scale=-1.0))
            act.activation(spare, spare, ACT.Exp, scale=-1.0).then_inc(g_low, 1)
            copy_turned("gT", big[:, 3, :])
            copy_rows("h2", 4, D, h_sb)
            softmax_pass("gat2")
            norm(2)
            copy_turned("x2T", xT)

            def relu_columns(name, bias, to):
                for c in range(NCOL):
                    for m in range(2):
                        bank = filled(name, 2 * c + m)
                        act.activation(big[:, to + m, c * COLS:(c + 1) * COLS], bank[:, 0:COLS], ACT.Relu,
                                       bias=weight(bias, 0)[:, m:m + 1]).then_inc(read_by["act"], 1)

            relu_columns("sh0", "sb0", 3)
            copy_rows("p1", 2, 256, low)
            act.wait_ge(read_by["act"], fills_read(FIRST_FILL["sh1"], "act"))
            act.sem_inc(table_ready["sage1"], 1)
            relu_columns("sh1", "sb1", 0)
            copy_rows("p2", 4, D, h_sb)
            act.wait_ge(read_by["act"], fills_read(FIRST_FILL["out2"], "act"))
            act.sem_inc(table_ready["sage2"], 1)
            norm(3)
            softmax_pass("pool")
            copy_turned("aT", xT)
            copy_rows("mo", 4, D, y_sb, ACT.Relu)
            norm(4)

        @block.vector
        def _(dve):
            links = [0]

            def link(ins):
                links[0] += 1
                ins.then_inc(dve_link, 1)
                dve.wait_ge(dve_link, links[0])

            link(dve.memset(ones[:, :], 1.0))
            dve.wait_ge(iotas_ready, 2)
            dve.tensor_copy(iota[:, :], iota_i[:, :])
            link(dve.tensor_copy(part[:, :], part_i[:, :]))
            link(dve.tensor_scalar(ident[:, :], iota[:, 0:P], part[:, 0:1], None, ALU.is_equal))
            dve.wait_ge(edges_loaded, 16)
            dve.tensor_copy(edges_f[0:CH].rearrange("p k c e -> p (k c e)"), edges_in[0:CH, :])
            link(dve.tensor_scalar(ends[:, :], iota[:, 0:NT], float(P), float(P), ALU.mult, ALU.add))
            for c in range(NCH):
                dve.tensor_scalar(chunk_part[:, c:c + 1], part[:, :], float(c * CH), None, ALU.add)
                ins = dve.tensor_scalar(below[0:CH, c, :], ends[0:CH, :], edges_f[0:CH, 1, c, P - 1:P], None, ALU.is_gt)
            ins.then_inc(below_ready, 1)
            dve.wait_ge(keys_summed, 1)
            link(dve.tensor_tensor(key[0:NT - 1, :], ps[0:NT - 1, 0, 0:1], part[0:NT - 1, :], ALU.add))
            dve.tensor_scalar(moved[0:NT - 1, :], iota[0:NT - 1, :], key[0:NT - 1, 0:1], None, ALU.is_gt)\
               .then_inc(moved_ready, 1)
            dve.wait_ge(tiles_spread, 1)
            dve.tensor_copy(tile_i[:, :], ps[0:1, 1, 0:S])
            dve.tensor_scalar(tile_f[:, :], ps[:, 1, 0:S], float(P), None, ALU.mult)
            link(dve.tensor_tensor(block_f[:, :], iota[:, :], ps[:, 1, 0:S], ALU.subtract))
            dve.tensor_copy(block_i[:, :], block_f[0:1, :])
            for c in range(NCH):
                ins = dve.tensor_scalar(sel[0:CH, c, :], block_f[0:CH, :], chunk_part[0:CH, c:c + 1], None, ALU.is_equal)
            ins.then_inc(sel_ready, 1)
            dve.wait_ge(cols_moved, 3)
            link(dve.memset(src_idx[:, :], 0))
            dve.tensor_copy(src_idx[:, 0:S], ps[:, 2, 0:S])
            dve.tensor_tensor(dst_rel[:, :], ps[:, 3, 0:S], tile_f[:, :], ALU.subtract)
            link(dve.tensor_copy(moved_last, ps[:, 4, 0:S]))
            link(dve.tensor_tensor(last_f[:, :], ps[:, 3, 0:S], moved_last, ALU.not_equal))
            link(dve.scalar_tensor_tensor(last_rel[:, :], dst_rel[:, :], 1.0, last_f[:, :], ALU.add, ALU.mult))
            link(dve.tensor_scalar(last_rel[:, :], last_rel[:, :], -1.0, None, ALU.add))
            dve.drain().then_inc(tables_ready, 1)
            for q in range(4):
                dve.wait_ge(rows_moved, q + 1)
                bank = ps[0:BCH, 5 + q % 2, :]
                link(dve.tensor_scalar(tile_col[0:BCH, q:q + 1], bank[:, 2 * P:2 * P + 1], float(P), None, ALU.mult))
                link(dve.tensor_copy(row_f[0:BCH, q, 0, :], bank[:, P:2 * P]))
                link(dve.tensor_tensor(row_f[0:BCH, q, 0, :], bank[:, 0:P], row_f[0:BCH, q, 0, :], ALU.not_equal))
                dve.tensor_scalar(row_b[0:BCH, q, 0, :], row_f[0:BCH, q, 0, :], NEG, None, ALU.mult)
                ins = dve.tensor_scalar(row_b[0:BCH, q, 1, :], bank[:, 0:P], tile_col[0:BCH, q:q + 1], None,
                                        ALU.subtract)
                ins.then_inc(rows_ready_parts, 1)
            dve.wait_ge(rows_ready_parts, 4)
            dve.drain().then_inc(rows_ready, 1)

            def zero(k, what):
                dve.memset(what, 0.0).then_inc(acc_zeroed, 1)
                dve.wait_ge(acc_zeroed, PASSES.index(k) + 1)

            def make_onehot(k, g, b, values):
                dve.tensor_tensor(onehot[:, b], iota[:, 0:P].unsqueeze(1).to_broadcast([P, G, P]),
                                  values[:, bass.ds(g * G, G)].unsqueeze(2).to_broadcast([P, G, P]),
                                  ALU.is_equal).then_inc(onehot_ready, 1)

            def accumulate(k, g, bank_of, acc):
                for j in range(G):
                    t = dve.value_load(tile_i[0:1, bass.ds(g * G + j, 1)], min_val=0, max_val=NT - 1)
                    to = acc(t)
                    done = G * (base[k] + g) + j
                    if not (isinstance(done, int) and done == 0):
                        dve.wait_ge(accumulated, done)
                    dve.tensor_tensor(to, to, bank_of(j), ALU.add).then_inc(accumulated, 1)

            dve.wait_ge(rows_stored, 128)
            zero("mlp", sum_T)
            dve.wait_ge(table_written, 16)

            def mlp_slot(g, b):
                if has(g):
                    if not early(g, 2):
                        dve.wait_ge(summed, g - 1)
                    make_onehot("mlp", g, b, dst_rel)
                    dve.wait_ge(edge_product, g + 1)
                    dve.wait_ge(gathered[b], 16 * G * (half(g, b) + 1))
                    if not early(g, 2):
                        dve.wait_ge(parts_ready, 3 * (g - 1))
                    dve.tensor_tensor(pre[:, b], ps[:, 2 * b:2 * b + 2, :].rearrange("p a (h f) -> p (a h) f", h=2),
                                      rows[:, b], ALU.add).then_inc(pre_ready, 1)
                if has(g, 2):
                    dve.wait_ge(summed, g - 1)
                    accumulate("mlp", g - 2, lambda j: ps[:, 4 + j, 0:3 * P].rearrange("p (c n) -> p c n", c=3),
                               lambda t: sum_T[:, :, bass.ds(t * P, P)])
                if has(g, 1):
                    q = 1 - b
                    dve.wait_ge(parts_ready, 3 * g)
                    dve.scalar_tensor_tensor(pos_part[:, q], neg_part[:, q], -1.0, pos_part[:, q], ALU.add, ALU.add)\
                       .then_inc(elu_ready, 1)
            slots(dve, mlp_slot, 2)
            dve.wait_ge(accumulated, G * NG)
            link(dve.tensor_scalar(inv_T[:, :], sum_T[:, 2, :], 1.0, None, ALU.max))
            link(dve.reciprocal(inv_T[:, :], inv_T[:, :]))
            dve.sem_inc(deg_summed, 1)

            def filled(name, u):
                n = FIRST_FILL[name] + u
                dve.wait_ge(fill_done, n + 1)
                return ps[:, n % RING, :]

            for c in range(NCOL):
                for m in range(2):
                    at = slice(c * COLS, (c + 1) * COLS)
                    dve.tensor_tensor(big[:, 3 + m, at], filled("agg0", 2 * c + m)[:, 0:COLS], inv_T[:, at], ALU.mult)\
                       .then_inc(read_by["dve"], 1)
            dve.wait_ge(read_by["dve"], 2 * NCOL)
            dve.sem_inc(agg0_ready, 2 * NCOL)
            for c in range(NCOL):
                for m in range(2):
                    u = 2 * c + m
                    dve.wait_ge(hid0_parts, u + 1)
                    dve.scalar_tensor_tensor(big[:, m, c * COLS:(c + 1) * COLS], neg_node(m), -1.0, pos_node(m),
                                             ALU.add, ALU.add).then_inc(hid0_ready, 1)
            for u, tiles in enumerate(packs(4)):
                at = slice(tiles[0], tiles[-1] + 1)
                dve.tensor_tensor(y_sb[:, at, :], filled("out0", u)[:, 0:len(tiles) * D]
                                  .rearrange("p (t f) -> p t f", f=D), x_sb[:, at, :], ALU.add)\
                   .then_inc(read_by["dve"], 1)
            dve.tensor_scalar(inv_row[:, :], filled("deg", 0)[:, 0:NT], 1.0, None, ALU.max).then_inc(read_by["dve"], 1)
            dve.wait_ge(read_by["dve"], fills_read(FIRST_FILL["x1T"], "dve"))
            link(dve.reciprocal(inv_row[:, :], inv_row[:, :]))

            def per_node(a):
                return a.unsqueeze(2).to_broadcast([P, NT, D])

            def norm(n):
                link(dve.tensor_reduce(stat[:, 0, :], y_sb[:, :, :], AX_X, ALU.add))
                link(dve.tensor_scalar(stat[:, 0, :], stat[:, 0, :], 1.0 / D, None, ALU.mult))
                dve.tensor_tensor(y_sb[:, :, :], y_sb[:, :, :], per_node(stat[:, 0, :]), ALU.subtract)\
                   .then_inc(centered, 1)
                dve.wait_ge(squared, n)
                link(dve.tensor_reduce(stat[:, 2, :], spare.rearrange("p (t f) -> p t f", t=NT), AX_X, ALU.add))
                dve.tensor_scalar(stat[:, 2, :], stat[:, 2, :], 1.0 / D, EPS, ALU.mult, ALU.add).then_inc(var_ready, 1)
                dve.wait_ge(rooted, n)
                link(dve.reciprocal(stat[:, 0, :], stat[:, 1, :]))
                dve.tensor_tensor(x_sb[:, :, :], y_sb[:, :, :], per_node(stat[:, 0, :]), ALU.mult).then_inc(x_ready, 1)
                dve.wait_ge(x_ready, n)

            norm(1)

            def attention_terms(k, a_src, a_dst, after):
                n, heads = SOFTMAX[k]
                dve.wait_ge(read_by["act"], fills_read(FIRST_FILL[after], "act"))
                prod = spare.rearrange("p (t f) -> p t f", t=NT)
                for row, to in ((a_src, h_sb[:, :, D:D + heads]), (a_dst, adst[:, :, 0:heads])):
                    link(dve.tensor_tensor(prod, h_sb[:, :, 0:D], over_tiles(spread(row)), ALU.mult))
                    link(dve.tensor_reduce(to, spare.rearrange("p (t h f) -> p t h f", t=NT, h=heads), AX_X, ALU.add))
                dve.sem_inc(h_ready, 1)
                dve.sem_inc(table_ready[k], 1)

            def softmax_pass(k):
                n, heads = SOFTMAX[k]
                at, all_at, width = n * NG, base[k], SUMS[k]
                acc = sum_rows(k)
                zero(k, acc)
                dve.memset(max_run[:, :, 0:1], 0.0)
                dve.memset(max_run[:, :, G * P:G * P + 1], 0.0)
                dve.memset(s_run[:, 1, G * P - 1:G * P], 0.0)
                link(dve.memset(w_run[:, 1, G * P - 1:G * P], 0.0))
                n_loads = 2 if heads else 1
                load_at = {"gat1": 0, "gat2": 2, "pool": 4}[k] * 16 * (NG // 2)

                def mark_nodes(x, b):
                    dve.wait_ge(neg_loaded[b], load_at + 16 * n_loads * (half(x, b) + 1))
                    if not early(x, 2):
                        dve.wait_ge(taken, at + x - 1)
                    dve.tensor_scalar(rel_T[:, b, :], rel_b[:, b, :], part[:, 0:1], None, ALU.is_equal)\
                       .then_inc(rel_ready, 1)

                def middle(x, b):
                    dve.wait_ge(exp_ready, at + x + 1)
                    if not early(x, 2):
                        dve.wait_ge(turn_done, at + x - 1)
                    decay, term = gaps[:, b, 0, :], gaps[:, b, 1, :]
                    value = ps[:, 2 + b, :] if heads else logit[:, b, :]
                    dve.tensor_tensor(hp[:, b, :], value, term, ALU.mult).then_inc(hp_ready, 1)
                    dve.tensor_tensor_scan(s_run[:, b, :], decay, term, s_run[:, 1 - b, G * P - 1:G * P],
                                           ALU.mult, ALU.add)
                    dve.wait_ge(hp_ready, at + x + 1)
                    dve.tensor_tensor_scan(w_run[:, b, :], decay, hp[:, b, :], w_run[:, 1 - b, G * P - 1:G * P],
                                           ALU.mult, ALU.add).then_inc(run_ready, 1)

                def front(x, b):
                    if heads:
                        dve.wait_ge(logit_turned, at + x + 1)
                        value = ps[:, b, :]
                    else:
                        dve.wait_ge(neg_loaded[b], load_at + 16 * n_loads * (half(x, b) + 1))
                        dve.wait_ge(taken, at + x + 1)
                        dve.wait_ge(ea_loaded[b], 16 * G * (NG // 2 + half(x, b) + 1))
                        dve.tensor_tensor(logit[:, b, :], ps[:, b, :],
                                          ea_sb[:, b].rearrange("p g e -> p (g e)"), ALU.add).then_inc(logit_ready, 1)
                        dve.wait_ge(logit_ready, at + x + 1)
                        value = logit[:, b, :]
                    if not early(x, 1):
                        dve.wait_ge(max_ready, at + x)
                    dve.tensor_copy(max_run[:, b, 0:1], max_run[:, 1 - b, G * P:G * P + 1]).then_inc(carry_ready, 1)
                    dve.wait_ge(carry_ready, at + x + 1)
                    dve.tensor_tensor_scan(max_run[:, b, 1:G * P + 1], neg_b[:, b, :], value,
                                           max_run[:, b, 0:1], ALU.add, ALU.max).then_inc(max_ready, 1)
                    dve.wait_ge(max_ready, at + x + 1)
                    dve.tensor_tensor(gaps[:, b, 0, :], max_run[:, b, 0:G * P], neg_b[:, b, :], ALU.add)\
                       .then_inc(old_max_ready, 1)
                    dve.tensor_tensor(gaps[:, b, 1, :], value, max_run[:, b, 1:G * P + 1], ALU.subtract)
                    dve.wait_ge(old_max_ready, at + x + 1)
                    dve.tensor_tensor(gaps[:, b, 0, :], gaps[:, b, 0, :], max_run[:, b, 1:G * P + 1], ALU.subtract)\
                       .then_inc(gaps_ready, 1)

                def leak(x, b):
                    dve.wait_ge(taken, at + x + 1)
                    if not early(x, 2):
                        dve.wait_ge(logit_ready, at + x - 1)
                    z = ps[:, 7, TERMS + b * G * heads:TERMS + (b + 1) * G * heads]
                    dve.tensor_scalar(leaks[:, b, 0, 0:G * heads], z, 0.2, None, ALU.mult).then_inc(leak_scaled, 1)
                    dve.wait_ge(leak_scaled, at + x + 1)
                    dve.tensor_tensor(leaks[:, b, 1, 0:G * heads], leaks[:, b, 0, 0:G * heads], z, ALU.max)\
                       .then_inc(leak_ready, 1)

                def slot(g, b):
                    if has(g) and heads:
                        mark_nodes(g, b)
                    if has(g, 2):
                        middle(g - 2, b)
                    if has(g, 1):
                        front(g - 1, 1 - b)
                    if has(g) and heads:
                        leak(g, b)
                    if has(g, 3):
                        dve.wait_ge(summed, all_at + g - 2)
                    if has(g, 1):
                        make_onehot(k, g - 1, 1 - b, last_rel)
                    if has(g, 3):
                        accumulate(k, g - 3, lambda j: ps[:, 6 + j // 2, (j % 2) * 256:(j % 2) * 256 + width]
                                   .unsqueeze(1), lambda t: acc[:, bass.ds(t, 1), :])
                slots(dve, slot, 3, head=4)
                dve.wait_ge(accumulated, G * (all_at + NG))
                return acc

            def attention_output(k, acc, bias):
                n, heads = SOFTMAX[k]
                m = NT * heads

                def sm(i):
                    return small[:, i, 0:m].rearrange("p (t h) -> p t h", t=NT)

                def over(a):
                    return a.unsqueeze(3).to_broadcast([P, NT, heads, D // heads])

                def heads_of(a):
                    return a.rearrange("p t (h f) -> p t h f", h=heads)

                total, top = acc[:, :, D:D + heads], acc[:, :, D + heads:D + 2 * heads]
                link(dve.tensor_tensor(sm(0), h_sb[:, :, D:D + heads], adst[:, :, 0:heads], ALU.add))
                link(dve.scalar_tensor_tensor(sm(1), sm(0), 0.2, sm(0), ALU.mult, ALU.max))
                link(dve.tensor_scalar(sm(0), total, 0.5, None, ALU.is_gt))
                link(dve.tensor_scalar(sm(0), sm(0), -1.0, -NEG, ALU.add, ALU.mult))
                link(dve.tensor_tensor(sm(0), sm(0), top, ALU.add))
                link(dve.tensor_tensor(sm(2), sm(0), sm(1), ALU.max))
                dve.tensor_tensor(sm(3), sm(0), sm(2), ALU.subtract)
                link(dve.tensor_tensor(sm(4), sm(1), sm(2), ALU.subtract))
                dve.drain().then_inc(gaps_in, 1)
                dve.wait_ge(gaps_out, n + 1)
                link(dve.tensor_tensor(sm(0), total, sm(3), ALU.mult))
                link(dve.tensor_tensor(sm(0), sm(0), sm(4), ALU.add))
                link(dve.tensor_scalar(sm(0), sm(0), 1e-16, None, ALU.add))
                link(dve.reciprocal(sm(0), sm(0)))
                dve.tensor_tensor(sm(3), sm(3), sm(0), ALU.mult)
                link(dve.tensor_tensor(sm(4), sm(4), sm(0), ALU.mult))
                dve.tensor_tensor(heads_of(y_sb[:, :, :]), heads_of(acc[:, :, 0:D]), over(sm(3)), ALU.mult)
                loop = spare.rearrange("p (t f) -> p t f", t=NT)
                link(dve.tensor_tensor(heads_of(loop), heads_of(h_sb[:, :, 0:D]), over(sm(4)), ALU.mult))
                link(dve.tensor_tensor(y_sb[:, :, :], y_sb[:, :, :], loop, ALU.add))
                link(dve.tensor_tensor(y_sb[:, :, :], y_sb[:, :, :], over_tiles(spread(bias)), ALU.add))

            dve.wait_ge(weights_loaded, 48)
            attention_terms("gat1", "as1", "ad1", "gT")
            attention_output("gat1", softmax_pass("gat1"), "gb1")
            dve.sem_inc(g_ready, 1)
            dve.wait_ge(g_low, 1)
            link(dve.tensor_scalar(y_sb[:, :, :], y_sb[:, :, :], 0.0, None, ALU.max))
            dve.scalar_tensor_tensor(y_sb[:, :, :], spare.rearrange("p (t f) -> p t f", t=NT), -1.0, y_sb[:, :, :],
                                     ALU.add, ALU.add).then_inc(g1_ready, 1)
            attention_terms("gat2", "as2", "ad2", "x2T")
            attention_output("gat2", softmax_pass("gat2"), "gb2")
            link(dve.tensor_tensor(y_sb[:, :, :], y_sb[:, :, :], x_sb[:, :, :], ALU.add))
            norm(2)
            dve.sem_inc(table_ready["sage0"], 1)

            def sum_pass(k, by_row):
                all_at = base[k]
                chunks = ROW[k] // P
                rows_acc = sum_rows(k) if by_row else None
                zero(k, rows_acc if by_row else big[:, 0:chunks, :])

                def slot(g, b):
                    if has(g):
                        if not early(g, 2):
                            dve.wait_ge(summed, all_at + g - 1)
                        make_onehot(k, g, b, dst_rel)
                    if has(g, 1):
                        q = 1 - b
                        dve.wait_ge(summed, all_at + g)
                        if by_row:
                            accumulate(k, g - 1, lambda j: ps[:, 4 + 2 * q + j // 2, (j % 2) * 256:(j % 2) * 256 + P]
                                       .unsqueeze(1), lambda t: rows_acc[:, bass.ds(t, 1), :])
                        else:
                            accumulate(k, g - 1, lambda j: ps[:, 4 + 2 * q + j // 2,
                                                              (j % 2) * 256:(j % 2) * 256 + chunks * P]
                                       .rearrange("p (c n) -> p c n", c=chunks),
                                       lambda t: big[:, 0:chunks, bass.ds(t * P, P)])
                slots(dve, slot, 1)
                dve.wait_ge(accumulated, G * (all_at + NG))

            sum_pass("sage0", False)
            dve.tensor_tensor(big[:, 0, :], big[:, 0, :], inv_T[:, :], ALU.mult).then_inc(agg_scaled, 1)
            dve.wait_ge(table_written, 16 * 5)
            sum_pass("sage1", False)
            dve.tensor_tensor(big[:, 0, :], big[:, 0, :], inv_T[:, :], ALU.mult)
            link(dve.tensor_tensor(big[:, 1, :], big[:, 1, :], inv_T[:, :], ALU.mult))
            dve.sem_inc(agg_scaled, 1)
            dve.wait_ge(read_by["act"], fills_read(FIRST_FILL["out2"], "act"))
            sum_pass("sage2", True)
            by_node = sum_rows("sage2")
            link(dve.tensor_tensor(by_node, by_node, per_node(inv_row[:, :]), ALU.mult))
            for u, tiles in enumerate(packs(4)):
                at = slice(tiles[0], tiles[-1] + 1)
                dve.tensor_tensor(y_sb[:, at, :], filled("out2", u)[:, 0:len(tiles) * D]
                                  .rearrange("p (t f) -> p t f", f=D), by_node[:, at, :], ALU.add)\
                   .then_inc(read_by["dve"], 1)
            dve.wait_ge(read_by["dve"], fills_read(FIRST_FILL["aT"], "dve"))
            link(dve.scalar_tensor_tensor(y_sb[:, :, :], y_sb[:, :, :], 0.0, x_sb[:, :, :], ALU.max, ALU.add))
            norm(3)
            dve.sem_inc(table_ready["pool"], 1)
            acc = softmax_pass("pool")
            link(dve.tensor_scalar(acc[:, :, D:2 * D], acc[:, :, D:2 * D], 1.0, None, ALU.max))
            link(dve.reciprocal(acc[:, :, D:2 * D], acc[:, :, D:2 * D]))
            dve.tensor_tensor(y_sb[:, :, :], acc[:, :, 0:D], acc[:, :, D:2 * D], ALU.mult).then_inc(agg3_ready, 1)
            dve.wait_ge(read_by["act"], fills_read(len(FILLS), "act"))
            link(dve.tensor_tensor(y_sb[:, :, :], y_sb[:, :, :], over_tiles(spread("scale")), ALU.mult))
            link(dve.scalar_tensor_tensor(y_sb[:, :, :], x_sb[:, :, :], 2.0, y_sb[:, :, :], ALU.mult, ALU.add))
            dve.wait_ge(table_written, 16 * 7)
            norm(4)


def lay_out(inputs):
    import numpy as np

    a = {k: np.asarray(v) for k, v in inputs.items()}
    n = NCH * CH * P
    src = np.zeros(n, np.int32)
    src[:N_EDGES] = a["src"]
    dst = np.full(n + 2, PAD_NODE, np.int32)
    dst[0] = -1
    dst[1:1 + N_EDGES] = a["dst"]
    dst[-1] = -1
    tables = [src, dst[1:-1], dst[:-2], dst[2:]]
    edges_i = np.ascontiguousarray(np.stack(tables).reshape(4, NCH, CH, P).transpose(2, 0, 1, 3)).reshape(CH, -1)
    ea = np.zeros((NB * P, D), np.float32)
    ea[:N_EDGES] = a["edge_attr_128"]
    ea_blocks = np.ascontiguousarray(ea.reshape(NB, P, D).transpose(0, 2, 1))
    x_rows = np.zeros((NODES, D), np.float32)
    x_rows[:N_NODES] = a["x"]
    weights = {"W1a": a["L0_gnn_W1a"], "W1b": a["L0_gnn_W1b"], "W2a": a["L0_gnn_W2a"], "W2b": a["L0_gnn_W2b"],
               "gW1": a["L1_gnn_W1"], "gW2": a["L1_gnn_W2"], "Ws0": a["L2_gnn_Ws0"], "Wn0": a["L2_gnn_Wn0"],
               "Ws1": a["L2_gnn_Ws1"], "Wn1": a["L2_gnn_Wn1"], "Ws2": a["L2_gnn_Ws2"], "Wn2": a["L2_gnn_Wn2"],
               "mlpT": a["L3_gnn_mlp_w"].T, "b2a": a["L0_gnn_b2a"].reshape(2, P).T,
               "sb0": a["L2_gnn_b0"].reshape(2, P).T, "sb1": a["L2_gnn_b1"].reshape(2, P).T}
    cols = []
    for name, (c, m) in WEIGHTS.items():
        cols.append(weights[name].reshape(c, P, m).transpose(1, 0, 2).reshape(P, c * m))
    bias = {"b1a": a["L0_gnn_b1a"], "b1b": a["L0_gnn_b1b"], "b2b": a["L0_gnn_b2b"], "sb2": a["L2_gnn_b2"],
            "mlp_b": a["L3_gnn_mlp_b"]}
    spread = {"as1": a["L1_gnn_att_src1"], "ad1": a["L1_gnn_att_dst1"], "gb1": a["L1_gnn_b1"],
              "as2": a["L1_gnn_att_src2"], "ad2": a["L1_gnn_att_dst2"], "gb2": a["L1_gnn_b2"],
              "scale": a["L3_gnn_scale"]}
    return {
        "edges_i": edges_i, "ea_blocks": ea_blocks, "x_rows": x_rows, "xT_in": np.ascontiguousarray(x_rows.T),
        "wpack": np.ascontiguousarray(np.concatenate(cols, axis=1)),
        "bpack": np.concatenate([bias[k].reshape(-1) for k in BIAS_ROWS]).reshape(1, -1),
        "rpack": np.concatenate([spread[k].reshape(-1) for k in SPREAD_ROWS]).reshape(1, -1),
    }


def kernel(**inputs):
    import concourse.bacc as _bacc
    from concourse import mybir as _mybir
    from concourse.bass_utils import run_bass_kernel_spmd as _run

    nc = _bacc.Bacc("TRN2", target_bir_lowering=False, num_devices=1)
    arrays, args = {}, []
    for name, a in lay_out(inputs).items():
        arrays[f"in_{name}"] = a
        args.append(nc.dram_tensor(f"in_{name}", a.shape, _mybir.dt.from_np(a.dtype), kind="ExternalInput").ap())
    args.append(nc.dram_tensor("out_0", (N_NODES, D), F32, kind="ExternalOutput").ap())
    program(nc, *args)
    r = _run(nc, [arrays], core_ids=[0])
    return r.results[0]["out_0"]
```

```python
from contextlib import ExitStack

import concourse.bass as bass
from concourse import mybir

F32 = mybir.dt.float32
BF16 = mybir.dt.bfloat16
I32 = mybir.dt.int32
ALU = mybir.AluOpType
ACT = mybir.ActivationFunctionType
AX_X = mybir.AxisListType.X

P = 128
N_NODES, N_EDGES, D = 3125, 50000, 128
NB = -(-N_EDGES // P)
NT = 26
NODES = NT * P
S = NB + NT - 1
G = 4
UNROLL = 4
NG = S // G
CH = 98
NCH = 4
BCH = S // 4
COLS = 416
NCOL = NODES // COLS
PAD_NODE = NODES - 1
NEG = -1.0e30
EPS = 1e-5
HEADS = 4
assert NG % UNROLL == 0 and UNROLL % 2 == 0 and S % (2 * G) == 0 and NCH * CH >= NB and NCOL * COLS == NODES and S <= 512 and NT * P > N_NODES + 1

WEIGHTS = {"W1a": (2, 256), "W1bT": (2, 256), "W2a": (3, 256), "W2b": (2, 128), "gW1": (1, 128), "gW2": (1, 128),
           "gW1T": (1, 128), "gW2T": (1, 128), "att1": (1, 2), "att2": (1, 2), "b1b": (1, 2),
           "Ws0": (1, 256), "Wn0": (1, 256), "Ws1": (2, 256), "Wn1": (2, 256), "Ws2": (2, 128), "Wn2": (2, 128),
           "mlpT": (1, 128), "b2a": (1, 2), "sb0": (1, 2), "sb1": (1, 2)}
BIAS_ROWS = {"b1a": 256, "b2b": 128, "sb2": 128, "mlp_b": 128}
SPREAD_ROWS = {"gb1": 128, "gb2": 128, "scale": 128}


def offsets(sizes):
    at, out = 0, {}
    for name, n in sizes.items():
        out[name] = at
        at += n
    return out, at


W_AT, W_COLS = offsets({k: c * n for k, (c, n) in WEIGHTS.items()})
B_AT, B_COLS = offsets(BIAS_ROWS)
R_AT, R_COLS = offsets(SPREAD_ROWS)

PASSES = ["mlp", "gat1", "gat2", "sage0", "sage1", "sage2", "pool"]
ROW = {"mlp": 256, "gat1": D + HEADS, "gat2": D + 1, "sage0": 128, "sage1": 256, "sage2": 128, "pool": 128}
SUMS = {"mlp": 2 * P + 1, "gat1": D + 2 * HEADS, "gat2": D + 2, "sage0": P, "sage1": 2 * P, "sage2": P, "pool": 2 * D}
SOFTMAX = {"gat1": (0, HEADS), "gat2": (1, 1), "pool": (2, 0)}

STAGES = [("Wc", 3, "dve"), ("att", 2, "dve"), ("tab0", 13, "act"), ("mT", 14, "act"), ("flag", 7, "act"),
          ("hid0", 16, "act"), ("out0", 7, "dve"), ("invT", 7, "act"), ("x1T", 7, "act"), ("h1", 9, "act"),
          ("gT", 7, "act"), ("h2", 9, "act"), ("x2T", 7, "act"), ("sh0", 16, "act"), ("p1", 13, "act"),
          ("sh1", 16, "act"), ("p2", 7, "act"), ("out2", 7, "dve"), ("aT", 7, "act"), ("mo", 7, "act")]
FILLS = [(name, u, who) for name, n, who in STAGES for u in range(n)]
FIRST_FILL = {name: [f[0] for f in FILLS].index(name) for name, _, _ in STAGES}
RING = 4
TERMS = (384, 448)



def fills_read(upto, who):
    return sum(f[2] == who for f in FILLS[:upto])


def packs(per):
    return [list(range(a, min(a + per, NT))) for a in range(0, NT, per)]


def program(nc, edges_i, ea_blocks, x_rows, xT_in, wpack, bpack, rpack, out):
    with ExitStack() as ctx:
        def sb(name, shape, dt=F32):
            return ctx.enter_context(nc.sbuf_tensor(name, shape, dt))

        def sem(name):
            return ctx.enter_context(nc.semaphore(name))

        table = {k: nc.dram_tensor(f"table_{k}", (NODES, ROW[k]), F32, kind="Internal").ap() for k in PASSES}
        neg_rows = nc.dram_tensor("neg_rows", (S, P), BF16, kind="Internal").ap()
        rel_rows = nc.dram_tensor("rel_rows", (S, P), BF16, kind="Internal").ap()

        ps = ctx.enter_context(nc.psum_tensor("ps", [P, 8, 512], F32))
        big = sb("big", [P, 5, NODES])
        x_sb = sb("x_sb", [P, NT, D])
        xT = sb("xT", [P, NODES])
        h_sb = sb("h_sb", [P, NT, D + 2 * HEADS])
        inv_T = sb("inv_T", [P, NODES])
        y_sb = sb("y_sb", [P, NT, D])
        w_sb = sb("w_sb", [P, W_COLS])
        b_sb = sb("b_sb", [1, B_COLS])
        r_sb = sb("r_sb", [P, R_COLS])
        ident = sb("ident", [P, P])
        ones = sb("ones", [P, P])
        iota_i = sb("iota_i", [P, S], I32)
        iota = sb("iota", [P, S])
        part_i = sb("part_i", [P, 1], I32)
        part = sb("part", [P, 1])
        src_idx = sb("src_idx", [P, S + 2 * G], I32)
        dst_rel = sb("dst_rel", [P, S])
        last_rel = sb("last_rel", [P, S])
        tile_i = sb("tile_i", [1, S], I32)
        block_i = sb("block_i", [1, S], I32)
        adst = sb("adst", [P, NT, 3 * HEADS], BF16)
        Wc = sb("Wc", [P, 2, 256])
        bc = sb("bc", [1, 256])
        gcat = {"gat1": sb("gcat1", [P, D + 2 * HEADS]), "gat2": sb("gcat2", [P, D + 2])}
        att_block = sb("att_block", [P, 2 * HEADS])
        head_mask = sb("head_mask", [P, HEADS])
        small = sb("small", [P, 8, NT * HEADS])
        stat = sb("stat", [P, 3, NT])
        inv_row = sb("inv_row", [P, NT])
        leaks = sb("leaks", [P, 2, 3, G * HEADS])
        idx_stage = sb("idx_stage", [P, 2, 2 * G], I32)
        rows = sb("rows", [P, 2, G, 256])
        onehot = sb("onehot", [P, 2, G, P])
        ea_sb = sb("ea_sb", [P, 2, G, P])
        s_run = sb("s_run", [P, 2, G * P])
        w_run = sb("w_run", [P, 2, G * P])

        flat = big[:, :, :].rearrange("p a n -> p (a n)")

        def part_of_big(at, n):
            return flat[:, at:at + n]

        lo = 3 * NODES
        pre = part_of_big(lo, 2048).rearrange("p (b g f) -> p b g f", b=2, g=G)
        neg_part = part_of_big(lo + 2048, 2048).rearrange("p (b g f) -> p b g f", b=2, g=G)
        pos_part = part_of_big(lo + 4096, 2 * G * 257).rearrange("p (b g f) -> p b g f", b=2, g=G)
        rel_T = part_of_big(lo, 512).bitcast(BF16).rearrange("p (b n) -> p b n", b=2)
        logit = part_of_big(lo + 512, 1024).rearrange("p (b n) -> p b n", b=2)
        max_run = part_of_big(lo + 1536, 1028).rearrange("p (b n) -> p b n", b=2)
        gaps = part_of_big(lo + 2568, 2048).rearrange("p (b k n) -> p b k n", b=2, k=2)
        rise = part_of_big(lo + 4616, 1024).rearrange("p (b n) -> p b n", b=2)
        neg_b = part_of_big(lo + 5640, 512).bitcast(BF16).rearrange("p (b n) -> p b n", b=2)
        assert 5640 + 512 <= 2 * NODES and 4096 + 2 * G * 257 <= 2 * NODES
        rel_b = ea_sb[:, :, :, :].rearrange("p b g e -> p (b g e)")[:, 0:512].bitcast(BF16)\
            .rearrange("p (b n) -> p b n", b=2)

        edges_in = part_of_big(0, 2048).bitcast(I32)
        edges_f = part_of_big(2048, 2048).rearrange("p (k c e) -> p k c e", k=4, c=NCH)
        sel = part_of_big(4096, NCH * S).rearrange("p (c s) -> p c s", c=NCH)
        moved = part_of_big(5760, S)
        tile_f = part_of_big(6176, S)
        block_f = part_of_big(6592, S)
        ends = part_of_big(7008, NT)
        below = part_of_big(7040, NCH * NT).rearrange("p (c t) -> p c t", c=NCH)
        chunk_part = part_of_big(7150, NCH)
        key = part_of_big(7155, 1)
        last_f = part_of_big(7160, S)
        tile_col = part_of_big(7580, 4)
        row_f = part_of_big(7600, 4 * 2 * P).rearrange("p (q k e) -> p q k e", q=4, k=2)
        moved_last = part_of_big(9160, S)
        row_b = part_of_big(8640, 4 * 2 * P // 2).bitcast(BF16).rearrange("p (q k e) -> p q k e", q=4, k=2)

        sum_T = big[:, 0:3, :]

        def sum_rows(k):
            at = lo if k == "sage2" else 0
            return part_of_big(at, NT * SUMS[k]).rearrange("p (t f) -> p t f", t=NT)

        spare = big[:, 2, :]
        y_flat = y_sb[:, :, :].rearrange("p t f -> p (t f)")
        turned = y_flat[:, 0:2048].rearrange("p (b g f) -> p b g f", b=2, g=G)
        hp = y_flat[:, 2048:3072].rearrange("p (b n) -> p b n", b=2)
        hidden = h_sb[:, :, :].rearrange("p t f -> p (t f)")[:, 0:8 * COLS].rearrange("p (k u n) -> p k u n", k=2, u=4)
        flags = y_sb[0:1, :, :].rearrange("p t f -> p (t f)")

        def neg_node(m):
            return hidden[:, 0, m, :]

        def pos_node(m):
            return hidden[:, 1, m, :]

        def weight(name, c, m0=0, m=None):
            n = WEIGHTS[name][1]
            at = W_AT[name] + c * n + m0
            return w_sb[:, at:at + (n - m0 if m is None else m)]

        def bias_row(name, m0=0, m=None):
            at = B_AT[name] + m0
            return b_sb[0:1, at:at + (BIAS_ROWS[name] - m0 if m is None else m)]

        def spread(name):
            return r_sb[:, R_AT[name]:R_AT[name] + SPREAD_ROWS[name]]

        def over_tiles(row):
            return row.unsqueeze(1).to_broadcast([P, NT, D])

        def pick(t):
            return slice(t * P, (t + 1) * P)

        edges_loaded, weights_loaded, x_loaded = sem("edges_loaded"), sem("weights_loaded"), sem("x_loaded")
        iotas_ready, consts_ready = sem("iotas_ready"), sem("consts_ready")
        below_ready, keys_summed, moved_ready, tiles_spread = (
            sem("below_ready"), sem("keys_summed"), sem("moved_ready"), sem("tiles_spread"))
        rows_ready_parts = sem("rows_ready_parts")
        terms_ready, leak_ready = sem("terms_ready"), sem("leak_ready")
        hp_ready, carry_ready, old_max_ready = sem("hp_ready"), sem("carry_ready"), sem("old_max_ready")
        sel_ready, cols_moved, rows_moved, tables_ready, rows_ready, rows_stored = (
            sem("sel_ready"), sem("cols_moved"), sem("rows_moved"), sem("tables_ready"), sem("rows_ready"),
            sem("rows_stored"))
        dve_link, act_link = sem("dve_link"), sem("act_link")
        fill_done, read_by = sem("fill_done"), {"act": sem("read_by_act"), "dve": sem("read_by_dve")}
        table_ready = {k: sem(f"table_ready_{k}") for k in PASSES}
        table_written = sem("table_written")
        acc_zeroed = sem("acc_zeroed")
        att_built, terms_built, mean_ready, inv_ready = (
            sem("att_built"), sem("terms_built"), sem("mean_ready"), sem("inv_ready"))
        hid0_ready, hid0_parts = sem("hid0_ready"), sem("hid0_parts")
        adst_ready = sem("adst_ready")
        gaps_in, gaps_out = sem("node_gaps"), sem("node_gaps_exp")
        g_ready, g_low = sem("g_ready"), sem("g_low")
        g1_ready = sem("g1_ready")
        centered, squared, var_ready, rooted = sem("centered"), sem("squared"), sem("var_ready"), sem("rooted")
        x_ready = sem("x_ready")
        agg_scaled = sem("agg_scaled")
        agg3_ready = sem("agg3_ready")
        out_written = sem("out_written")
        gathered = [sem("gathered0"), sem("gathered1")]
        idx_staged, pool_tick = sem("idx_staged"), sem("pool_tick")
        onehot_ready, summed, accumulated = sem("onehot_ready"), sem("summed"), sem("accumulated")
        ea_loaded = [sem("ea_loaded0"), sem("ea_loaded1")]
        edge_product, pre_ready, parts_ready, elu_ready = (
            sem("edge_product"), sem("pre_ready"), sem("parts_ready"), sem("elu_ready"))
        neg_loaded = [sem("neg_loaded0"), sem("neg_loaded1")]
        rel_loaded = [sem("rel_loaded0"), sem("rel_loaded1")]
        squares_ready, term_done, heads_turned = sem("squares_ready"), sem("term_done"), sem("heads_turned")
        dst_terms_ready = sem("dst_terms_ready")
        rel_ready, taken, logit_ready, logit_turned = (
            sem("rel_ready"), sem("taken"), sem("logit_ready"), sem("logit_turned"))
        max_ready, rise_ready, gaps_split, exp_ready, run_ready = (
            sem("max_ready"), sem("rise_ready"), sem("gaps_split"), sem("exp_ready"), sem("run_ready"))
        turn_done, turned_ready = sem("turn_done"), sem("turned_ready")

        def has(g, back=0):
            return not isinstance(g, int) or 0 <= g - back < NG

        def early(x, n):
            return isinstance(x, int) and x < n

        def slots(eng, slot, tail, head=2, tiles_of=None):
            head = -(-head // UNROLL) * UNROLL

            def tiles(g, groups):
                if not tiles_of or not has(g, tiles_of[1]):
                    return [()] * groups
                values = step_values(tiles_of[0], tile_i, g - tiles_of[1], NT - 1, groups)
                return [(values[u * G:(u + 1) * G],) for u in range(groups)]

            for g in range(head):
                slot(g, g % 2, *tiles(g, 1)[0])
            with eng.Fori(head // UNROLL, NG // UNROLL) as i:
                values = tiles(i * UNROLL, UNROLL)
                for u in range(UNROLL):
                    slot(i * UNROLL + u, u % 2, *values[u])
            for g in range(NG, NG + tail):
                slot(g, g % 2, *tiles(g, 1)[0])

        def half(g, b):
            return g // 2 if isinstance(g, int) else (g - b) // 2

        def step_values(eng_type, ints, g, top, groups=1):
            return nc.values_load_multi_w_load_instructions(
                ints[0:1, bass.ds(g * G, groups * G)], engines=(eng_type,), min_val=0, max_val=top,
                skip_runtime_bounds_check_because="the merge path, counted on the chip, stays in the grid")[1]

        base = {k: NG * n for n, k in enumerate(PASSES)}
        ea_base = {"mlp": 0, "pool": NG}

        block = ctx.enter_context(nc.Block())

        @block.sync
        def _(sp):
            sp.dma_start(edges_in[0:CH, :], edges_i).then_inc(edges_loaded, 16)
            sp.dma_start(xT[:, :], xT_in).then_inc(x_loaded, 16)
            sp.dma_start(x_sb[:, :, :], x_rows.rearrange("(t p) f -> p t f", p=P)).then_inc(x_loaded, 16)
            sp.wait_ge(rows_ready, 1)
            for q in range(4):
                sp.dma_start(neg_rows[q * BCH:(q + 1) * BCH, :], row_b[0:BCH, q, 0, :]).then_inc(rows_stored, 16)
                sp.dma_start(rel_rows[q * BCH:(q + 1) * BCH, :], row_b[0:BCH, q, 1, :]).then_inc(rows_stored, 16)

            def write_table(k, rows_sb):
                sp.wait_ge(table_ready[k], 1)
                sp.dma_start(table[k].rearrange("(t p) f -> p t f", p=P), rows_sb).then_inc(table_written, 16)

            def load_ea(g, b, freed, at):
                if not early(g, 2):
                    sp.wait_ge(freed, at + g - 1)
                for j, blk in enumerate(step_values(mybir.EngineType.SP, block_i, g, NB - 1)):
                    sp.dma_start(ea_sb[:, b, j, :], ea_blocks[bass.ds(blk, 1), :, :].rearrange("o p e -> p (o e)"))\
                      .then_inc(ea_loaded[b], 16)

            def load_rows_of(rows_in_dram, to, loaded, g, b):
                sp.dma_start(to[:, b, :],
                             rows_in_dram[bass.ds(g * G, G), :].rearrange("s e -> (s e)").partition_broadcast(P))\
                  .then_inc(loaded[b], 16)

            wide = big[:, 3:5, :].rearrange("p a n -> p (a n)").rearrange("p (t f) -> p t f", t=NT)
            low = big[:, 0:2, :].rearrange("p a n -> p (a n)").rearrange("p (t f) -> p t f", t=NT)
            write_table("mlp", wide)
            sp.wait_ge(tables_ready, 1)
            slots(sp, lambda g, b: load_ea(g, b, edge_product, 0), 0)

            def softmax_rows(k):
                n, heads = SOFTMAX[k]
                sp.wait_ge(rows_stored, 128)
                sp.wait_ge(acc_zeroed, PASSES.index(k) + 1)

                def slot(s, b):
                    if has(s, 1):
                        if not early(s, 3):
                            sp.wait_ge(rise_ready, n * NG + s - 2)
                        load_rows_of(neg_rows, neg_b, neg_loaded, s - 1, 1 - b)
                    if has(s):
                        if not heads:
                            load_ea(s, b, taken, n * NG)
                        else:
                            if not early(s, 2):
                                sp.wait_ge(rel_ready, n * NG + s - 1)
                            load_rows_of(rel_rows, rel_b, rel_loaded, s, b)
                slots(sp, slot, 1, head=4)

            write_table("gat1", h_sb[:, :, 0:ROW["gat1"]])
            softmax_rows("gat1")
            write_table("gat2", h_sb[:, :, 0:ROW["gat2"]])
            softmax_rows("gat2")
            write_table("sage0", x_sb[:, :, :])
            write_table("sage1", low)
            write_table("sage2", h_sb[:, :, 0:D])
            write_table("pool", x_sb[:, :, :])
            softmax_rows("pool")
            sp.wait_ge(x_ready, 4)
            full = N_NODES // P
            sp.dma_start(out[0:full * P, :].rearrange("(t p) f -> p t f", p=P), x_sb[:, 0:full, :])\
              .then_inc(out_written, 16)
            sp.dma_start(out[full * P:N_NODES, :], x_sb[0:N_NODES - full * P, full, :]).then_inc(out_written, 16)
            sp.wait_ge(out_written, 32)

        @block.gpsimd
        def _(pool):
            pool.iota(iota_i[:, :], pattern=[[1, S]], base=0, channel_multiplier=0).then_inc(iotas_ready, 1)
            pool.iota(part_i[:, :], pattern=[[0, 1]], base=0, channel_multiplier=1).then_inc(iotas_ready, 1)
            pool.wait_ge(tables_ready, 1)

            def gather_pass(k, *freed):
                first = base[k] // 2

                def stage(pair, to):
                    pool.tensor_copy(idx_stage[:, to, :], src_idx[:, bass.ds(pair * 2 * G, 2 * G)])\
                        .then_inc(idx_staged, 1)

                def pair(p, par, peeled):
                    for b in range(2):
                        if not (peeled and p == 0):
                            for read, read_at in freed:
                                pool.wait_ge(read, read_at + p * 2 + b - 1)
                        if b == 0:
                            pool.wait_ge(idx_staged, PASSES.index(k) * (NG // 2 + 1) + p + 1)
                            pool.sem_inc(pool_tick, 1)
                        else:
                            stage(p + 1, 1 - par)
                        for j in range(G):
                            pool.indirect_dma_start(
                                rows[:, b, j, 0:ROW[k]], None, table[k],
                                bass.IndirectOffsetOnAxis(idx_stage[:, par, b * G + j:b * G + j + 1], 0))\
                                .then_inc(gathered[b], 16)

                pool.wait_ge(table_written, 16 * (PASSES.index(k) + 1))
                if first:
                    pool.wait_ge(idx_staged, PASSES.index(k) * (NG // 2 + 1))
                stage(0, 0)
                pair(0, 0, True)
                pair(1, 1, True)
                with pool.Fori(1, NG // 4) as i:
                    pair(i * 2, 0, False)
                    pair(i * 2 + 1, 1, False)

            gather_pass("mlp", (pre_ready, 0))
            gather_pass("gat1", (leak_ready, 0), (taken, 0))
            gather_pass("gat2", (leak_ready, NG), (taken, NG))
            gather_pass("sage0", (summed, base["sage0"]))
            gather_pass("sage1", (summed, base["sage1"]))
            gather_pass("sage2", (summed, base["sage2"]))
            gather_pass("pool", (taken, 2 * NG))

        @block.tensor
        def _(pe):
            pe.wait_ge(below_ready, 1)
            for c in range(NCH):
                mm = pe.matmul(ps[0:NT - 1, 0, 0:1], below[0:CH, c, 0:NT - 1], ones[0:CH, 0:1],
                               start=(c == 0), stop=(c == NCH - 1))
            mm.then_inc(keys_summed, 1)
            pe.wait_ge(moved_ready, 1)
            pe.matmul(ps[:, 1, 0:S], ones[0:NT - 1, :], moved[0:NT - 1, :], start=True, stop=True)\
              .then_inc(tiles_spread, 1)
            pe.wait_ge(sel_ready, 1)
            for n, k in enumerate((0, 1, 3)):
                for c in range(NCH):
                    mm = pe.matmul(ps[:, 2 + n, 0:S], edges_f[0:CH, k, c, :], sel[0:CH, c, :],
                                   start=(c == 0), stop=(c == NCH - 1))
                mm.then_inc(cols_moved, 1)
            for q in range(4):
                at = slice(q * BCH, (q + 1) * BCH)
                for n, k in enumerate((1, 2)):
                    for c in range(NCH):
                        pe.matmul(ps[0:BCH, 5 + q % 2, n * P:(n + 1) * P], sel[0:CH, c, at], edges_f[0:CH, k, c, :],
                                  start=(c == 0), stop=(c == NCH - 1))
                mm = pe.matmul(ps[0:BCH, 5 + q % 2, 2 * P:2 * P + 1], moved[0:NT - 1, at], ones[0:NT - 1, 0:1],
                               start=True, stop=True)
                mm.then_inc(rows_moved, 1)
                if 1 <= q < 3:
                    pe.wait_ge(rows_ready_parts, q)

            def fill(name, u):
                n = FIRST_FILL[name] + u
                if n >= RING:
                    who = FILLS[n - RING][2]
                    pe.wait_ge(read_by[who], fills_read(n - RING + 1, who))
                return ps[:, n % RING, :]

            def row_products(name, per, width, terms, bias):
                for u, tiles in enumerate(packs(per)):
                    bank = fill(name, u)
                    for i, t in enumerate(tiles):
                        to = bank[:, i * width:(i + 1) * width]
                        for n, (act, w) in enumerate(terms):
                            mm = pe.matmul(to, act[:, pick(t)], w, start=(n == 0),
                                           stop=(n == len(terms) - 1 and bias is None))
                        if bias is not None:
                            mm = pe.matmul(to, ones[0:1, :], bias, start=False, stop=True)
                    mm.then_inc(fill_done, 1)

            def column_products(name, terms_of):
                for c in range(NCOL):
                    at = slice(c * COLS, (c + 1) * COLS)
                    for m in range(2):
                        bank = fill(name, 2 * c + m)
                        terms = terms_of(m)
                        for n, (w, act) in enumerate(terms):
                            mm = pe.matmul(bank[:, 0:COLS], w, act[:, at], start=(n == 0), stop=(n == len(terms) - 1))
                        mm.then_inc(fill_done, 1)

            def turn_rows(name, of):
                for u, tiles in enumerate(packs(4)):
                    bank = fill(name, u)
                    for i, t in enumerate(tiles):
                        mm = pe.transpose(bank[:, i * P:(i + 1) * P], of(t), ident[:, :])
                    mm.then_inc(fill_done, 1)

            pe.wait_ge(weights_loaded, 48)
            pe.wait_ge(x_loaded, 32)
            pe.wait_ge(rows_ready, 1)
            for m in range(2):
                bank = fill("Wc", m)
                for k in range(2):
                    mm = pe.matmul(bank[:, 0:256], weight("W1bT", k, m * P, P), weight("W2a", 1 + k),
                                   start=(k == 0), stop=(k == 1))
                mm.then_inc(fill_done, 1)
            bank = fill("Wc", 2)
            for k in range(2):
                mm = pe.matmul(bank[0:1, 0:256], weight("b1b", 0, k, 1), weight("W2a", 1 + k),
                               start=(k == 0), stop=(k == 1))
            mm.then_inc(fill_done, 1)
            pe.wait_ge(att_built, 1)
            pe.matmul(fill("att", 0)[:, 0:2 * HEADS], weight("gW1T", 0), att_block[:, :], start=True, stop=True)\
              .then_inc(fill_done, 1)
            pe.matmul(fill("att", 1)[:, 0:2], weight("gW2T", 0), weight("att2", 0), start=True, stop=True)\
              .then_inc(fill_done, 1)
            row_products("tab0", 2, 256, [(xT, weight("W1a", 0))], bias_row("b1a"))

            def mlp_slot(g, b):
                if has(g):
                    if not early(g, 2):
                        pe.wait_ge(pre_ready, g - 1)
                    pe.wait_ge(ea_loaded[b], 16 * G * (half(g, b) + 1))
                    for j in range(G):
                        mm = pe.matmul(ps[:, 2 * b + j // 2, (j % 2) * 256:(j % 2) * 256 + 256], ea_sb[:, b, j, :],
                                       weight("W1a", 1), start=True, stop=True)
                    mm.then_inc(edge_product, 1)
                if has(g, 3):
                    pe.wait_ge(elu_ready, g - 2)
                    pe.wait_ge(onehot_ready, g - 2)
                    q = 1 - b
                    for j in range(G):
                        if has(g, 4):
                            pe.wait_ge(accumulated, G * (g - 4) + j + 1)
                        mm = pe.matmul(ps[:, 4 + j, 0:SUMS["mlp"]], onehot[:, q, j, :], pos_part[:, q, j, :],
                                       start=True, stop=True)
                    mm.then_inc(summed, 1)

            pe.wait_ge(read_by["act"], fills_read(FIRST_FILL["mT"], "act"))
            slots(pe, mlp_slot, 3, head=4)

            pe.wait_ge(mean_ready, 1)
            mean = sum_rows("mlp")
            for m in range(2):
                for u, tiles in enumerate(packs(4)):
                    bank = fill("mT", 7 * m + u)
                    for i, t in enumerate(tiles):
                        mm = pe.transpose(bank[:, i * P:(i + 1) * P], mean[:, t, m * P:(m + 1) * P], ident[:, :])
                    mm.then_inc(fill_done, 1)
            for u, tiles in enumerate(packs(4)):
                bank = fill("flag", u)
                for i, t in enumerate(tiles):
                    mm = pe.transpose(bank[0:1, i * P:(i + 1) * P], mean[:, t, 2 * P:2 * P + 1], ident[:, :])
                mm.then_inc(fill_done, 1)
            pe.wait_ge(read_by["act"], fills_read(FIRST_FILL["hid0"], "act"))
            column_products("hid0", lambda m: [(weight("W2a", 0, m * P, P), xT),
                                               (Wc[:, 0, m * P:(m + 1) * P], big[:, 3, :]),
                                               (Wc[:, 1, m * P:(m + 1) * P], big[:, 4, :]),
                                               (bc[0:1, m * P:(m + 1) * P], flags)])
            pe.wait_ge(hid0_ready, 2 * NCOL)
            row_products("out0", 4, D, [(big[:, 0, :], weight("W2b", 0)), (big[:, 1, :], weight("W2b", 1))],
                         bias_row("b2b"))
            for u, tiles in enumerate(packs(4)):
                bank = fill("invT", u)
                for i, t in enumerate(tiles):
                    mm = pe.matmul(bank[:, i * P:(i + 1) * P], inv_row[:, t:t + 1].to_broadcast([P, P]), ident[:, :],
                                   start=True, stop=True)
                mm.then_inc(fill_done, 1)
            pe.wait_ge(x_ready, 1)
            turn_rows("x1T", lambda t: x_sb[:, t, :])
            pe.wait_ge(read_by["act"], fills_read(FIRST_FILL["h1"], "act"))
            row_products("h1", 3, D + 2 * HEADS, [(xT, gcat["gat1"][:, :])], None)

            def softmax_pass(k):
                n, heads = SOFTMAX[k]
                at, all_at = n * NG, base[k]
                width = SUMS[k]
                if heads:
                    pe.wait_ge(adst_ready, n + 1)

                def take(x, b):
                    pe.wait_ge(gathered[b], 16 * G * (all_at // 2 + half(x, b) + 1))
                    if not heads:
                        pe.wait_ge(ea_loaded[b], 16 * G * (NG // 2 + half(x, b) + 1))
                    if not early(x, 2):
                        pe.wait_ge(hp_ready, at + x - 1)
                    for j in range(G):
                        if heads:
                            mm = pe.transpose(ps[:, 2 + b, j * P:(j + 1) * P], rows[:, b, j, 0:D], ident[:, :])
                        else:
                            to = ps[:, b, j * P:(j + 1) * P]
                            pe.matmul(to, ident[:, :], ea_sb[:, b, j, :], start=True, stop=False)
                            mm = pe.matmul(to, rows[:, b, j, 0:D], ident[:, :], start=False, stop=True)
                    mm.then_inc(taken, 1)

                def add_terms(x, b, tiles):
                    pe.wait_ge(rel_ready, at + x + 1)
                    if not early(x, 1):
                        pe.wait_ge(dst_terms_ready, at + x)
                    if not early(x, 4):
                        pe.wait_ge(turned_ready, at + x - 3)
                    for j, t in enumerate(tiles):
                        at_j = TERMS[b] + j * 3 * heads
                        mm = pe.matmul(ps[:, 5, at_j:at_j + 3 * heads], rel_T[:, b, j * P:(j + 1) * P],
                                       adst[:, bass.ds(t, 1), 0:3 * heads].rearrange("p o h -> p (o h)"),
                                       start=True, stop=True)
                    mm.then_inc(term_done, 1)

                def spread_logits(x, b):
                    pe.wait_ge(logit_ready, at + x + 1)
                    if not early(x, 2):
                        pe.wait_ge(rise_ready, at + x - 1)
                    for j in range(G):
                        mm = pe.transpose(ps[:, b, j * P:(j + 1) * P], logit[:, b, j * P:(j + 1) * P], ident[:, :])
                    mm.then_inc(logit_turned, 1)

                def turn_maxima(x, b):
                    for j in range(G):
                        at_j = ((b * G + j) * 2 + 1) * heads
                        mm = pe.transpose(ps[:, 5, at_j:at_j + heads], max_run[0:heads, b, 1 + j * P:1 + (j + 1) * P],
                                          ident[0:heads, 0:heads])
                    mm.then_inc(heads_turned, 1)

                def wait_for_maxima(x):
                    pe.wait_ge(max_ready, at + x + 1)
                    pe.wait_ge(dst_terms_ready, min(at + x + 3, at + NG) if isinstance(x, int) else at + x + 3)
                    if not early(x, 2):
                        pe.wait_ge(turned_ready, at + x - 1)

                def turn_both(s, b):
                    x = s - 4
                    if has(s, 4):
                        pe.wait_ge(run_ready, at + x + 1)
                        if not early(x, 1):
                            pe.wait_ge(turned_ready, at + x)
                    for j in range(G):
                        if j == G - 1 and heads and has(s, 3):
                            wait_for_maxima(s - 3)
                        if has(s, 4):
                            cols = slice(j * P, (j + 1) * P)
                            mm = pe.transpose(ps[:, 4, cols], w_run[:, b, cols], ident[:, :])
                    if heads and has(s, 3):
                        turn_maxima(s - 3, 1 - b)
                    if has(s, 4):
                        for j in range(G):
                            cols = slice(j * P, (j + 1) * P)
                            if heads:
                                at_j = (b * G + j) * 2 * heads
                                mm = pe.transpose(ps[:, 5, at_j:at_j + heads], s_run[0:heads, b, cols],
                                                  ident[0:heads, 0:heads])
                            else:
                                mm = pe.transpose(ps[:, 5, cols], s_run[:, b, cols], ident[:, :])
                        mm.then_inc(turn_done, 1)

                def finish(x, b):
                    pe.wait_ge(turned_ready, at + x + 1)
                    pe.wait_ge(onehot_ready, all_at + x + 1)
                    for j in range(G):
                        if not early(x, 1) and j % 2 == 0:
                            pe.wait_ge(accumulated, G * (all_at + x - 1) + j + 2)
                        mm = pe.matmul(ps[:, 6 + j // 2, (j % 2) * 256:(j % 2) * 256 + width], onehot[:, b, j, :],
                                       turned[:, b, j, 0:width], start=True, stop=True)
                    mm.then_inc(summed, 1)

                def slot(s, b, tiles=None):
                    turn_both(s, b)
                    if has(s, 1):
                        take(s - 1, 1 - b)
                    if has(s, 1) and heads:
                        spread_logits(s - 1, 1 - b)
                    if has(s) and heads:
                        add_terms(s, b, tiles)
                    if has(s, 4):
                        finish(s - 4, b)
                slots(pe, slot, 4, head=6, tiles_of=(mybir.EngineType.PE, 0) if heads else None)

            pe.wait_ge(read_by["act"], fills_read(FIRST_FILL["gT"], "act"))
            softmax_pass("gat1")
            pe.wait_ge(g1_ready, 1)
            turn_rows("gT", lambda t: y_sb[:, t, :])
            pe.wait_ge(read_by["act"], fills_read(FIRST_FILL["h2"], "act"))
            row_products("h2", 3, D + 2, [(big[:, 3, :], gcat["gat2"][:, :])], None)
            pe.wait_ge(read_by["act"], fills_read(FIRST_FILL["x2T"], "act"))
            softmax_pass("gat2")
            pe.wait_ge(x_ready, 2)
            turn_rows("x2T", lambda t: x_sb[:, t, :])

            def sum_pass(k, by_row):
                all_at = base[k]
                chunks = ROW[k] // P

                def slot(g, b):
                    pe.wait_ge(gathered[b], 16 * G * (all_at // 2 + half(g, b) + 1))
                    pe.wait_ge(onehot_ready, all_at + g + 1)
                    if not early(g, 2):
                        pe.wait_ge(accumulated, G * (all_at + g - 1))
                    for j in range(G):
                        to = ps[:, 4 + 2 * b + j // 2, (j % 2) * 256:(j % 2) * 256 + 256]
                        if by_row:
                            mm = pe.matmul(to[:, 0:P], onehot[:, b, j, :], rows[:, b, j, 0:P], start=True, stop=True)
                        else:
                            for c in range(chunks):
                                mm = pe.matmul(to[:, c * P:(c + 1) * P], rows[:, b, j, c * P:(c + 1) * P],
                                               onehot[:, b, j, :], start=True, stop=True)
                    mm.then_inc(summed, 1)
                slots(pe, slot, 0)

            sum_pass("sage0", False)
            pe.wait_ge(agg_scaled, 1)
            pe.wait_ge(read_by["act"], fills_read(FIRST_FILL["sh0"], "act"))
            column_products("sh0", lambda m: [(weight("Ws0", 0, m * P, P), xT),
                                              (weight("Wn0", 0, m * P, P), sum_T[:, 0, :])])
            pe.wait_ge(read_by["act"], fills_read(FIRST_FILL["p1"], "act"))
            row_products("p1", 2, 256, [(big[:, 3, :], weight("Wn1", 0)), (big[:, 4, :], weight("Wn1", 1))], None)
            sum_pass("sage1", False)
            pe.wait_ge(agg_scaled, 2)
            column_products("sh1", lambda m: [(weight("Ws1", 0, m * P, P), big[:, 3, :]),
                                              (weight("Ws1", 1, m * P, P), big[:, 4, :]),
                                              (ident[:, :], sum_T[:, m, :])])
            pe.wait_ge(read_by["act"], fills_read(FIRST_FILL["p2"], "act"))
            row_products("p2", 4, D, [(big[:, 0, :], weight("Wn2", 0)), (big[:, 1, :], weight("Wn2", 1))], None)
            sum_pass("sage2", True)
            row_products("out2", 4, D, [(big[:, 0, :], weight("Ws2", 0)), (big[:, 1, :], weight("Ws2", 1))],
                         bias_row("sb2"))
            pe.wait_ge(read_by["dve"], fills_read(FIRST_FILL["aT"], "dve"))
            softmax_pass("pool")
            pe.wait_ge(agg3_ready, 1)
            turn_rows("aT", lambda t: y_sb[:, t, :])
            pe.wait_ge(read_by["act"], fills_read(FIRST_FILL["mo"], "act"))
            row_products("mo", 4, D, [(xT, weight("mlpT", 0))], bias_row("mlp_b"))

        @block.scalar
        def _(act):
            links = [0]

            def link(ins):
                links[0] += 1
                ins.then_inc(act_link, 1)
                act.wait_ge(act_link, links[0])

            act.dma_start(w_sb[:, :], wpack).then_inc(weights_loaded, 16)
            act.dma_start(b_sb[:, :], bpack).then_inc(weights_loaded, 16)
            act.dma_start(r_sb[:, :], rpack.rearrange("o n -> (o n)").partition_broadcast(P)).then_inc(weights_loaded, 16)

            fills = [0]

            def filled(name, u):
                n = FIRST_FILL[name] + u
                act.wait_ge(fill_done, n + 1)
                return ps[:, n % RING, :]

            def copy_rows(name, per, width, to, func=ACT.Copy):
                for u, tiles in enumerate(packs(per)):
                    bank = filled(name, u)[:, 0:len(tiles) * width].rearrange("p (t f) -> p t f", f=width)
                    act.activation(to[:, tiles[0]:tiles[-1] + 1, 0:width], bank, func).then_inc(read_by["act"], 1)

            def copy_turned(name, to):
                for u, tiles in enumerate(packs(4)):
                    bank = filled(name, u)
                    act.activation(to[:, tiles[0] * P:(tiles[-1] + 1) * P], bank[:, 0:len(tiles) * P], ACT.Copy)\
                       .then_inc(read_by["act"], 1)

            low = big[:, 0:2, :].rearrange("p a n -> p (a n)").rearrange("p (t f) -> p t f", t=NT)
            wide = big[:, 3:5, :].rearrange("p a n -> p (a n)").rearrange("p (t f) -> p t f", t=NT)
            copy_rows("tab0", 2, 256, wide)
            act.wait_ge(read_by["act"], fills_read(FIRST_FILL["mT"], "act"))
            act.sem_inc(table_ready["mlp"], 1)

            def square_distances(k, x, b, values):
                if not early(x, 2):
                    act.wait_ge(summed, base[k] + x - 1)
                for j in range(G):
                    ins = act.activation(onehot[:, b, j, :], iota[:, 0:P], ACT.Square,
                                         bias=values[:, bass.ds(x * G + j, 1)], scale=-1.0)
                ins.then_inc(squares_ready, 1)

            def mark_edges(nth, x, b):
                act.wait_ge(squares_ready, nth * NG + x + 1)
                act.activation(onehot[:, b], onehot[:, b], ACT.Relu, bias=ones[:, 0:1], scale=-1.0)\
                   .then_inc(onehot_ready, 1)

            act.wait_ge(tables_ready, 1)

            def mlp_slot(g, b):
                act.wait_ge(pre_ready, g + 1)
                if not early(g, 2):
                    act.wait_ge(elu_ready, g - 1)
                act.activation(neg_part[:, b], pre[:, b], ACT.Relu, scale=-1.0).then_inc(parts_ready, 1)
                if not early(g, 2):
                    act.wait_ge(summed, g - 1)
                act.activation(pos_part[:, b, :, 0:256], pre[:, b], ACT.Relu).then_inc(parts_ready, 1)
                act.wait_ge(parts_ready, 3 * g + 2)
                act.activation(neg_part[:, b], neg_part[:, b], ACT.Exp, scale=-1.0).then_inc(parts_ready, 1)
            slots(act, mlp_slot, 0)

            for m in range(2):
                for u, tiles in enumerate(packs(4)):
                    act.activation(big[:, 3 + m, tiles[0] * P:(tiles[-1] + 1) * P],
                                   filled("mT", 7 * m + u)[:, 0:len(tiles) * P], ACT.Copy)\
                       .then_inc(read_by["act"], 1)
            for u, tiles in enumerate(packs(4)):
                act.activation(flags[:, tiles[0] * P:(tiles[-1] + 1) * P],
                               filled("flag", u)[0:1, 0:len(tiles) * P], ACT.Copy).then_inc(read_by["act"], 1)
            low_bias = small[:, 0, 0:2]
            link(act.mul(low_bias, weight("b2a", 0), -1.0))

            def low_exp(u):
                act.wait_ge(hid0_parts, 2 * u + 1)
                act.activation(neg_node(u % 4), neg_node(u % 4), ACT.Exp, scale=-1.0).then_inc(hid0_parts, 1)

            for c in range(NCOL):
                for m in range(2):
                    u = 2 * c + m
                    bank = filled("hid0", u)
                    if u >= 4:
                        act.wait_ge(hid0_ready, u - 3)
                    act.activation(neg_node(u % 4), bank[:, 0:COLS], ACT.Relu, bias=low_bias[:, m:m + 1],
                                   scale=-1.0).then_inc(hid0_parts, 1)
                    act.activation(pos_node(u % 4), bank[:, 0:COLS], ACT.Relu, bias=weight("b2a", 0)[:, m:m + 1])\
                       .then_inc(read_by["act"], 1)
                    low_exp(u)

            def norm(n):
                act.wait_ge(centered, n)
                act.activation(spare, y_sb[:, :, :].rearrange("p t f -> p (t f)"), ACT.Square).then_inc(squared, 1)
                act.wait_ge(var_ready, n)
                act.activation(stat[:, 1, :], stat[:, 2, :], ACT.Sqrt).then_inc(rooted, 1)

            copy_turned("invT", inv_T)
            norm(1)
            copy_turned("x1T", xT)
            copy_rows("h1", 3, D + 2 * HEADS, h_sb)
            act.wait_ge(read_by["act"], fills_read(FIRST_FILL["gT"], "act"))
            act.sem_inc(table_ready["gat1"], 1)

            def softmax_pass(k):
                n, heads = SOFTMAX[k]
                at = n * NG
                extra = 2 * heads if heads else D

                def make_logits(x, b):
                    act.wait_ge(leak_ready, at + x + 1)
                    if not early(x, 2):
                        act.wait_ge(logit_turned, at + x - 1)
                    terms = leaks[:, b, 1, 0:G * heads].rearrange("p (g h) -> p g h", g=G).unsqueeze(2)\
                        .to_broadcast([P, G, D // heads, heads])
                    act.activation(logit[:, b, :].rearrange("p (g f h) -> p g f h", g=G, h=heads), terms, ACT.Copy)\
                       .then_inc(logit_ready, 1)

                def copy_turned_sums(x, b):
                    act.wait_ge(turn_done, at + x + 1)
                    if not early(x, 2):
                        act.wait_ge(summed, base[k] + x - 1)
                    act.activation(turned[:, b, :, 0:D], ps[:, 4, :].rearrange("p (g f) -> p g f", g=G), ACT.Copy)
                    at_5 = b * G * extra if heads else 0
                    act.activation(turned[:, b, :, D:D + extra],
                                   ps[:, 5, at_5:at_5 + G * extra].rearrange("p (g f) -> p g f", g=G), ACT.Copy)\
                       .then_inc(turned_ready, 1)

                def exponentials(x, b):
                    act.wait_ge(rise_ready, at + x + 1)
                    if not early(x, 2):
                        act.wait_ge(run_ready, at + x - 1)
                    act.activation(gaps[:, b, 0, :], rise[:, b, :], ACT.Relu).then_inc(gaps_split, 1)
                    act.activation(gaps[:, b, 1, :], rise[:, b, :], ACT.Relu, scale=-1.0).then_inc(gaps_split, 1)
                    act.wait_ge(gaps_split, 2 * (at + x + 1))
                    act.activation(gaps[:, b], gaps[:, b], ACT.Exp, scale=-1.0).then_inc(exp_ready, 1)

                def slot(s, b):
                    if has(s, 3):
                        square_distances(k, s - 3, 1 - b, last_rel)
                    if has(s, 4):
                        copy_turned_sums(s - 4, b)
                    if has(s, 1) and heads:
                        make_logits(s - 1, 1 - b)
                    if has(s, 3):
                        mark_edges(n, s - 3, 1 - b)
                    if has(s, 2):
                        exponentials(s - 2, b)
                slots(act, slot, 4, head=6)
                if heads:
                    act.wait_ge(gaps_in, n + 1)
                    m = NT * heads
                    act.activation(small[:, 3:5, 0:m], small[:, 3:5, 0:m], ACT.Exp).then_inc(gaps_out, 1)

            softmax_pass("gat1")
            act.wait_ge(g_ready, 1)
            y_flat = y_sb[:, :, :].rearrange("p t f -> p (t f)")
            link(act.activation(spare, y_flat, ACT.Relu, scale=-1.0))
            act.activation(spare, spare, ACT.Exp, scale=-1.0).then_inc(g_low, 1)
            copy_turned("gT", big[:, 3, :])
            copy_rows("h2", 3, D + 2, h_sb)
            act.wait_ge(read_by["act"], fills_read(FIRST_FILL["x2T"], "act"))
            act.sem_inc(table_ready["gat2"], 1)
            softmax_pass("gat2")
            norm(2)
            copy_turned("x2T", xT)

            def relu_columns(name, bias, to):
                for c in range(NCOL):
                    for m in range(2):
                        bank = filled(name, 2 * c + m)
                        act.activation(big[:, to + m, c * COLS:(c + 1) * COLS], bank[:, 0:COLS], ACT.Relu,
                                       bias=weight(bias, 0)[:, m:m + 1]).then_inc(read_by["act"], 1)

            relu_columns("sh0", "sb0", 3)
            copy_rows("p1", 2, 256, low)
            act.wait_ge(read_by["act"], fills_read(FIRST_FILL["sh1"], "act"))
            act.sem_inc(table_ready["sage1"], 1)
            relu_columns("sh1", "sb1", 0)
            copy_rows("p2", 4, D, h_sb)
            act.wait_ge(read_by["act"], fills_read(FIRST_FILL["out2"], "act"))
            act.sem_inc(table_ready["sage2"], 1)
            norm(3)
            softmax_pass("pool")
            copy_turned("aT", xT)
            copy_rows("mo", 4, D, y_sb, ACT.Relu)
            norm(4)

        @block.vector
        def _(dve):
            links = [0]

            def link(ins):
                links[0] += 1
                ins.then_inc(dve_link, 1)
                dve.wait_ge(dve_link, links[0])

            link(dve.memset(ones[:, :], 1.0))
            dve.wait_ge(iotas_ready, 2)
            dve.tensor_copy(iota[:, :], iota_i[:, :])
            link(dve.tensor_copy(part[:, :], part_i[:, :]))
            link(dve.tensor_scalar(ident[:, :], iota[:, 0:P], part[:, 0:1], None, ALU.is_equal))
            dve.wait_ge(edges_loaded, 16)
            dve.tensor_copy(edges_f[0:CH].rearrange("p k c e -> p (k c e)"), edges_in[0:CH, :])
            link(dve.tensor_scalar(ends[:, :], iota[:, 0:NT], float(P), float(P), ALU.mult, ALU.add))
            for c in range(NCH):
                dve.tensor_scalar(chunk_part[:, c:c + 1], part[:, :], float(c * CH), None, ALU.add)
                ins = dve.tensor_scalar(below[0:CH, c, :], ends[0:CH, :], edges_f[0:CH, 1, c, P - 1:P], None, ALU.is_gt)
            ins.then_inc(below_ready, 1)
            dve.wait_ge(keys_summed, 1)
            link(dve.tensor_tensor(key[0:NT - 1, :], ps[0:NT - 1, 0, 0:1], part[0:NT - 1, :], ALU.add))
            dve.tensor_scalar(moved[0:NT - 1, :], iota[0:NT - 1, :], key[0:NT - 1, 0:1], None, ALU.is_gt)\
               .then_inc(moved_ready, 1)
            dve.wait_ge(tiles_spread, 1)
            dve.tensor_copy(tile_i[:, :], ps[0:1, 1, 0:S])
            dve.tensor_scalar(tile_f[:, :], ps[:, 1, 0:S], float(P), None, ALU.mult)
            link(dve.tensor_tensor(block_f[:, :], iota[:, :], ps[:, 1, 0:S], ALU.subtract))
            dve.tensor_copy(block_i[:, :], block_f[0:1, :])
            for c in range(NCH):
                ins = dve.tensor_scalar(sel[0:CH, c, :], block_f[0:CH, :], chunk_part[0:CH, c:c + 1], None, ALU.is_equal)
            ins.then_inc(sel_ready, 1)
            dve.wait_ge(cols_moved, 3)
            link(dve.memset(src_idx[:, :], 0))
            dve.tensor_copy(src_idx[:, 0:S], ps[:, 2, 0:S])
            dve.tensor_tensor(dst_rel[:, :], ps[:, 3, 0:S], tile_f[:, :], ALU.subtract)
            link(dve.tensor_copy(moved_last, ps[:, 4, 0:S]))
            link(dve.tensor_tensor(last_f[:, :], ps[:, 3, 0:S], moved_last, ALU.not_equal))
            link(dve.scalar_tensor_tensor(last_rel[:, :], dst_rel[:, :], 1.0, last_f[:, :], ALU.add, ALU.mult))
            link(dve.tensor_scalar(last_rel[:, :], last_rel[:, :], -1.0, None, ALU.add))
            dve.drain().then_inc(tables_ready, 1)
            for q in range(4):
                dve.wait_ge(rows_moved, q + 1)
                bank = ps[0:BCH, 5 + q % 2, :]
                link(dve.tensor_scalar(tile_col[0:BCH, q:q + 1], bank[:, 2 * P:2 * P + 1], float(P), None, ALU.mult))
                link(dve.tensor_copy(row_f[0:BCH, q, 0, :], bank[:, P:2 * P]))
                link(dve.tensor_tensor(row_f[0:BCH, q, 0, :], bank[:, 0:P], row_f[0:BCH, q, 0, :], ALU.not_equal))
                dve.tensor_scalar(row_b[0:BCH, q, 0, :], row_f[0:BCH, q, 0, :], NEG, None, ALU.mult)
                ins = dve.tensor_scalar(row_b[0:BCH, q, 1, :], bank[:, 0:P], tile_col[0:BCH, q:q + 1], None,
                                        ALU.subtract)
                ins.then_inc(rows_ready_parts, 1)
            dve.wait_ge(rows_ready_parts, 4)
            dve.drain().then_inc(rows_ready, 1)

            def filled(name, u):
                n = FIRST_FILL[name] + u
                dve.wait_ge(fill_done, n + 1)
                return ps[:, n % RING, :]

            dve.wait_ge(weights_loaded, 48)
            link(dve.tensor_reduce(head_mask[:, :], ident[:, :].rearrange("p (c h) -> p h c", h=HEADS), AX_X, ALU.add))
            for i in range(2):
                dve.tensor_scalar(att_block[:, i * HEADS:(i + 1) * HEADS], head_mask[:, :],
                                  weight("att1", 0, i, 1), None, ALU.mult).then_inc(terms_built, 1)
            dve.wait_ge(terms_built, 2)
            dve.sem_inc(att_built, 1)
            for m in range(2):
                dve.tensor_copy(Wc[:, m, :], filled("Wc", m)[:, 0:256]).then_inc(read_by["dve"], 1)
            dve.tensor_copy(bc[:, :], filled("Wc", 2)[0:1, 0:256]).then_inc(read_by["dve"], 1)
            dve.tensor_copy(gcat["gat1"][:, D:D + 2 * HEADS], filled("att", 0)[:, 0:2 * HEADS])\
               .then_inc(read_by["dve"], 1)
            dve.tensor_copy(gcat["gat2"][:, D:D + 2], filled("att", 1)[:, 0:2]).then_inc(read_by["dve"], 1)
            dve.tensor_copy(gcat["gat1"][:, 0:D], weight("gW1", 0))
            link(dve.tensor_copy(gcat["gat2"][:, 0:D], weight("gW2", 0)))

            def zero(k, what):
                dve.memset(what, 0.0).then_inc(acc_zeroed, 1)
                dve.wait_ge(acc_zeroed, PASSES.index(k) + 1)

            def make_onehot(k, g, b, values):
                dve.tensor_tensor(onehot[:, b], iota[:, 0:P].unsqueeze(1).to_broadcast([P, G, P]),
                                  values[:, bass.ds(g * G, G)].unsqueeze(2).to_broadcast([P, G, P]),
                                  ALU.is_equal).then_inc(onehot_ready, 1)

            def adding(k, g, tiles, bank_of, acc):
                def add(j):
                    to = acc(tiles[j])
                    done = G * (base[k] + g) + j
                    if not (isinstance(done, int) and done == 0):
                        dve.wait_ge(accumulated, done)
                    dve.tensor_tensor(to, to, bank_of(j), ALU.add).then_inc(accumulated, 1)
                return add

            def accumulate(k, g, tiles, bank_of, acc):
                add = adding(k, g, tiles, bank_of, acc)
                for j in range(G):
                    add(j)

            dve.wait_ge(rows_stored, 128)
            mean = sum_rows("mlp")
            zero("mlp", mean)
            dve.wait_ge(table_written, 16)
            link(dve.memset(pos_part[:, :, :, 256:257], 1.0))

            def mlp_slot(g, b, tiles=None):
                if has(g, 3):
                    dve.wait_ge(summed, g - 2)
                    add = adding("mlp", g - 3, tiles, lambda j: ps[:, 4 + j, 0:SUMS["mlp"]].unsqueeze(1),
                                 lambda t: mean[:, bass.ds(t, 1), :])
                for j in range(G):
                    if has(g, 3):
                        add(j)
                    if has(g):
                        if j == 0:
                            dve.wait_ge(edge_product, g + 1)
                            dve.wait_ge(gathered[b], 16 * G * (half(g, b) + 1))
                            if not early(g, 2):
                                dve.wait_ge(parts_ready, 3 * (g - 1))
                        ins = dve.tensor_tensor(pre[:, b, j, :], ps[:, 2 * b + j // 2, (j % 2) * 256:(j % 2) * 256 + 256],
                                                rows[:, b, j, :], ALU.add)
                if has(g):
                    ins.then_inc(pre_ready, 1)
                if has(g, 1):
                    q = 1 - b
                    if not early(g, 3):
                        dve.wait_ge(summed, g - 2)
                    make_onehot("mlp", g - 1, q, dst_rel)
                    dve.wait_ge(parts_ready, 3 * g)
                    dve.scalar_tensor_tensor(pos_part[:, q, :, 0:256], neg_part[:, q], -1.0,
                                             pos_part[:, q, :, 0:256], ALU.add, ALU.add)\
                       .then_inc(elu_ready, 1)
            slots(dve, mlp_slot, 3, head=4, tiles_of=(mybir.EngineType.DVE, 3))
            dve.wait_ge(accumulated, G * NG)
            link(dve.tensor_scalar(inv_row[:, :].unsqueeze(2), mean[:, :, 2 * P:2 * P + 1], 1.0, None, ALU.max))
            link(dve.reciprocal(inv_row[:, :], inv_row[:, :]))
            link(dve.tensor_tensor(mean, mean, inv_row[:, :].unsqueeze(2).to_broadcast([P, NT, SUMS["mlp"]]),
                                   ALU.mult))
            dve.sem_inc(mean_ready, 1)
            for c in range(NCOL):
                for m in range(2):
                    u = 2 * c + m
                    dve.wait_ge(hid0_parts, 2 * (u + 1))
                    dve.wait_ge(read_by["act"], fills_read(FIRST_FILL["hid0"] + u + 1, "act"))
                    dve.scalar_tensor_tensor(big[:, m, c * COLS:(c + 1) * COLS], neg_node(u % 4), -1.0,
                                             pos_node(u % 4),
                                             ALU.add, ALU.add).then_inc(hid0_ready, 1)
            for u, tiles in enumerate(packs(4)):
                at = slice(tiles[0], tiles[-1] + 1)
                dve.tensor_tensor(y_sb[:, at, :], filled("out0", u)[:, 0:len(tiles) * D]
                                  .rearrange("p (t f) -> p t f", f=D), x_sb[:, at, :], ALU.add)\
                   .then_inc(read_by["dve"], 1)
            dve.wait_ge(read_by["dve"], fills_read(FIRST_FILL["invT"], "dve"))

            def per_node(a):
                return a.unsqueeze(2).to_broadcast([P, NT, D])

            def norm(n):
                link(dve.tensor_reduce(stat[:, 0, :], y_sb[:, :, :], AX_X, ALU.add))
                link(dve.tensor_scalar(stat[:, 0, :], stat[:, 0, :], 1.0 / D, None, ALU.mult))
                dve.tensor_tensor(y_sb[:, :, :], y_sb[:, :, :], per_node(stat[:, 0, :]), ALU.subtract)\
                   .then_inc(centered, 1)
                dve.wait_ge(squared, n)
                link(dve.tensor_reduce(stat[:, 2, :], spare.rearrange("p (t f) -> p t f", t=NT), AX_X, ALU.add))
                dve.tensor_scalar(stat[:, 2, :], stat[:, 2, :], 1.0 / D, EPS, ALU.mult, ALU.add).then_inc(var_ready, 1)
                dve.wait_ge(rooted, n)
                link(dve.reciprocal(stat[:, 0, :], stat[:, 1, :]))
                dve.tensor_tensor(x_sb[:, :, :], y_sb[:, :, :], per_node(stat[:, 0, :]), ALU.mult).then_inc(x_ready, 1)
                dve.wait_ge(x_ready, n)

            norm(1)

            def split_terms(k):
                n, heads = SOFTMAX[k]
                left = small[:, 0, 0:NT * heads].rearrange("p (t h) -> p t h", t=NT)
                part3 = small[:, 1, 0:NT * heads].rearrange("p (t h) -> p t h", t=NT)
                link(dve.tensor_copy(left, h_sb[:, :, D + heads:D + 2 * heads]))
                for i in range(3):
                    link(dve.tensor_copy(adst[:, :, i * heads:(i + 1) * heads], left))
                    if i < 2:
                        link(dve.tensor_copy(part3, adst[:, :, i * heads:(i + 1) * heads]))
                        link(dve.tensor_tensor(left, left, part3, ALU.subtract))
                dve.sem_inc(adst_ready, 1)

            def softmax_pass(k):
                n, heads = SOFTMAX[k]
                at, all_at, width = n * NG, base[k], SUMS[k]
                acc = sum_rows(k)
                zero(k, acc)
                dve.memset(max_run[:, :, 0:1], 0.0)
                dve.memset(s_run[:, 1, G * P - 1:G * P], 0.0)
                link(dve.memset(w_run[:, 1, G * P - 1:G * P], 0.0))
                loads_at = n * NG // 2

                def mark_nodes(x, b):
                    dve.wait_ge(rel_loaded[b], 16 * (loads_at + half(x, b) + 1))
                    if not early(x, 2):
                        dve.wait_ge(term_done, at + x - 1)
                    dve.tensor_scalar(rel_T[:, b, :], rel_b[:, b, :], part[:, 0:1], None, ALU.is_equal)\
                       .then_inc(rel_ready, 1)

                def weigh(x, b):
                    dve.wait_ge(exp_ready, at + x + 1)
                    if not early(x, 2):
                        dve.wait_ge(run_ready, at + x - 1)
                    value = ps[:, 2 + b, :] if heads else ps[:, b, :]
                    dve.tensor_tensor(hp[:, b, :], value, gaps[:, b, 1, :], ALU.mult).then_inc(hp_ready, 1)

                def run_weights(x, b):
                    if not early(x, 2):
                        dve.wait_ge(turn_done, at + x - 1)
                    dve.tensor_tensor_scan(s_run[:, b, :], gaps[:, b, 0, :], gaps[:, b, 1, :],
                                           s_run[:, 1 - b, G * P - 1:G * P], ALU.mult, ALU.add)

                def run_products(x, b):
                    dve.wait_ge(hp_ready, at + x + 1)
                    dve.tensor_tensor_scan(w_run[:, b, :], gaps[:, b, 0, :], hp[:, b, :], w_run[:, 1 - b, G * P - 1:G * P],
                                           ALU.mult, ALU.add).then_inc(run_ready, 1)

                def spread_value(b):
                    return ps[:, b, :]

                def run_max(x, b):
                    dve.wait_ge(neg_loaded[b], 16 * (loads_at + half(x, b) + 1))
                    if heads:
                        dve.wait_ge(logit_turned, at + x + 1)
                        if not early(x, 2):
                            dve.wait_ge(heads_turned, at + x - 1)
                    else:
                        dve.wait_ge(taken, at + x + 1)
                    if not early(x, 1):
                        dve.wait_ge(carry_ready, at + x)
                    dve.tensor_tensor_scan(max_run[:, b, 1:G * P + 1], neg_b[:, b, :], spread_value(b),
                                           max_run[:, b, 0:1], ALU.add, ALU.max).then_inc(max_ready, 1)

                def old_max(x, b):
                    dve.wait_ge(max_ready, at + x + 1)
                    if not early(x, 2):
                        dve.wait_ge(exp_ready, at + x - 1)
                    dve.tensor_tensor(rise[:, b, :], max_run[:, b, 0:G * P], neg_b[:, b, :], ALU.add)\
                       .then_inc(old_max_ready, 1)
                    dve.tensor_copy(max_run[:, 1 - b, 0:1], max_run[:, b, G * P:G * P + 1]).then_inc(carry_ready, 1)

                def rise_above(x, b):
                    dve.wait_ge(old_max_ready, at + x + 1)
                    dve.tensor_tensor(rise[:, b, :], spread_value(b), rise[:, b, :], ALU.subtract)\
                       .then_inc(rise_ready, 1)

                def of_edges(b, i):
                    return leaks[:, b, i, 0:G * heads].rearrange("p (g h) -> p g h", g=G)

                def join_parts(x, b):
                    dve.wait_ge(term_done, at + x + 1)
                    parts = ps[:, 5, TERMS[b]:TERMS[b] + G * 3 * heads].rearrange("p (g k h) -> p g h k", g=G, k=3)
                    dve.tensor_reduce(of_edges(b, 2), parts, AX_X, ALU.add).then_inc(dst_terms_ready, 1)

                def add_edge_terms(x, b):
                    dve.wait_ge(gathered[b], 16 * G * (all_at // 2 + half(x, b) + 1))
                    dve.wait_ge(dst_terms_ready, at + x + 1)
                    dve.tensor_tensor(of_edges(b, 0), of_edges(b, 2), rows[:, b, :, D:D + heads], ALU.add)\
                       .then_inc(terms_ready, 1)

                def leak(x, b):
                    dve.wait_ge(terms_ready, at + x + 1)
                    if not early(x, 2):
                        dve.wait_ge(logit_ready, at + x - 1)
                    dve.scalar_tensor_tensor(of_edges(b, 1), of_edges(b, 0), 0.2, of_edges(b, 0), ALU.mult, ALU.max)\
                       .then_inc(leak_ready, 1)

                def slot(s, b, tiles=None):
                    def add(j):
                        pass
                    if has(s, 5):
                        add = adding(k, s - 5, tiles, lambda j: ps[:, 6 + j // 2, (j % 2) * 256:(j % 2) * 256 + width]
                                     .unsqueeze(1), lambda t: acc[:, bass.ds(t, 1), :])
                    if has(s, 1) and heads:
                        join_parts(s - 1, 1 - b)
                    if has(s, 2):
                        run_max(s - 2, b)
                    if has(s, 1) and heads:
                        add_edge_terms(s - 1, 1 - b)
                    if has(s, 5):
                        dve.wait_ge(summed, all_at + s - 4)
                    add(0)
                    if has(s, 3):
                        weigh(s - 3, 1 - b)
                    if has(s, 1) and heads:
                        leak(s - 1, 1 - b)
                    add(1)
                    if has(s, 2):
                        old_max(s - 2, b)
                    if has(s) and heads:
                        mark_nodes(s, b)
                    if has(s, 2):
                        rise_above(s - 2, b)
                    add(2)
                    if has(s, 3):
                        run_weights(s - 3, 1 - b)
                    add(3)
                    if has(s, 3):
                        run_products(s - 3, 1 - b)
                slots(dve, slot, 5, head=6, tiles_of=(mybir.EngineType.DVE, 5))
                dve.wait_ge(accumulated, G * (all_at + NG))
                return acc

            def attention_output(k, acc, bias):
                n, heads = SOFTMAX[k]
                m = NT * heads

                def sm(i):
                    return small[:, i, 0:m].rearrange("p (t h) -> p t h", t=NT)

                def over(a):
                    return a.unsqueeze(2).to_broadcast([P, NT, D // heads, heads])

                def heads_of(a):
                    return a.rearrange("p t (f h) -> p t f h", h=heads)

                total, top = acc[:, :, D:D + heads], acc[:, :, D + heads:D + 2 * heads]
                link(dve.tensor_tensor(sm(0), h_sb[:, :, D:D + heads], h_sb[:, :, D + heads:D + 2 * heads], ALU.add))
                link(dve.scalar_tensor_tensor(sm(1), sm(0), 0.2, sm(0), ALU.mult, ALU.max))
                link(dve.tensor_scalar(sm(0), total, 0.5, None, ALU.is_gt))
                link(dve.tensor_scalar(sm(0), sm(0), -1.0, -NEG, ALU.add, ALU.mult))
                link(dve.tensor_tensor(sm(0), sm(0), top, ALU.add))
                link(dve.tensor_tensor(sm(2), sm(0), sm(1), ALU.max))
                dve.tensor_tensor(sm(3), sm(0), sm(2), ALU.subtract)
                link(dve.tensor_tensor(sm(4), sm(1), sm(2), ALU.subtract))
                dve.drain().then_inc(gaps_in, 1)
                dve.wait_ge(gaps_out, n + 1)
                link(dve.tensor_tensor(sm(0), total, sm(3), ALU.mult))
                link(dve.tensor_tensor(sm(0), sm(0), sm(4), ALU.add))
                link(dve.tensor_scalar(sm(0), sm(0), 1e-16, None, ALU.add))
                link(dve.reciprocal(sm(0), sm(0)))
                dve.tensor_tensor(sm(3), sm(3), sm(0), ALU.mult)
                link(dve.tensor_tensor(sm(4), sm(4), sm(0), ALU.mult))
                dve.tensor_tensor(heads_of(y_sb[:, :, :]), heads_of(acc[:, :, 0:D]), over(sm(3)), ALU.mult)
                loop = spare.rearrange("p (t f) -> p t f", t=NT)
                link(dve.tensor_tensor(heads_of(loop), heads_of(h_sb[:, :, 0:D]), over(sm(4)), ALU.mult))
                link(dve.tensor_tensor(y_sb[:, :, :], y_sb[:, :, :], loop, ALU.add))
                link(dve.tensor_tensor(y_sb[:, :, :], y_sb[:, :, :], over_tiles(spread(bias)), ALU.add))

            dve.wait_ge(read_by["act"], fills_read(FIRST_FILL["gT"], "act"))
            split_terms("gat1")
            attention_output("gat1", softmax_pass("gat1"), "gb1")
            dve.sem_inc(g_ready, 1)
            dve.wait_ge(g_low, 1)
            link(dve.tensor_scalar(y_sb[:, :, :], y_sb[:, :, :], 0.0, None, ALU.max))
            dve.scalar_tensor_tensor(y_sb[:, :, :], spare.rearrange("p (t f) -> p t f", t=NT), -1.0, y_sb[:, :, :],
                                     ALU.add, ALU.add).then_inc(g1_ready, 1)
            dve.wait_ge(read_by["act"], fills_read(FIRST_FILL["x2T"], "act"))
            split_terms("gat2")
            attention_output("gat2", softmax_pass("gat2"), "gb2")
            link(dve.tensor_tensor(y_sb[:, :, :], y_sb[:, :, :], x_sb[:, :, :], ALU.add))
            norm(2)
            dve.sem_inc(table_ready["sage0"], 1)

            def sum_pass(k, by_row):
                all_at = base[k]
                chunks = ROW[k] // P
                rows_acc = sum_rows(k) if by_row else None
                zero(k, rows_acc if by_row else big[:, 0:chunks, :])

                def slot(g, b, tiles=None):
                    if has(g):
                        if not early(g, 2):
                            dve.wait_ge(summed, all_at + g - 1)
                        make_onehot(k, g, b, dst_rel)
                    if has(g, 1):
                        q = 1 - b
                        dve.wait_ge(summed, all_at + g)
                        if by_row:
                            accumulate(k, g - 1, tiles, lambda j: ps[:, 4 + 2 * q + j // 2, (j % 2) * 256:(j % 2) * 256 + P]
                                       .unsqueeze(1), lambda t: rows_acc[:, bass.ds(t, 1), :])
                        else:
                            accumulate(k, g - 1, tiles, lambda j: ps[:, 4 + 2 * q + j // 2,
                                                              (j % 2) * 256:(j % 2) * 256 + chunks * P]
                                       .rearrange("p (c n) -> p c n", c=chunks),
                                       lambda t: big[:, 0:chunks, bass.ds(t * P, P)])
                slots(dve, slot, 1, tiles_of=(mybir.EngineType.DVE, 1))
                dve.wait_ge(accumulated, G * (all_at + NG))

            sum_pass("sage0", False)
            dve.tensor_tensor(big[:, 0, :], big[:, 0, :], inv_T[:, :], ALU.mult).then_inc(agg_scaled, 1)
            dve.wait_ge(table_written, 16 * 5)
            sum_pass("sage1", False)
            dve.tensor_tensor(big[:, 0, :], big[:, 0, :], inv_T[:, :], ALU.mult)
            link(dve.tensor_tensor(big[:, 1, :], big[:, 1, :], inv_T[:, :], ALU.mult))
            dve.sem_inc(agg_scaled, 1)
            dve.wait_ge(read_by["act"], fills_read(FIRST_FILL["out2"], "act"))
            sum_pass("sage2", True)
            by_node = sum_rows("sage2")
            link(dve.tensor_tensor(by_node, by_node, per_node(inv_row[:, :]), ALU.mult))
            for u, tiles in enumerate(packs(4)):
                at = slice(tiles[0], tiles[-1] + 1)
                dve.tensor_tensor(y_sb[:, at, :], filled("out2", u)[:, 0:len(tiles) * D]
                                  .rearrange("p (t f) -> p t f", f=D), by_node[:, at, :], ALU.add)\
                   .then_inc(read_by["dve"], 1)
            dve.wait_ge(read_by["dve"], fills_read(FIRST_FILL["aT"], "dve"))
            link(dve.scalar_tensor_tensor(y_sb[:, :, :], y_sb[:, :, :], 0.0, x_sb[:, :, :], ALU.max, ALU.add))
            norm(3)
            dve.sem_inc(table_ready["pool"], 1)
            acc = softmax_pass("pool")
            link(dve.tensor_scalar(acc[:, :, D:2 * D], acc[:, :, D:2 * D], 1.0, None, ALU.max))
            link(dve.reciprocal(acc[:, :, D:2 * D], acc[:, :, D:2 * D]))
            dve.tensor_tensor(y_sb[:, :, :], acc[:, :, 0:D], acc[:, :, D:2 * D], ALU.mult).then_inc(agg3_ready, 1)
            dve.wait_ge(read_by["act"], fills_read(len(FILLS), "act"))
            link(dve.tensor_tensor(y_sb[:, :, :], y_sb[:, :, :], over_tiles(spread("scale")), ALU.mult))
            link(dve.scalar_tensor_tensor(y_sb[:, :, :], x_sb[:, :, :], 2.0, y_sb[:, :, :], ALU.mult, ALU.add))
            dve.wait_ge(table_written, 16 * 7)
            norm(4)


def lay_out(inputs):
    import numpy as np

    a = {k: np.asarray(v) for k, v in inputs.items()}
    n = NCH * CH * P
    src = np.zeros(n, np.int32)
    src[:N_EDGES] = a["src"]
    dst = np.full(n + 2, PAD_NODE, np.int32)
    dst[0] = -1
    dst[1:1 + N_EDGES] = a["dst"]
    dst[-1] = -1
    tables = [src, dst[1:-1], dst[:-2], dst[2:]]
    edges_i = np.ascontiguousarray(np.stack(tables).reshape(4, NCH, CH, P).transpose(2, 0, 1, 3)).reshape(CH, -1)
    ea = np.zeros((NB * P, D), np.float32)
    ea[:N_EDGES] = a["edge_attr_128"]
    ea_blocks = np.ascontiguousarray(ea.reshape(NB, P, D).transpose(0, 2, 1))
    x_rows = np.zeros((NODES, D), np.float32)
    x_rows[:N_NODES] = a["x"]

    def head_last(w, axis):
        shape = list(w.shape)
        if w.shape == (HEADS, D // HEADS):
            return w.T
        cut_shape = shape[:axis] + [HEADS, D // HEADS] + shape[axis + 1:]
        return np.swapaxes(w.reshape(cut_shape), axis, axis + 1).reshape(shape)

    gW1, gW2 = head_last(a["L1_gnn_W1"], 1), head_last(a["L1_gnn_W2"], 0)
    weights = {"W1a": a["L0_gnn_W1a"], "W1bT": a["L0_gnn_W1b"].T, "W2a": a["L0_gnn_W2a"], "W2b": a["L0_gnn_W2b"],
               "gW1": gW1, "gW2": gW2, "gW1T": gW1.T, "gW2T": gW2.T, "b1b": a["L0_gnn_b1b"].reshape(2, P).T,
               "att1": np.stack([head_last(a["L1_gnn_att_src1"], 0).reshape(P),
                                 head_last(a["L1_gnn_att_dst1"], 0).reshape(P)], axis=1),
               "att2": np.stack([a["L1_gnn_att_src2"].reshape(P), a["L1_gnn_att_dst2"].reshape(P)], axis=1),
 "Ws0": a["L2_gnn_Ws0"], "Wn0": a["L2_gnn_Wn0"],
               "Ws1": a["L2_gnn_Ws1"], "Wn1": a["L2_gnn_Wn1"], "Ws2": a["L2_gnn_Ws2"], "Wn2": a["L2_gnn_Wn2"],
               "mlpT": a["L3_gnn_mlp_w"].T, "b2a": a["L0_gnn_b2a"].reshape(2, P).T,
               "sb0": a["L2_gnn_b0"].reshape(2, P).T, "sb1": a["L2_gnn_b1"].reshape(2, P).T}
    cols = []
    for name, (c, m) in WEIGHTS.items():
        cols.append(weights[name].reshape(c, P, m).transpose(1, 0, 2).reshape(P, c * m))
    bias = {"b1a": a["L0_gnn_b1a"], "b2b": a["L0_gnn_b2b"], "sb2": a["L2_gnn_b2"],
            "mlp_b": a["L3_gnn_mlp_b"]}
    spread = {"gb1": head_last(a["L1_gnn_b1"], 0), "gb2": a["L1_gnn_b2"], "scale": a["L3_gnn_scale"]}
    return {
        "edges_i": edges_i, "ea_blocks": ea_blocks, "x_rows": x_rows, "xT_in": np.ascontiguousarray(x_rows.T),
        "wpack": np.ascontiguousarray(np.concatenate(cols, axis=1)),
        "bpack": np.concatenate([bias[k].reshape(-1) for k in BIAS_ROWS]).reshape(1, -1),
        "rpack": np.concatenate([spread[k].reshape(-1) for k in SPREAD_ROWS]).reshape(1, -1),
    }


def kernel(**inputs):
    import concourse.bacc as _bacc
    from concourse import mybir as _mybir
    from concourse.bass_utils import run_bass_kernel_spmd as _run

    nc = _bacc.Bacc("TRN2", target_bir_lowering=False, num_devices=1)
    arrays, args = {}, []
    for name, a in lay_out(inputs).items():
        arrays[f"in_{name}"] = a
        args.append(nc.dram_tensor(f"in_{name}", a.shape, _mybir.dt.from_np(a.dtype), kind="ExternalInput").ap())
    args.append(nc.dram_tensor("out_0", (N_NODES, D), F32, kind="ExternalOutput").ap())
    program(nc, *args)
    r = _run(nc, [arrays], core_ids=[0])
    return r.results[0]["out_0"]
```

```python
from contextlib import ExitStack

import concourse.bass as bass
from concourse import mybir

F32 = mybir.dt.float32
BF16 = mybir.dt.bfloat16
I32 = mybir.dt.int32
ALU = mybir.AluOpType
ACT = mybir.ActivationFunctionType
AX_X = mybir.AxisListType.X

P = 128
N_NODES, N_EDGES, D = 3125, 50000, 128
NB = -(-N_EDGES // P)
NT = 26
NODES = NT * P
S = NB + NT - 1
G = 4
PAIRS = 4
UNROLL = 4
NG = S // G
CH = 98
NCH = 4
BCH = S // 4
COLS = 416
NCOL = NODES // COLS
PAD_NODE = NODES - 1
NEG = -1.0e30
EPS = 1e-5
HEADS = 4
assert NG % (2 * PAIRS) == 0 and NG % UNROLL == 0 and UNROLL % 4 == 0 and S % G == 0
assert NCH * CH >= NB and NCOL * COLS == NODES and S <= 512 and NT * P > N_NODES + 1

WEIGHTS = {"W1a": (2, 256), "W1bT": (2, 256), "W2a": (3, 256), "W2b": (2, 128), "gW1": (1, 128), "gW2": (1, 128),
           "gW1T": (1, 128), "gW2T": (1, 128), "att1": (1, 2), "att2": (1, 2), "b1b": (1, 2),
           "Ws0": (1, 256), "Wn0": (1, 256), "Ws1": (2, 256), "Wn1": (2, 256), "Ws2": (2, 128), "Wn2": (2, 128),
           "mlpT": (1, 128), "b2a": (1, 2), "sb0": (1, 2), "sb1": (1, 2)}
BIAS_ROWS = {"sb2": 128, "mlp_b": 128}
SPREAD_ROWS = {"b1a": 256, "b2b": 128, "gb1": 128, "gb2": 128, "scale": 128}


def offsets(sizes):
    at, out = 0, {}
    for name, n in sizes.items():
        out[name] = at
        at += n
    return out, at


W_AT, W_COLS = offsets({k: c * n for k, (c, n) in WEIGHTS.items()})
B_AT, B_COLS = offsets(BIAS_ROWS)
R_AT, R_COLS = offsets(SPREAD_ROWS)

PASSES = ["mlp", "gat1", "gat2", "sage0", "sage1", "sage2", "pool"]
ROW = {"mlp": 256, "gat1": D + HEADS, "gat2": D + 1, "sage0": 128, "sage1": 256, "sage2": 128, "pool": 128}
SUMS = {"mlp": 2 * P + 1, "gat1": D + 2 * HEADS, "gat2": D + 2, "sage0": P, "sage1": 2 * P, "sage2": P, "pool": 2 * D}
SOFTMAX = {"gat1": (0, HEADS), "gat2": (1, 1), "pool": (2, 0)}

STAGES = [("tab0", 13, "dve"), ("Wc", 3, "dve"), ("att", 2, "dve"), ("mT", 14, "act"), ("flag", 7, "act"),
          ("hid0", 16, "act"), ("out0", 7, "dve"), ("x1T", 7, "act"), ("h1", 9, "act"), ("invT", 7, "act"),
          ("gT", 7, "act"), ("h2", 9, "act"), ("x2T", 7, "act"), ("sh0", 16, "act"), ("p1", 13, "act"),
          ("sh1", 16, "act"), ("p2", 7, "act"), ("out2", 7, "dve"), ("last", 14, "act")]
FILLS = [(name, u, who) for name, n, who in STAGES for u in range(n)]
FIRST_FILL = {name: [f[0] for f in FILLS].index(name) for name, _, _ in STAGES}
RING = 4
TABLE_PARTS = 4
NPACK = -(-NT // 4)
TERMS = (384, 448)



def fills_read(upto, who):
    return sum(f[2] == who for f in FILLS[:upto])


def packs(per):
    return [list(range(a, min(a + per, NT))) for a in range(0, NT, per)]


def program(nc, edges_i, ea_blocks, x_rows, xT_in, wpack, bpack, rpack, out):
    with ExitStack() as ctx:
        def sb(name, shape, dt=F32):
            return ctx.enter_context(nc.sbuf_tensor(name, shape, dt))

        def sem(name):
            return ctx.enter_context(nc.semaphore(name))

        table = {k: nc.dram_tensor(f"table_{k}", (NODES, ROW[k]), F32, kind="Internal").ap() for k in PASSES}
        neg_rows = nc.dram_tensor("neg_rows", (S, P), BF16, kind="Internal").ap()
        rel_rows = nc.dram_tensor("rel_rows", (S, P), BF16, kind="Internal").ap()

        ps = ctx.enter_context(nc.psum_tensor("ps", [P, 8, 512], F32))
        big = sb("big", [P, 5, NODES])
        x_sb = sb("x_sb", [P, NT, D])
        xT = sb("xT", [P, NODES])
        h_sb = sb("h_sb", [P, NT, D + 2 * HEADS])
        inv_T = sb("inv_T", [P, NODES])
        y_sb = sb("y_sb", [P, NT, D])
        w_sb = sb("w_sb", [P, W_COLS])
        b_sb = sb("b_sb", [1, B_COLS])
        r_sb = sb("r_sb", [P, R_COLS])
        ident = sb("ident", [P, P])
        ones = sb("ones", [P, P])
        iota_i = sb("iota_i", [P, S], I32)
        iota = sb("iota", [P, S])
        part_i = sb("part_i", [P, 1], I32)
        part = sb("part", [P, 1])
        src_idx = sb("src_idx", [P, S + 2 * G], I32)
        dst_rel = sb("dst_rel", [P, S])
        last_rel = sb("last_rel", [P, S])
        tile_i = sb("tile_i", [1, S], I32)
        block_i = sb("block_i", [1, S], I32)
        adst = sb("adst", [P, NT, 3 * HEADS], BF16)
        Wc = sb("Wc", [P, 2, 256])
        bc = sb("bc", [1, 256])
        gcat = {"gat1": sb("gcat1", [P, D + 2 * HEADS]), "gat2": sb("gcat2", [P, D + 2])}
        att_block = sb("att_block", [P, 2 * HEADS])
        head_mask = sb("head_mask", [P, HEADS])
        small = sb("small", [P, 8, NT * HEADS])
        stat = sb("stat", [P, 3, NT])
        inv_row = sb("inv_row", [P, NT])
        leaks = sb("leaks", [P, 2, 3, G * HEADS])
        idx_stage = sb("idx_stage", [P, PAIRS, 2 * G], I32)
        rows = sb("rows", [P, 2, G, 256])
        onehot = sb("onehot", [P, 2, G, P])
        ea_sb = sb("ea_sb", [P, 2, G, P])
        s_run = sb("s_run", [P, 2, G * P])
        w_run = sb("w_run", [P, 2, G * P])

        flat = big[:, :, :].rearrange("p a n -> p (a n)")

        def part_of_big(at, n):
            return flat[:, at:at + n]

        lo = 3 * NODES
        pre = part_of_big(lo, 2048).rearrange("p (b g f) -> p b g f", b=2, g=G)
        neg_part = part_of_big(lo + 2048, 2048).rearrange("p (b g f) -> p b g f", b=2, g=G)
        pos_part = part_of_big(lo + 4096, 2 * G * 257).rearrange("p (b g f) -> p b g f", b=2, g=G)
        rel_T = part_of_big(lo, 512).bitcast(BF16).rearrange("p (b n) -> p b n", b=2)
        logit = part_of_big(lo + 512, 1024).rearrange("p (b n) -> p b n", b=2)
        max_run = part_of_big(lo + 1536, 1028).rearrange("p (b n) -> p b n", b=2)
        gaps = part_of_big(lo + 2568, 2048).rearrange("p (b k n) -> p b k n", b=2, k=2)
        rise = part_of_big(lo + 4616, 1024).rearrange("p (b n) -> p b n", b=2)
        neg_b = part_of_big(lo + 5640, 512).bitcast(BF16).rearrange("p (b n) -> p b n", b=2)
        assert 5640 + 512 <= 2 * NODES and 4096 + 2 * G * 257 <= 2 * NODES
        rel_b = ea_sb[:, :, :, :].rearrange("p b g e -> p (b g e)")[:, 0:512].bitcast(BF16)\
            .rearrange("p (b n) -> p b n", b=2)

        edges_in = part_of_big(0, 2048).bitcast(I32)
        edges_f = part_of_big(2048, 2048).rearrange("p (k c e) -> p k c e", k=4, c=NCH)
        sel = part_of_big(4096, NCH * S).rearrange("p (c s) -> p c s", c=NCH)
        moved = part_of_big(5760, S)
        tile_f = part_of_big(6176, S)
        block_f = part_of_big(6592, S)
        ends = part_of_big(7008, NT)
        below = part_of_big(7040, NCH * NT).rearrange("p (c t) -> p c t", c=NCH)
        chunk_part = part_of_big(7150, NCH)
        key = part_of_big(7155, 1)
        last_f = part_of_big(7160, S)
        tile_col = part_of_big(7580, 4)
        row_f = part_of_big(7600, 4 * 2 * P).rearrange("p (q k e) -> p q k e", q=4, k=2)
        moved_last = part_of_big(9160, S)
        row_b = part_of_big(8640, 4 * 2 * P // 2).bitcast(BF16).rearrange("p (q k e) -> p q k e", q=4, k=2)

        sum_T = big[:, 0:3, :]

        def sum_rows(k):
            at = lo if k == "sage2" else 0
            return part_of_big(at, NT * SUMS[k]).rearrange("p (t f) -> p t f", t=NT)

        spare = big[:, 2, :]
        big_rows = big[:, 3:5, :].rearrange("p a n -> p (a n)").rearrange("p (t f) -> p t f", t=NT)
        y_flat = y_sb[:, :, :].rearrange("p t f -> p (t f)")
        turned = y_flat[:, 0:2048].rearrange("p (b g f) -> p b g f", b=2, g=G)
        hp = y_flat[:, 2048:3072].rearrange("p (b n) -> p b n", b=2)
        hidden = h_sb[:, :, :].rearrange("p t f -> p (t f)")[:, 0:8 * COLS].rearrange("p (k u n) -> p k u n", k=2, u=4)
        flags = y_sb[0:1, :, :].rearrange("p t f -> p (t f)")

        def neg_node(m):
            return hidden[:, 0, m, :]

        def pos_node(m):
            return hidden[:, 1, m, :]

        def weight(name, c, m0=0, m=None):
            n = WEIGHTS[name][1]
            at = W_AT[name] + c * n + m0
            return w_sb[:, at:at + (n - m0 if m is None else m)]

        def bias_row(name, m0=0, m=None):
            at = B_AT[name] + m0
            return b_sb[0:1, at:at + (BIAS_ROWS[name] - m0 if m is None else m)]

        def spread(name):
            return r_sb[:, R_AT[name]:R_AT[name] + SPREAD_ROWS[name]]

        def pick(t):
            return slice(t * P, (t + 1) * P)

        def pack_columns(u):
            tiles = packs(4)[u]
            return slice(tiles[0] * D, (tiles[-1] + 1) * D)

        edges_loaded, weights_loaded, x_loaded = sem("edges_loaded"), sem("weights_loaded"), sem("x_loaded")
        x_rows_loaded, src_ready, bias_added = sem("x_rows_loaded"), sem("src_ready"), sem("bias_added")
        iotas_ready = sem("iotas_ready")
        below_ready, keys_summed, moved_ready, tiles_spread = (
            sem("below_ready"), sem("keys_summed"), sem("moved_ready"), sem("tiles_spread"))
        rows_ready_parts = sem("rows_ready_parts")
        terms_ready, leak_ready = sem("terms_ready"), sem("leak_ready")
        hp_ready, carry_ready, old_max_ready = sem("hp_ready"), sem("carry_ready"), sem("old_max_ready")
        sel_ready, cols_moved, rows_moved, tables_ready, rows_ready, rows_stored = (
            sem("sel_ready"), sem("cols_moved"), sem("rows_moved"), sem("tables_ready"), sem("rows_ready"),
            sem("rows_stored"))
        dve_link, act_link = sem("dve_link"), sem("act_link")
        fill_done, read_by = sem("fill_done"), {"act": sem("read_by_act"), "dve": sem("read_by_dve")}
        table_written = sem("table_written")
        acc_zeroed = sem("acc_zeroed")
        att_built, terms_built, mean_ready = sem("att_built"), sem("terms_built"), sem("mean_ready")
        hid0_ready, hid0_parts = sem("hid0_ready"), sem("hid0_parts")
        adst_ready = sem("adst_ready")
        gaps_in, gaps_out = sem("node_gaps"), sem("node_gaps_exp")
        g_low = sem("g_low")
        g1_ready = sem("g1_ready")
        centered, squared, var_ready, rooted = sem("centered"), sem("squared"), sem("var_ready"), sem("rooted")
        x_ready = sem("x_ready")
        y_half, y_made, row_summed = sem("y_half"), sem("y_made"), sem("row_summed")
        squares_summed = sem("squares_summed")
        sums_scaled = sem("sums_scaled")
        edges_weighed, loops_weighed, loops_added, attended = (
            sem("edges_weighed"), sem("loops_weighed"), sem("loops_added"), sem("attended"))
        totals_bounded, totals_inverted = sem("totals_bounded"), sem("totals_inverted")
        negative_ready, positive_ready = sem("negative_ready"), sem("positive_ready")
        agg_scaled = sem("agg_scaled")
        agg3_ready = sem("agg3_ready")
        out_written = sem("out_written")
        gathered = [sem("gathered0"), sem("gathered1")]
        wide_gathered = [sem(f"wide_gathered{q}") for q in range(4)]
        idx_staged, pool_tick = sem("idx_staged"), sem("pool_tick")
        onehot_ready, summed, accumulated = sem("onehot_ready"), sem("summed"), sem("accumulated")
        ea_loaded = [sem("ea_loaded0"), sem("ea_loaded1")]
        edge_product, pre_ready, parts_ready, elu_ready = (
            sem("edge_product"), sem("pre_ready"), sem("parts_ready"), sem("elu_ready"))
        neg_loaded = [sem("neg_loaded0"), sem("neg_loaded1")]
        rel_loaded = [sem("rel_loaded0"), sem("rel_loaded1")]
        squares_ready, term_done, heads_turned = sem("squares_ready"), sem("term_done"), sem("heads_turned")
        dst_terms_ready = sem("dst_terms_ready")
        rel_ready, taken, logit_ready, logit_turned = (
            sem("rel_ready"), sem("taken"), sem("logit_ready"), sem("logit_turned"))
        max_ready, rise_ready, gaps_split, exp_ready, run_ready = (
            sem("max_ready"), sem("rise_ready"), sem("gaps_split"), sem("exp_ready"), sem("run_ready"))
        turn_done, turned_ready = sem("turn_done"), sem("turned_ready")

        def has(g, back=0):
            return not isinstance(g, int) or 0 <= g - back < NG

        def early(x, n):
            return isinstance(x, int) and x < n

        def slots(eng, slot, tail, head=2, tiles_of=None, ways=2):
            head = -(-head // UNROLL) * UNROLL

            def tiles(g, groups):
                if not tiles_of or not has(g, tiles_of[1]):
                    return [()] * groups
                values = step_values(tiles_of[0], tile_i, g - tiles_of[1], NT - 1, groups)
                return [(values[u * G:(u + 1) * G],) for u in range(groups)]

            for g in range(head):
                slot(g, g % ways, *tiles(g, 1)[0])
            with eng.Fori(head // UNROLL, NG // UNROLL) as i:
                values = tiles(i * UNROLL, UNROLL)
                for u in range(UNROLL):
                    slot(i * UNROLL + u, u % ways, *values[u])
            for g in range(NG, NG + tail):
                slot(g, g % ways, *tiles(g, 1)[0])

        def half(g, b):
            return g // 2 if isinstance(g, int) else (g - b) // 2

        def step_values(eng_type, ints, g, top, groups=1):
            return nc.values_load_multi_w_load_instructions(
                ints[0:1, bass.ds(g * G, groups * G)], engines=(eng_type,), min_val=0, max_val=top,
                skip_runtime_bounds_check_because="the merge path, counted on the chip, stays in the grid")[1]

        base = {k: NG * n for n, k in enumerate(PASSES)}

        def row_buffers(k):
            if k == "sage1":
                more = y_flat[:, 0:2 * G * 256].rearrange("p (b g f) -> p b g f", b=2, g=G)
                return [rows[:, 0], rows[:, 1], more[:, 0], more[:, 1]], wide_gathered
            return [rows[:, 0], rows[:, 1]], gathered

        def loads_before(k):
            return sum(NG // 2 for p in PASSES[:PASSES.index(k)] if p != "sage1")

        block = ctx.enter_context(nc.Block())

        @block.sync
        def _(sp):
            sp.dma_start(edges_in[0:CH, :], edges_i).then_inc(edges_loaded, 16)
            sp.dma_start(xT[:, :], xT_in).then_inc(x_loaded, 16)
            def write_parts(to, rows_sb, per, ready):
                units = packs(per)
                for i in range(TABLE_PARTS):
                    lo, hi = (-(-len(units) * k // TABLE_PARTS) for k in (i, i + 1))
                    tiles = slice(units[lo][0], units[hi - 1][-1] + 1)
                    sp.wait_ge(*ready(hi - 1))
                    sp.dma_start(to[:, tiles, :], rows_sb[:, tiles, :]).then_inc(table_written, 16)

            def write_table(k, rows_sb, stage=None, per=4, norms=0, who="act"):
                if stage:
                    def ready(u):
                        return read_by[who], fills_read(FIRST_FILL[stage] + u + 1, who)
                else:
                    def ready(u):
                        return x_ready, (norms - 1) * NPACK + u + 1
                write_parts(table[k].rearrange("(t p) f -> p t f", p=P), rows_sb, per, ready)

            def load_ea(g, b, freed, at):
                if not early(g, 2):
                    sp.wait_ge(freed, at + g - 1)
                for j, blk in enumerate(step_values(mybir.EngineType.SP, block_i, g, NB - 1)):
                    sp.dma_start(ea_sb[:, b, j, :], ea_blocks[bass.ds(blk, 1), :, :].rearrange("o p e -> p (o e)"))\
                      .then_inc(ea_loaded[b], 16)

            def load_rows_of(rows_in_dram, to, loaded, g, b):
                sp.dma_start(to[:, b, :],
                             rows_in_dram[bass.ds(g * G, G), :].rearrange("s e -> (s e)").partition_broadcast(P))\
                  .then_inc(loaded[b], 16)

            wide = big[:, 3:5, :].rearrange("p a n -> p (a n)").rearrange("p (t f) -> p t f", t=NT)
            low = big[:, 0:2, :].rearrange("p a n -> p (a n)").rearrange("p (t f) -> p t f", t=NT)
            write_table("mlp", wide, "tab0", 2, who="dve")
            sp.wait_ge(sel_ready, 1)
            slots(sp, lambda g, b: load_ea(g, b, edge_product, 0), 0)

            def softmax_rows(k):
                n, heads = SOFTMAX[k]
                sp.wait_ge(rows_stored, 128)
                sp.wait_ge(acc_zeroed, PASSES.index(k) + 1)

                def slot(s, b):
                    if has(s, 1):
                        if not early(s, 3):
                            sp.wait_ge(rise_ready, n * NG + s - 2)
                        load_rows_of(neg_rows, neg_b, neg_loaded, s - 1, 1 - b)
                    if has(s):
                        if not heads:
                            load_ea(s, b, taken, n * NG)
                        else:
                            if not early(s, 2):
                                sp.wait_ge(rel_ready, n * NG + s - 1)
                            load_rows_of(rel_rows, rel_b, rel_loaded, s, b)
                slots(sp, slot, 1, head=4)

            write_table("gat1", h_sb[:, :, 0:ROW["gat1"]], "h1", 3)
            softmax_rows("gat1")
            write_table("gat2", h_sb[:, :, 0:ROW["gat2"]], "h2", 3)
            softmax_rows("gat2")
            write_table("sage0", x_sb[:, :, :], norms=2)
            write_table("sage1", low, "p1", 2)
            write_table("sage2", h_sb[:, :, 0:D], "p2", 4)
            write_table("pool", x_sb[:, :, :], norms=3)
            softmax_rows("pool")
            full = N_NODES // P
            out_tiles = out[0:full * P, :].rearrange("(t p) f -> p t f", p=P)
            for u, tiles in enumerate(packs(4)):
                sp.wait_ge(x_ready, 3 * NPACK + u + 1)
                at = slice(tiles[0], min(tiles[-1] + 1, full))
                if at.start < at.stop:
                    sp.dma_start(out_tiles[:, at, :], x_sb[:, at, :]).then_inc(out_written, 16)
            sp.dma_start(out[full * P:N_NODES, :], x_sb[0:N_NODES - full * P, full, :]).then_inc(out_written, 16)
            sp.wait_ge(out_written, 16 * (1 + -(-full // 4)))

        @block.gpsimd
        def _(pool):
            pool.iota(iota_i[:, :], pattern=[[1, S]], base=0, channel_multiplier=0).then_inc(iotas_ready, 1)
            pool.iota(part_i[:, :], pattern=[[0, 1]], base=0, channel_multiplier=1).then_inc(iotas_ready, 1)
            pool.wait_ge(src_ready, 1)

            def gather_pass(k, *freed):
                to, loaded = row_buffers(k)
                n = len(to)
                first = base[k] // 2

                def stage(pair, to):
                    pool.tensor_copy(idx_stage[:, to, :], src_idx[:, bass.ds(pair * 2 * G, 2 * G)])\
                        .then_inc(idx_staged, 1)

                def pair(p, par, peeled):
                    for b in range(2):
                        if not (peeled and p * 2 < n):
                            for read, read_at in freed:
                                pool.wait_ge(read, read_at + p * 2 + b - (n - 1))
                        if b == 0:
                            pool.wait_ge(idx_staged, PASSES.index(k) * (NG // 2 + 1) + p + 1)
                            pool.sem_inc(pool_tick, 1)
                        else:
                            stage(p + 1, (par + 1) % PAIRS)
                        for j in range(G):
                            pool.indirect_dma_start(
                                to[(2 * par + b) % n][:, j, 0:ROW[k]], None, table[k],
                                bass.IndirectOffsetOnAxis(idx_stage[:, par, b * G + j:b * G + j + 1], 0))\
                                .then_inc(loaded[(2 * par + b) % n], 16)

                pool.wait_ge(table_written, 16 * TABLE_PARTS * (PASSES.index(k) + 1))
                if first:
                    pool.wait_ge(idx_staged, PASSES.index(k) * (NG // 2 + 1))
                stage(0, 0)
                for p in range(PAIRS):
                    pair(p, p, True)
                with pool.Fori(1, NG // (2 * PAIRS)) as i:
                    for p in range(PAIRS):
                        pair(i * PAIRS + p, p, False)

            gather_pass("mlp", (pre_ready, 0))
            gather_pass("gat1", (leak_ready, 0), (taken, 0))
            gather_pass("gat2", (leak_ready, NG), (taken, NG))
            gather_pass("sage0", (summed, base["sage0"]))
            gather_pass("sage1", (summed, base["sage1"]))
            gather_pass("sage2", (summed, base["sage2"]))
            gather_pass("pool", (taken, 2 * NG))

        @block.tensor
        def _(pe):
            pe.wait_ge(below_ready, 1)
            for c in range(NCH):
                mm = pe.matmul(ps[0:NT - 1, 0, 0:1], below[0:CH, c, 0:NT - 1], ones[0:CH, 0:1],
                               start=(c == 0), stop=(c == NCH - 1))
            mm.then_inc(keys_summed, 1)
            pe.wait_ge(moved_ready, 1)
            pe.matmul(ps[:, 1, 0:S], ones[0:NT - 1, :], moved[0:NT - 1, :], start=True, stop=True)\
              .then_inc(tiles_spread, 1)
            def fill(name, u):
                n = FIRST_FILL[name] + u
                if n >= RING:
                    who = FILLS[n - RING][2]
                    pe.wait_ge(read_by[who], fills_read(n - RING + 1, who))
                return ps[:, n % RING, :]

            def row_products(name, per, width, terms, bias, wait_for=None):
                for u, tiles in enumerate(packs(per)):
                    bank = fill(name, u)
                    if wait_for:
                        wait_for(tiles)
                    for i, t in enumerate(tiles):
                        to = bank[:, i * width:(i + 1) * width]
                        for n, (act, w) in enumerate(terms):
                            mm = pe.matmul(to, act[:, pick(t)], w, start=(n == 0),
                                           stop=(n == len(terms) - 1 and bias is None))
                        if bias is not None:
                            mm = pe.matmul(to, ones[0:1, :], bias, start=False, stop=True)
                    mm.then_inc(fill_done, 1)

            def column_products(name, terms_of):
                for c in range(NCOL):
                    at = slice(c * COLS, (c + 1) * COLS)
                    for m in range(2):
                        bank = fill(name, 2 * c + m)
                        terms = terms_of(m)
                        for n, (w, act) in enumerate(terms):
                            mm = pe.matmul(bank[:, 0:COLS], w, act[:, at], start=(n == 0), stop=(n == len(terms) - 1))
                        mm.then_inc(fill_done, 1)

            def turn_rows(name, of, ready, before=0):
                for u, tiles in enumerate(packs(4)):
                    bank = fill(name, u)
                    pe.wait_ge(ready, before + u + 1)
                    for i, t in enumerate(tiles):
                        mm = pe.transpose(bank[:, i * P:(i + 1) * P], of(t), ident[:, :])
                    mm.then_inc(fill_done, 1)

            pe.wait_ge(weights_loaded, 48)
            pe.wait_ge(x_loaded, 16)
            pe.wait_ge(sel_ready, 1)
            row_products("tab0", 2, 256, [(xT, weight("W1a", 0))], None)
            pe.wait_ge(read_by["dve"], fills_read(FIRST_FILL["Wc"], "dve"))
            for n, k in enumerate((0, 1, 3)):
                for c in range(NCH):
                    mm = pe.matmul(ps[:, 2 + n, 0:S], edges_f[0:CH, k, c, :], sel[0:CH, c, :],
                                   start=(c == 0), stop=(c == NCH - 1))
                mm.then_inc(cols_moved, 1)
            for q in range(4):
                at = slice(q * BCH, (q + 1) * BCH)
                for n, k in enumerate((1, 2)):
                    for c in range(NCH):
                        pe.matmul(ps[0:BCH, 5 + q % 2, n * P:(n + 1) * P], sel[0:CH, c, at], edges_f[0:CH, k, c, :],
                                  start=(c == 0), stop=(c == NCH - 1))
                mm = pe.matmul(ps[0:BCH, 5 + q % 2, 2 * P:2 * P + 1], moved[0:NT - 1, at], ones[0:NT - 1, 0:1],
                               start=True, stop=True)
                mm.then_inc(rows_moved, 1)
                if 1 <= q < 3:
                    pe.wait_ge(rows_ready_parts, q)
            pe.wait_ge(rows_ready, 1)
            for m in range(2):
                bank = fill("Wc", m)
                for k in range(2):
                    mm = pe.matmul(bank[:, 0:256], weight("W1bT", k, m * P, P), weight("W2a", 1 + k),
                                   start=(k == 0), stop=(k == 1))
                mm.then_inc(fill_done, 1)
            bank = fill("Wc", 2)
            for k in range(2):
                mm = pe.matmul(bank[0:1, 0:256], weight("b1b", 0, k, 1), weight("W2a", 1 + k),
                               start=(k == 0), stop=(k == 1))
            mm.then_inc(fill_done, 1)
            pe.wait_ge(att_built, 1)
            pe.matmul(fill("att", 0)[:, 0:2 * HEADS], weight("gW1T", 0), att_block[:, :], start=True, stop=True)\
              .then_inc(fill_done, 1)
            pe.matmul(fill("att", 1)[:, 0:2], weight("gW2T", 0), weight("att2", 0), start=True, stop=True)\
              .then_inc(fill_done, 1)

            def mlp_slot(g, b):
                if has(g):
                    if not early(g, 2):
                        pe.wait_ge(pre_ready, g - 1)
                    pe.wait_ge(ea_loaded[b], 16 * G * (half(g, b) + 1))
                    for j in range(G):
                        mm = pe.matmul(ps[:, 2 * b + j // 2, (j % 2) * 256:(j % 2) * 256 + 256], ea_sb[:, b, j, :],
                                       weight("W1a", 1), start=True, stop=True)
                    mm.then_inc(edge_product, 1)
                if has(g, 3):
                    pe.wait_ge(elu_ready, g - 2)
                    pe.wait_ge(onehot_ready, g - 2)
                    q = 1 - b
                    for j in range(G):
                        if has(g, 4):
                            pe.wait_ge(accumulated, G * (g - 4) + j + 1)
                        mm = pe.matmul(ps[:, 4 + j, 0:SUMS["mlp"]], onehot[:, q, j, :], pos_part[:, q, j, :],
                                       start=True, stop=True)
                    mm.then_inc(summed, 1)

            pe.wait_ge(read_by["dve"], fills_read(FIRST_FILL["mT"], "dve"))
            slots(pe, mlp_slot, 3, head=4)

            pe.wait_ge(mean_ready, 1)
            mean = sum_rows("mlp")
            for m in range(2):
                for u, tiles in enumerate(packs(4)):
                    bank = fill("mT", 7 * m + u)
                    for i, t in enumerate(tiles):
                        mm = pe.transpose(bank[:, i * P:(i + 1) * P], mean[:, t, m * P:(m + 1) * P], ident[:, :])
                    mm.then_inc(fill_done, 1)
            for u, tiles in enumerate(packs(4)):
                bank = fill("flag", u)
                for i, t in enumerate(tiles):
                    mm = pe.transpose(bank[0:1, i * P:(i + 1) * P], mean[:, t, 2 * P:2 * P + 1], ident[:, :])
                mm.then_inc(fill_done, 1)
            pe.wait_ge(read_by["act"], fills_read(FIRST_FILL["hid0"], "act"))
            column_products("hid0", lambda m: [(weight("W2a", 0, m * P, P), xT),
                                               (Wc[:, 0, m * P:(m + 1) * P], big[:, 3, :]),
                                               (Wc[:, 1, m * P:(m + 1) * P], big[:, 4, :]),
                                               (bc[0:1, m * P:(m + 1) * P], flags)])

            def wait_for_hidden(tiles):
                pe.wait_ge(hid0_ready, 2 * -(-(tiles[-1] + 1) * P // COLS))
            row_products("out0", 4, D, [(big[:, 0, :], weight("W2b", 0)), (big[:, 1, :], weight("W2b", 1))], None,
                         wait_for_hidden)
            turn_rows("x1T", lambda t: x_sb[:, t, :], x_ready)
            pe.wait_ge(read_by["act"], fills_read(FIRST_FILL["h1"], "act"))
            row_products("h1", 3, D + 2 * HEADS, [(xT, gcat["gat1"][:, :])], None)
            for u, tiles in enumerate(packs(4)):
                bank = fill("invT", u)
                for i, t in enumerate(tiles):
                    mm = pe.matmul(bank[:, i * P:(i + 1) * P], inv_row[:, t:t + 1].to_broadcast([P, P]), ident[:, :],
                                   start=True, stop=True)
                mm.then_inc(fill_done, 1)

            def softmax_pass(k):
                n, heads = SOFTMAX[k]
                at, all_at = n * NG, base[k]
                width = SUMS[k]
                if heads:
                    pe.wait_ge(adst_ready, n + 1)

                def take(x, b):
                    pe.wait_ge(gathered[b], 16 * G * (loads_before(k) + half(x, b) + 1))
                    if not heads:
                        pe.wait_ge(ea_loaded[b], 16 * G * (NG // 2 + half(x, b) + 1))
                    if not early(x, 2):
                        pe.wait_ge(hp_ready, at + x - 1)
                    for j in range(G):
                        if heads:
                            mm = pe.transpose(ps[:, 2 + b, j * P:(j + 1) * P], rows[:, b, j, 0:D], ident[:, :])
                        else:
                            to = ps[:, b, j * P:(j + 1) * P]
                            pe.matmul(to, ident[:, :], ea_sb[:, b, j, :], start=True, stop=False)
                            mm = pe.matmul(to, rows[:, b, j, 0:D], ident[:, :], start=False, stop=True)
                    mm.then_inc(taken, 1)

                def add_terms(x, b, tiles):
                    pe.wait_ge(rel_ready, at + x + 1)
                    if not early(x, 1):
                        pe.wait_ge(dst_terms_ready, at + x)
                    if not early(x, 4):
                        pe.wait_ge(turned_ready, at + x - 3)
                    for j, t in enumerate(tiles):
                        at_j = TERMS[b] + j * 3 * heads
                        mm = pe.matmul(ps[:, 5, at_j:at_j + 3 * heads], rel_T[:, b, j * P:(j + 1) * P],
                                       adst[:, bass.ds(t, 1), 0:3 * heads].rearrange("p o h -> p (o h)"),
                                       start=True, stop=True)
                    mm.then_inc(term_done, 1)

                def spread_logits(x, b):
                    pe.wait_ge(logit_ready, at + x + 1)
                    if not early(x, 2):
                        pe.wait_ge(rise_ready, at + x - 1)
                    for j in range(G):
                        mm = pe.transpose(ps[:, b, j * P:(j + 1) * P], logit[:, b, j * P:(j + 1) * P], ident[:, :])
                    mm.then_inc(logit_turned, 1)

                def turn_maxima(x, b):
                    for j in range(G):
                        at_j = ((b * G + j) * 2 + 1) * heads
                        mm = pe.transpose(ps[:, 5, at_j:at_j + heads], max_run[0:heads, b, 1 + j * P:1 + (j + 1) * P],
                                          ident[0:heads, 0:heads])
                    mm.then_inc(heads_turned, 1)

                def wait_for_maxima(x):
                    pe.wait_ge(max_ready, at + x + 1)
                    pe.wait_ge(dst_terms_ready, min(at + x + 3, at + NG) if isinstance(x, int) else at + x + 3)
                    if not early(x, 2):
                        pe.wait_ge(turned_ready, at + x - 1)

                def turn_both(s, b):
                    x = s - 4
                    if has(s, 4):
                        pe.wait_ge(run_ready, at + x + 1)
                        if not early(x, 1):
                            pe.wait_ge(turned_ready, at + x)
                    for j in range(G):
                        if j == G - 1 and heads and has(s, 3):
                            wait_for_maxima(s - 3)
                        if has(s, 4):
                            cols = slice(j * P, (j + 1) * P)
                            mm = pe.transpose(ps[:, 4, cols], w_run[:, b, cols], ident[:, :])
                    if heads and has(s, 3):
                        turn_maxima(s - 3, 1 - b)
                    if has(s, 4):
                        for j in range(G):
                            cols = slice(j * P, (j + 1) * P)
                            if heads:
                                at_j = (b * G + j) * 2 * heads
                                mm = pe.transpose(ps[:, 5, at_j:at_j + heads], s_run[0:heads, b, cols],
                                                  ident[0:heads, 0:heads])
                            else:
                                mm = pe.transpose(ps[:, 5, cols], s_run[:, b, cols], ident[:, :])
                        mm.then_inc(turn_done, 1)

                def finish(x, b):
                    pe.wait_ge(turned_ready, at + x + 1)
                    pe.wait_ge(onehot_ready, all_at + x + 1)
                    for j in range(G):
                        if not early(x, 1) and j % 2 == 0:
                            pe.wait_ge(accumulated, G * (all_at + x - 1) + j + 2)
                        mm = pe.matmul(ps[:, 6 + j // 2, (j % 2) * 256:(j % 2) * 256 + width], onehot[:, b, j, :],
                                       turned[:, b, j, 0:width], start=True, stop=True)
                    mm.then_inc(summed, 1)

                def slot(s, b, tiles=None):
                    turn_both(s, b)
                    if has(s, 1):
                        take(s - 1, 1 - b)
                    if has(s, 1) and heads:
                        spread_logits(s - 1, 1 - b)
                    if has(s) and heads:
                        add_terms(s, b, tiles)
                    if has(s, 4):
                        finish(s - 4, b)
                slots(pe, slot, 4, head=6, tiles_of=(mybir.EngineType.PE, 0) if heads else None)

            pe.wait_ge(read_by["act"], fills_read(FIRST_FILL["gT"], "act"))
            softmax_pass("gat1")
            turn_rows("gT", lambda t: y_sb[:, t, :], g1_ready)
            pe.wait_ge(read_by["act"], fills_read(FIRST_FILL["h2"], "act"))
            row_products("h2", 3, D + 2, [(big[:, 3, :], gcat["gat2"][:, :])], None)
            pe.wait_ge(read_by["act"], fills_read(FIRST_FILL["x2T"], "act"))
            softmax_pass("gat2")
            turn_rows("x2T", lambda t: x_sb[:, t, :], x_ready, NPACK)

            def sum_pass(k, by_row):
                all_at = base[k]
                chunks = ROW[k] // P

                buffers, loaded = row_buffers(k)
                ways = len(buffers)

                def slot(g, q):
                    b = q % 2
                    if ways == 2:
                        pe.wait_ge(loaded[q], 16 * G * (loads_before(k) + half(g, q) + 1))
                    else:
                        pe.wait_ge(loaded[q], 16 * G * ((g - q) // 4 + 1))
                    pe.wait_ge(onehot_ready, all_at + g + 1)
                    if not early(g, 2):
                        pe.wait_ge(accumulated, G * (all_at + g - 1))
                    for j in range(G):
                        to = ps[:, 4 + 2 * b + j // 2, (j % 2) * 256:(j % 2) * 256 + 256]
                        if by_row:
                            mm = pe.matmul(to[:, 0:P], onehot[:, b, j, :], buffers[q][:, j, 0:P], start=True, stop=True)
                        else:
                            for c in range(chunks):
                                mm = pe.matmul(to[:, c * P:(c + 1) * P], buffers[q][:, j, c * P:(c + 1) * P],
                                               onehot[:, b, j, :], start=True, stop=True)
                    mm.then_inc(summed, 1)
                slots(pe, slot, 0, ways=ways)

            sum_pass("sage0", False)
            pe.wait_ge(agg_scaled, 1)
            pe.wait_ge(read_by["act"], fills_read(FIRST_FILL["sh0"], "act"))
            column_products("sh0", lambda m: [(weight("Ws0", 0, m * P, P), xT),
                                              (weight("Wn0", 0, m * P, P), sum_T[:, 0, :])])
            pe.wait_ge(read_by["act"], fills_read(FIRST_FILL["p1"], "act"))
            row_products("p1", 2, 256, [(big[:, 3, :], weight("Wn1", 0)), (big[:, 4, :], weight("Wn1", 1))], None)
            sum_pass("sage1", False)
            pe.wait_ge(agg_scaled, 2)
            column_products("sh1", lambda m: [(weight("Ws1", 0, m * P, P), big[:, 3, :]),
                                              (weight("Ws1", 1, m * P, P), big[:, 4, :]),
                                              (ident[:, :], sum_T[:, m, :])])
            pe.wait_ge(read_by["act"], fills_read(FIRST_FILL["p2"], "act"))
            row_products("p2", 4, D, [(big[:, 0, :], weight("Wn2", 0)), (big[:, 1, :], weight("Wn2", 1))], None)
            sum_pass("sage2", True)
            row_products("out2", 4, D, [(big[:, 0, :], weight("Ws2", 0)), (big[:, 1, :], weight("Ws2", 1))],
                         bias_row("sb2"))
            pe.wait_ge(read_by["dve"], fills_read(FIRST_FILL["last"], "dve"))
            softmax_pass("pool")
            for u, tiles in enumerate(packs(4)):
                bank = fill("last", 2 * u)
                pe.wait_ge(agg3_ready, u + 1)
                for i, t in enumerate(tiles):
                    mm = pe.transpose(bank[:, i * P:(i + 1) * P], y_sb[:, t, :], ident[:, :])
                mm.then_inc(fill_done, 1)
                bank = fill("last", 2 * u + 1)
                pe.wait_ge(read_by["act"], fills_read(FIRST_FILL["last"] + 2 * u + 1, "act"))
                for i, t in enumerate(tiles):
                    to = bank[:, i * D:(i + 1) * D]
                    pe.matmul(to, xT[:, pick(t)], weight("mlpT", 0), start=True, stop=False)
                    mm = pe.matmul(to, ones[0:1, :], bias_row("mlp_b"), start=False, stop=True)
                mm.then_inc(fill_done, 1)

        @block.scalar
        def _(act):
            links = [0]

            def link(ins):
                links[0] += 1
                ins.then_inc(act_link, 1)
                act.wait_ge(act_link, links[0])

            act.dma_start(w_sb[:, :], wpack).then_inc(weights_loaded, 16)
            act.dma_start(b_sb[:, :], bpack).then_inc(weights_loaded, 16)
            act.dma_start(r_sb[:, :], rpack.rearrange("o n -> (o n)").partition_broadcast(P)).then_inc(weights_loaded, 16)
            act.dma_start(x_sb[:, :, :], x_rows.rearrange("(t p) f -> p t f", p=P)).then_inc(x_rows_loaded, 16)

            def filled(name, u):
                n = FIRST_FILL[name] + u
                act.wait_ge(fill_done, n + 1)
                return ps[:, n % RING, :]

            def copy_rows(name, per, width, to, func=ACT.Copy):
                for u, tiles in enumerate(packs(per)):
                    bank = filled(name, u)[:, 0:len(tiles) * width].rearrange("p (t f) -> p t f", f=width)
                    act.activation(to[:, tiles[0]:tiles[-1] + 1, 0:width], bank, func).then_inc(read_by["act"], 1)

            def copy_turned(name, to):
                for u, tiles in enumerate(packs(4)):
                    bank = filled(name, u)
                    act.activation(to[:, tiles[0] * P:(tiles[-1] + 1) * P], bank[:, 0:len(tiles) * P], ACT.Copy)\
                       .then_inc(read_by["act"], 1)

            low = big[:, 0:2, :].rearrange("p a n -> p (a n)").rearrange("p (t f) -> p t f", t=NT)
            wide = big[:, 3:5, :].rearrange("p a n -> p (a n)").rearrange("p (t f) -> p t f", t=NT)

            def square_distances(k, x, b, values):
                if not early(x, 2):
                    act.wait_ge(summed, base[k] + x - 1)
                for j in range(G):
                    ins = act.activation(onehot[:, b, j, :], iota[:, 0:P], ACT.Square,
                                         bias=values[:, bass.ds(x * G + j, 1)], scale=-1.0)
                ins.then_inc(squares_ready, 1)

            def mark_edges(nth, x, b):
                act.wait_ge(squares_ready, nth * NG + x + 1)
                act.activation(onehot[:, b], onehot[:, b], ACT.Relu, bias=ones[:, 0:1], scale=-1.0)\
                   .then_inc(onehot_ready, 1)

            act.wait_ge(rows_ready, 1)
            for q in range(4):
                act.dma_start(neg_rows[q * BCH:(q + 1) * BCH, :], row_b[0:BCH, q, 0, :]).then_inc(rows_stored, 16)
                act.dma_start(rel_rows[q * BCH:(q + 1) * BCH, :], row_b[0:BCH, q, 1, :]).then_inc(rows_stored, 16)
            act.wait_ge(rows_stored, 128)
            mean = sum_rows("mlp")
            zeros = ones[:, 0:1].unsqueeze(2).to_broadcast([P, NT, SUMS["mlp"]])
            act.activation(mean, zeros, ACT.Copy, scale=0.0).then_inc(acc_zeroed, 1)

            def mlp_slot(g, b):
                act.wait_ge(pre_ready, g + 1)
                if not early(g, 2):
                    act.wait_ge(elu_ready, g - 1)
                act.activation(neg_part[:, b], pre[:, b], ACT.Relu, scale=-1.0).then_inc(parts_ready, 1)
                if not early(g, 2):
                    act.wait_ge(summed, g - 1)
                act.activation(pos_part[:, b, :, 0:256], pre[:, b], ACT.Relu).then_inc(parts_ready, 1)
                act.wait_ge(parts_ready, 3 * g + 2)
                act.activation(neg_part[:, b], neg_part[:, b], ACT.Exp, scale=-1.0).then_inc(parts_ready, 1)
            slots(act, mlp_slot, 0)

            for m in range(2):
                for u, tiles in enumerate(packs(4)):
                    act.activation(big[:, 3 + m, tiles[0] * P:(tiles[-1] + 1) * P],
                                   filled("mT", 7 * m + u)[:, 0:len(tiles) * P], ACT.Copy)\
                       .then_inc(read_by["act"], 1)
            for u, tiles in enumerate(packs(4)):
                act.activation(flags[:, tiles[0] * P:(tiles[-1] + 1) * P],
                               filled("flag", u)[0:1, 0:len(tiles) * P], ACT.Copy).then_inc(read_by["act"], 1)
            low_bias = small[:, 0, 0:2]
            link(act.mul(low_bias, weight("b2a", 0), -1.0))

            def low_exp(u):
                act.wait_ge(hid0_parts, 2 * u + 1)
                act.activation(neg_node(u % 4), neg_node(u % 4), ACT.Exp, scale=-1.0).then_inc(hid0_parts, 1)

            for c in range(NCOL):
                for m in range(2):
                    u = 2 * c + m
                    bank = filled("hid0", u)
                    if u >= 4:
                        act.wait_ge(hid0_ready, u - 3)
                    act.activation(neg_node(u % 4), bank[:, 0:COLS], ACT.Relu, bias=low_bias[:, m:m + 1],
                                   scale=-1.0).then_inc(hid0_parts, 1)
                    act.activation(pos_node(u % 4), bank[:, 0:COLS], ACT.Relu, bias=weight("b2a", 0)[:, m:m + 1])\
                       .then_inc(read_by["act"], 1)
                    low_exp(u)

            def norm(n):
                for u in range(NPACK):
                    act.wait_ge(centered, (n - 1) * NPACK + u + 1)
                    at = pack_columns(u)
                    act.activation(spare[:, at], y_flat[:, at], ACT.Square).then_inc(squared, 1)
                act.wait_ge(var_ready, n)
                act.activation(stat[:, 1, :], stat[:, 2, :], ACT.Sqrt).then_inc(rooted, 1)

            norm(1)
            copy_turned("x1T", xT)
            copy_rows("h1", 3, D + 2 * HEADS, h_sb)
            copy_turned("invT", inv_T)

            def softmax_pass(k):
                n, heads = SOFTMAX[k]
                at = n * NG
                extra = 2 * heads if heads else D

                def make_logits(x, b):
                    act.wait_ge(leak_ready, at + x + 1)
                    if not early(x, 2):
                        act.wait_ge(logit_turned, at + x - 1)
                    terms = leaks[:, b, 1, 0:G * heads].rearrange("p (g h) -> p g h", g=G).unsqueeze(2)\
                        .to_broadcast([P, G, D // heads, heads])
                    act.activation(logit[:, b, :].rearrange("p (g f h) -> p g f h", g=G, h=heads), terms, ACT.Copy)\
                       .then_inc(logit_ready, 1)

                def copy_turned_sums(x, b):
                    act.wait_ge(turn_done, at + x + 1)
                    if not early(x, 2):
                        act.wait_ge(summed, base[k] + x - 1)
                    act.activation(turned[:, b, :, 0:D], ps[:, 4, :].rearrange("p (g f) -> p g f", g=G), ACT.Copy)
                    at_5 = b * G * extra if heads else 0
                    act.activation(turned[:, b, :, D:D + extra],
                                   ps[:, 5, at_5:at_5 + G * extra].rearrange("p (g f) -> p g f", g=G), ACT.Copy)\
                       .then_inc(turned_ready, 1)

                def exponentials(x, b):
                    act.wait_ge(rise_ready, at + x + 1)
                    if not early(x, 2):
                        act.wait_ge(run_ready, at + x - 1)
                    act.activation(gaps[:, b, 0, :], rise[:, b, :], ACT.Relu).then_inc(gaps_split, 1)
                    act.activation(gaps[:, b, 1, :], rise[:, b, :], ACT.Relu, scale=-1.0).then_inc(gaps_split, 1)
                    act.wait_ge(gaps_split, 2 * (at + x + 1))
                    act.activation(gaps[:, b], gaps[:, b], ACT.Exp, scale=-1.0).then_inc(exp_ready, 1)

                def slot(s, b):
                    if has(s, 3):
                        square_distances(k, s - 3, 1 - b, last_rel)
                    if has(s, 4):
                        copy_turned_sums(s - 4, b)
                    if has(s, 1) and heads:
                        make_logits(s - 1, 1 - b)
                    if has(s, 3):
                        mark_edges(n, s - 3, 1 - b)
                    if has(s, 2):
                        exponentials(s - 2, b)
                slots(act, slot, 4, head=6)
                if heads:
                    act.wait_ge(gaps_in, n + 1)
                    m = NT * heads
                    act.activation(small[:, 3:5, 0:m], small[:, 3:5, 0:m], ACT.Exp).then_inc(gaps_out, 1)

            softmax_pass("gat1")
            for step in range(NPACK + 1):
                if step < NPACK:
                    at = pack_columns(step)
                    act.wait_ge(attended, step + 1)
                    act.activation(spare[:, at], y_flat[:, at], ACT.Relu, scale=-1.0).then_inc(negative_ready, 1)
                if step:
                    at = pack_columns(step - 1)
                    act.wait_ge(negative_ready, step)
                    act.activation(spare[:, at], spare[:, at], ACT.Exp, scale=-1.0).then_inc(g_low, 1)
            copy_turned("gT", big[:, 3, :])
            copy_rows("h2", 3, D + 2, h_sb)
            softmax_pass("gat2")
            norm(2)
            copy_turned("x2T", xT)

            def relu_columns(name, bias, to):
                for c in range(NCOL):
                    for m in range(2):
                        bank = filled(name, 2 * c + m)
                        act.activation(big[:, to + m, c * COLS:(c + 1) * COLS], bank[:, 0:COLS], ACT.Relu,
                                       bias=weight(bias, 0)[:, m:m + 1]).then_inc(read_by["act"], 1)

            relu_columns("sh0", "sb0", 3)
            copy_rows("p1", 2, 256, low)
            relu_columns("sh1", "sb1", 0)
            copy_rows("p2", 4, D, h_sb)
            norm(3)
            softmax_pass("pool")
            for u, tiles in enumerate(packs(4)):
                at = pack_columns(u)
                act.activation(xT[:, at], filled("last", 2 * u)[:, 0:len(tiles) * P], ACT.Copy).then_inc(read_by["act"], 1)
                act.activation(y_flat[:, at], filled("last", 2 * u + 1)[:, 0:len(tiles) * D], ACT.Relu)\
                   .then_inc(read_by["act"], 1)
            norm(4)

        @block.vector
        def _(dve):
            links = [0]

            def link(ins):
                links[0] += 1
                ins.then_inc(dve_link, 1)
                dve.wait_ge(dve_link, links[0])

            link(dve.memset(ones[:, :], 1.0))
            dve.wait_ge(iotas_ready, 2)
            dve.tensor_copy(iota[:, :], iota_i[:, :])
            link(dve.tensor_copy(part[:, :], part_i[:, :]))
            link(dve.tensor_scalar(ident[:, :], iota[:, 0:P], part[:, 0:1], None, ALU.is_equal))
            dve.wait_ge(edges_loaded, 16)
            dve.tensor_copy(edges_f[0:CH].rearrange("p k c e -> p (k c e)"), edges_in[0:CH, :])
            link(dve.tensor_scalar(ends[:, :], iota[:, 0:NT], float(P), float(P), ALU.mult, ALU.add))
            for c in range(NCH):
                dve.tensor_scalar(chunk_part[:, c:c + 1], part[:, :], float(c * CH), None, ALU.add)
                ins = dve.tensor_scalar(below[0:CH, c, :], ends[0:CH, :], edges_f[0:CH, 1, c, P - 1:P], None, ALU.is_gt)
            ins.then_inc(below_ready, 1)
            dve.wait_ge(keys_summed, 1)
            link(dve.tensor_tensor(key[0:NT - 1, :], ps[0:NT - 1, 0, 0:1], part[0:NT - 1, :], ALU.add))
            dve.tensor_scalar(moved[0:NT - 1, :], iota[0:NT - 1, :], key[0:NT - 1, 0:1], None, ALU.is_gt)\
               .then_inc(moved_ready, 1)
            dve.wait_ge(tiles_spread, 1)
            dve.tensor_copy(tile_i[:, :], ps[0:1, 1, 0:S])
            dve.tensor_scalar(tile_f[:, :], ps[:, 1, 0:S], float(P), None, ALU.mult)
            link(dve.tensor_tensor(block_f[:, :], iota[:, :], ps[:, 1, 0:S], ALU.subtract))
            dve.tensor_copy(block_i[:, :], block_f[0:1, :])
            for c in range(NCH):
                ins = dve.tensor_scalar(sel[0:CH, c, :], block_f[0:CH, :], chunk_part[0:CH, c:c + 1], None, ALU.is_equal)
            ins.then_inc(sel_ready, 1)
            link(dve.memset(src_idx[:, :], 0))

            def filled(name, u):
                n = FIRST_FILL[name] + u
                dve.wait_ge(fill_done, n + 1)
                return ps[:, n % RING, :]

            dve.wait_ge(weights_loaded, 48)
            for u, tiles in enumerate(packs(2)):
                dve.tensor_tensor(big_rows[:, tiles[0]:tiles[-1] + 1, :],
                                  filled("tab0", u).rearrange("p (t f) -> p t f", t=2)[:, 0:len(tiles), :],
                                  spread("b1a").unsqueeze(1).to_broadcast([P, len(tiles), 256]), ALU.add)\
                   .then_inc(read_by["dve"], 1)
            dve.wait_ge(cols_moved, 1)
            dve.tensor_copy(src_idx[:, 0:S], ps[:, 2, 0:S]).then_inc(src_ready, 1)
            dve.wait_ge(cols_moved, 3)
            dve.tensor_tensor(dst_rel[:, :], ps[:, 3, 0:S], tile_f[:, :], ALU.subtract)
            link(dve.tensor_copy(moved_last, ps[:, 4, 0:S]))
            link(dve.tensor_tensor(last_f[:, :], ps[:, 3, 0:S], moved_last, ALU.not_equal))
            link(dve.scalar_tensor_tensor(last_rel[:, :], dst_rel[:, :], 1.0, last_f[:, :], ALU.add, ALU.mult))
            link(dve.tensor_scalar(last_rel[:, :], last_rel[:, :], -1.0, None, ALU.add))
            dve.drain().then_inc(tables_ready, 1)
            for q in range(4):
                dve.wait_ge(rows_moved, q + 1)
                bank = ps[0:BCH, 5 + q % 2, :]
                link(dve.tensor_scalar(tile_col[0:BCH, q:q + 1], bank[:, 2 * P:2 * P + 1], float(P), None, ALU.mult))
                link(dve.tensor_copy(row_f[0:BCH, q, 0, :], bank[:, P:2 * P]))
                link(dve.tensor_tensor(row_f[0:BCH, q, 0, :], bank[:, 0:P], row_f[0:BCH, q, 0, :], ALU.not_equal))
                dve.tensor_scalar(row_b[0:BCH, q, 0, :], row_f[0:BCH, q, 0, :], NEG, None, ALU.mult)
                ins = dve.tensor_scalar(row_b[0:BCH, q, 1, :], bank[:, 0:P], tile_col[0:BCH, q:q + 1], None,
                                        ALU.subtract)
                ins.then_inc(rows_ready_parts, 1)
            dve.wait_ge(rows_ready_parts, 4)
            dve.drain().then_inc(rows_ready, 1)

            link(dve.tensor_reduce(head_mask[:, :], ident[:, :].rearrange("p (c h) -> p h c", h=HEADS), AX_X, ALU.add))
            for i in range(2):
                dve.tensor_scalar(att_block[:, i * HEADS:(i + 1) * HEADS], head_mask[:, :],
                                  weight("att1", 0, i, 1), None, ALU.mult).then_inc(terms_built, 1)
            dve.wait_ge(terms_built, 2)
            dve.sem_inc(att_built, 1)
            for m in range(2):
                dve.tensor_copy(Wc[:, m, :], filled("Wc", m)[:, 0:256]).then_inc(read_by["dve"], 1)
            dve.tensor_copy(bc[:, :], filled("Wc", 2)[0:1, 0:256]).then_inc(read_by["dve"], 1)
            dve.tensor_copy(gcat["gat1"][:, D:D + 2 * HEADS], filled("att", 0)[:, 0:2 * HEADS])\
               .then_inc(read_by["dve"], 1)
            dve.tensor_copy(gcat["gat2"][:, D:D + 2], filled("att", 1)[:, 0:2]).then_inc(read_by["dve"], 1)
            dve.tensor_copy(gcat["gat1"][:, 0:D], weight("gW1", 0))
            link(dve.tensor_copy(gcat["gat2"][:, 0:D], weight("gW2", 0)))

            def zero(k, what):
                dve.memset(what, 0.0).then_inc(acc_zeroed, 1)
                dve.wait_ge(acc_zeroed, PASSES.index(k) + 1)

            def make_onehot(k, g, b, values):
                dve.tensor_tensor(onehot[:, b], iota[:, 0:P].unsqueeze(1).to_broadcast([P, G, P]),
                                  values[:, bass.ds(g * G, G)].unsqueeze(2).to_broadcast([P, G, P]),
                                  ALU.is_equal).then_inc(onehot_ready, 1)

            def adding(k, g, tiles, bank_of, acc):
                def add(j):
                    to = acc(tiles[j])
                    done = G * (base[k] + g) + j
                    if not (isinstance(done, int) and done == 0):
                        dve.wait_ge(accumulated, done)
                    dve.tensor_tensor(to, to, bank_of(j), ALU.add).then_inc(accumulated, 1)
                return add

            def accumulate(k, g, tiles, bank_of, acc):
                add = adding(k, g, tiles, bank_of, acc)
                for j in range(G):
                    add(j)

            dve.wait_ge(rows_stored, 128)
            mean = sum_rows("mlp")
            dve.wait_ge(table_written, 16 * TABLE_PARTS)
            link(dve.memset(pos_part[:, :, :, 256:257], 1.0))

            def mlp_slot(g, b, tiles=None):
                if isinstance(g, int) and g == 3:
                    dve.wait_ge(acc_zeroed, 1)
                if has(g, 3):
                    dve.wait_ge(summed, g - 2)
                    add = adding("mlp", g - 3, tiles, lambda j: ps[:, 4 + j, 0:SUMS["mlp"]].unsqueeze(1),
                                 lambda t: mean[:, bass.ds(t, 1), :])
                for j in range(G):
                    if has(g, 3):
                        add(j)
                    if has(g):
                        if j == 0:
                            dve.wait_ge(edge_product, g + 1)
                            dve.wait_ge(gathered[b], 16 * G * (half(g, b) + 1))
                            if not early(g, 2):
                                dve.wait_ge(parts_ready, 3 * (g - 1))
                        ins = dve.tensor_tensor(pre[:, b, j, :], ps[:, 2 * b + j // 2, (j % 2) * 256:(j % 2) * 256 + 256],
                                                rows[:, b, j, :], ALU.add)
                if has(g):
                    ins.then_inc(pre_ready, 1)
                if has(g, 1):
                    q = 1 - b
                    if not early(g, 3):
                        dve.wait_ge(summed, g - 2)
                    make_onehot("mlp", g - 1, q, dst_rel)
                    dve.wait_ge(parts_ready, 3 * g)
                    dve.scalar_tensor_tensor(pos_part[:, q, :, 0:256], neg_part[:, q], -1.0,
                                             pos_part[:, q, :, 0:256], ALU.add, ALU.add)\
                       .then_inc(elu_ready, 1)
            slots(dve, mlp_slot, 3, head=4, tiles_of=(mybir.EngineType.DVE, 3))
            dve.wait_ge(accumulated, G * NG)
            link(dve.tensor_scalar(inv_row[:, :].unsqueeze(2), mean[:, :, 2 * P:2 * P + 1], 1.0, None, ALU.max))
            link(dve.reciprocal(inv_row[:, :], inv_row[:, :]))
            link(dve.tensor_tensor(mean, mean, inv_row[:, :].unsqueeze(2).to_broadcast([P, NT, SUMS["mlp"]]),
                                   ALU.mult))
            dve.sem_inc(mean_ready, 1)
            dve.wait_ge(x_rows_loaded, 16)
            for c in range(NCOL):
                if c < NPACK:
                    at = slice(packs(4)[c][0], packs(4)[c][-1] + 1)
                    dve.tensor_tensor(x_sb[:, at, :], x_sb[:, at, :],
                                      spread("b2b").unsqueeze(1).to_broadcast([P, len(packs(4)[c]), D]), ALU.add)\
                       .then_inc(bias_added, 1)
                for m in range(2):
                    u = 2 * c + m
                    dve.wait_ge(hid0_parts, 2 * (u + 1))
                    dve.wait_ge(read_by["act"], fills_read(FIRST_FILL["hid0"] + u + 1, "act"))
                    dve.scalar_tensor_tensor(big[:, m, c * COLS:(c + 1) * COLS], neg_node(u % 4), -1.0,
                                             pos_node(u % 4),
                                             ALU.add, ALU.add).then_inc(hid0_ready, 1)

            def per_node(a):
                return a.unsqueeze(2).to_broadcast([P, a.shape[1], D])

            def of_pack(u):
                return slice(packs(4)[u][0], packs(4)[u][-1] + 1)

            def bank_rows(name, u):
                return filled(name, u)[:, 0:len(packs(4)[u]) * D].rearrange("p (t f) -> p t f", f=D)

            def pause(u):
                pass

            def in_packs(*stages):
                for step in range(NPACK + len(stages) - 1):
                    for k in reversed(range(len(stages))):
                        if 0 <= step - k < NPACK:
                            stages[k](step - k)

            def norm(n, *makers):
                first = (n - 1) * NPACK

                def sum_rows_of(u):
                    dve.wait_ge(y_made, first + u + 1)
                    dve.tensor_reduce(stat[:, 0, of_pack(u)], y_sb[:, of_pack(u), :], AX_X, ALU.add)\
                       .then_inc(row_summed, 1)

                def center(u):
                    dve.wait_ge(row_summed, first + u + 1)
                    dve.scalar_tensor_tensor(y_sb[:, of_pack(u), :], per_node(stat[:, 0, of_pack(u)]), 1.0 / D,
                                             y_sb[:, of_pack(u), :], ALU.mult, ALU.subtract).then_inc(centered, 1)

                def sum_squares(u):
                    dve.wait_ge(squared, first + u + 1)
                    dve.tensor_reduce(stat[:, 2, of_pack(u)], spare.rearrange("p (t f) -> p t f", t=NT)[:, of_pack(u), :],
                                      AX_X, ALU.add).then_inc(squares_summed, 1)

                in_packs(*makers, sum_rows_of, center, pause, sum_squares)
                dve.wait_ge(squares_summed, first + NPACK)
                dve.tensor_scalar(stat[:, 2, :], stat[:, 2, :], 1.0 / D, EPS, ALU.mult, ALU.add).then_inc(var_ready, 1)
                dve.wait_ge(rooted, n)
                link(dve.reciprocal(stat[:, 0, :], stat[:, 1, :]))
                for u in range(NPACK):
                    dve.scalar_tensor_tensor(x_sb[:, of_pack(u), :], y_sb[:, of_pack(u), :], -1.0,
                                             per_node(stat[:, 0, of_pack(u)]), ALU.mult, ALU.mult).then_inc(x_ready, 1)
                dve.wait_ge(x_ready, first + NPACK)

            def join_mlp(u):
                dve.wait_ge(bias_added, u + 1)
                dve.tensor_tensor(y_sb[:, of_pack(u), :], bank_rows("out0", u), x_sb[:, of_pack(u), :], ALU.add)\
                   .then_inc(read_by["dve"], 1)

            def wait_for_join(u):
                dve.wait_ge(read_by["dve"], fills_read(FIRST_FILL["out0"] + u + 1, "dve"))
                dve.sem_inc(y_made, 1)

            norm(1, join_mlp, wait_for_join)

            def split_terms(k):
                n, heads = SOFTMAX[k]
                left = small[:, 0, 0:NT * heads].rearrange("p (t h) -> p t h", t=NT)
                part3 = small[:, 1, 0:NT * heads].rearrange("p (t h) -> p t h", t=NT)
                link(dve.tensor_copy(left, h_sb[:, :, D + heads:D + 2 * heads]))
                for i in range(3):
                    link(dve.tensor_copy(adst[:, :, i * heads:(i + 1) * heads], left))
                    if i < 2:
                        link(dve.tensor_copy(part3, adst[:, :, i * heads:(i + 1) * heads]))
                        link(dve.tensor_tensor(left, left, part3, ALU.subtract))
                dve.sem_inc(adst_ready, 1)

            def softmax_pass(k):
                n, heads = SOFTMAX[k]
                at, all_at, width = n * NG, base[k], SUMS[k]
                acc = sum_rows(k)
                zero(k, acc)
                dve.memset(max_run[:, :, 0:1], 0.0)
                dve.memset(s_run[:, 1, G * P - 1:G * P], 0.0)
                link(dve.memset(w_run[:, 1, G * P - 1:G * P], 0.0))
                loads_at = n * NG // 2

                def mark_nodes(x, b):
                    dve.wait_ge(rel_loaded[b], 16 * (loads_at + half(x, b) + 1))
                    if not early(x, 2):
                        dve.wait_ge(term_done, at + x - 1)
                    dve.tensor_scalar(rel_T[:, b, :], rel_b[:, b, :], part[:, 0:1], None, ALU.is_equal)\
                       .then_inc(rel_ready, 1)

                def weigh(x, b):
                    dve.wait_ge(exp_ready, at + x + 1)
                    if not early(x, 2):
                        dve.wait_ge(run_ready, at + x - 1)
                    value = ps[:, 2 + b, :] if heads else ps[:, b, :]
                    dve.tensor_tensor(hp[:, b, :], value, gaps[:, b, 1, :], ALU.mult).then_inc(hp_ready, 1)

                def run_weights(x, b):
                    if not early(x, 2):
                        dve.wait_ge(turn_done, at + x - 1)
                    dve.tensor_tensor_scan(s_run[:, b, :], gaps[:, b, 0, :], gaps[:, b, 1, :],
                                           s_run[:, 1 - b, G * P - 1:G * P], ALU.mult, ALU.add)

                def run_products(x, b):
                    dve.wait_ge(hp_ready, at + x + 1)
                    dve.tensor_tensor_scan(w_run[:, b, :], gaps[:, b, 0, :], hp[:, b, :], w_run[:, 1 - b, G * P - 1:G * P],
                                           ALU.mult, ALU.add).then_inc(run_ready, 1)

                def spread_value(b):
                    return ps[:, b, :]

                def run_max(x, b):
                    dve.wait_ge(neg_loaded[b], 16 * (loads_at + half(x, b) + 1))
                    if heads:
                        dve.wait_ge(logit_turned, at + x + 1)
                        if not early(x, 2):
                            dve.wait_ge(heads_turned, at + x - 1)
                    else:
                        dve.wait_ge(taken, at + x + 1)
                    if not early(x, 1):
                        dve.wait_ge(carry_ready, at + x)
                    dve.tensor_tensor_scan(max_run[:, b, 1:G * P + 1], neg_b[:, b, :], spread_value(b),
                                           max_run[:, b, 0:1], ALU.add, ALU.max).then_inc(max_ready, 1)

                def old_max(x, b):
                    dve.wait_ge(max_ready, at + x + 1)
                    if not early(x, 2):
                        dve.wait_ge(exp_ready, at + x - 1)
                    dve.tensor_tensor(rise[:, b, :], max_run[:, b, 0:G * P], neg_b[:, b, :], ALU.add)\
                       .then_inc(old_max_ready, 1)
                    dve.tensor_copy(max_run[:, 1 - b, 0:1], max_run[:, b, G * P:G * P + 1]).then_inc(carry_ready, 1)

                def rise_above(x, b):
                    dve.wait_ge(old_max_ready, at + x + 1)
                    dve.tensor_tensor(rise[:, b, :], spread_value(b), rise[:, b, :], ALU.subtract)\
                       .then_inc(rise_ready, 1)

                def of_edges(b, i):
                    return leaks[:, b, i, 0:G * heads].rearrange("p (g h) -> p g h", g=G)

                def join_parts(x, b):
                    dve.wait_ge(term_done, at + x + 1)
                    parts = ps[:, 5, TERMS[b]:TERMS[b] + G * 3 * heads].rearrange("p (g k h) -> p g h k", g=G, k=3)
                    dve.tensor_reduce(of_edges(b, 2), parts, AX_X, ALU.add).then_inc(dst_terms_ready, 1)

                def add_edge_terms(x, b):
                    dve.wait_ge(gathered[b], 16 * G * (loads_before(k) + half(x, b) + 1))
                    dve.wait_ge(dst_terms_ready, at + x + 1)
                    dve.tensor_tensor(of_edges(b, 0), of_edges(b, 2), rows[:, b, :, D:D + heads], ALU.add)\
                       .then_inc(terms_ready, 1)

                def leak(x, b):
                    dve.wait_ge(terms_ready, at + x + 1)
                    if not early(x, 2):
                        dve.wait_ge(logit_ready, at + x - 1)
                    dve.scalar_tensor_tensor(of_edges(b, 1), of_edges(b, 0), 0.2, of_edges(b, 0), ALU.mult, ALU.max)\
                       .then_inc(leak_ready, 1)

                def slot(s, b, tiles=None):
                    def add(j):
                        pass
                    if has(s, 5):
                        add = adding(k, s - 5, tiles, lambda j: ps[:, 6 + j // 2, (j % 2) * 256:(j % 2) * 256 + width]
                                     .unsqueeze(1), lambda t: acc[:, bass.ds(t, 1), :])
                    if has(s, 1) and heads:
                        join_parts(s - 1, 1 - b)
                    if has(s, 2):
                        run_max(s - 2, b)
                    if has(s, 1) and heads:
                        add_edge_terms(s - 1, 1 - b)
                    if has(s, 5):
                        dve.wait_ge(summed, all_at + s - 4)
                    add(0)
                    if has(s, 3):
                        weigh(s - 3, 1 - b)
                    if has(s, 1) and heads:
                        leak(s - 1, 1 - b)
                    add(1)
                    if has(s, 2):
                        old_max(s - 2, b)
                    if has(s) and heads:
                        mark_nodes(s, b)
                    if has(s, 2):
                        rise_above(s - 2, b)
                    add(2)
                    if has(s, 3):
                        run_weights(s - 3, 1 - b)
                    add(3)
                    if has(s, 3):
                        run_products(s - 3, 1 - b)
                slots(dve, slot, 5, head=6, tiles_of=(mybir.EngineType.DVE, 5))
                dve.wait_ge(accumulated, G * (all_at + NG))
                return acc

            def attention_output(k, acc, bias):
                n, heads = SOFTMAX[k]
                m = NT * heads

                def sm(i):
                    return small[:, i, 0:m].rearrange("p (t h) -> p t h", t=NT)

                total, top = acc[:, :, D:D + heads], acc[:, :, D + heads:D + 2 * heads]
                link(dve.tensor_tensor(sm(0), h_sb[:, :, D:D + heads], h_sb[:, :, D + heads:D + 2 * heads], ALU.add))
                link(dve.scalar_tensor_tensor(sm(1), sm(0), 0.2, sm(0), ALU.mult, ALU.max))
                link(dve.tensor_scalar(sm(0), total, 0.5, None, ALU.is_gt))
                link(dve.tensor_scalar(sm(0), sm(0), -1.0, -NEG, ALU.add, ALU.mult))
                link(dve.tensor_tensor(sm(0), sm(0), top, ALU.add))
                link(dve.tensor_tensor(sm(2), sm(0), sm(1), ALU.max))
                dve.tensor_tensor(sm(3), sm(0), sm(2), ALU.subtract)
                link(dve.tensor_tensor(sm(4), sm(1), sm(2), ALU.subtract))
                dve.drain().then_inc(gaps_in, 1)
                dve.wait_ge(gaps_out, n + 1)
                link(dve.tensor_tensor(sm(0), total, sm(3), ALU.mult))
                link(dve.tensor_tensor(sm(0), sm(0), sm(4), ALU.add))
                link(dve.tensor_scalar(sm(0), sm(0), 1e-16, None, ALU.add))
                link(dve.reciprocal(sm(0), sm(0)))
                dve.tensor_tensor(sm(3), sm(3), sm(0), ALU.mult)
                link(dve.tensor_tensor(sm(4), sm(4), sm(0), ALU.mult))
                loop = spare.rearrange("p (t f) -> p t f", t=NT)
                first = n * NPACK

                def over(a, u):
                    return a[:, of_pack(u), :].unsqueeze(2).to_broadcast([P, len(packs(4)[u]), D // heads, heads])

                def heads_of(a, u):
                    return a[:, of_pack(u), 0:D].rearrange("p t (f h) -> p t f h", h=heads)

                def weigh_edges(u):
                    dve.tensor_tensor(heads_of(y_sb, u), heads_of(acc, u), over(sm(3), u), ALU.mult)\
                       .then_inc(edges_weighed, 1)

                def weigh_loop(u):
                    dve.tensor_tensor(heads_of(loop, u), heads_of(h_sb, u), over(sm(4), u), ALU.mult)\
                       .then_inc(loops_weighed, 1)

                def add_loop(u):
                    dve.wait_ge(edges_weighed, first + u + 1)
                    dve.wait_ge(loops_weighed, first + u + 1)
                    dve.tensor_tensor(y_sb[:, of_pack(u), :], y_sb[:, of_pack(u), :], loop[:, of_pack(u), :], ALU.add)\
                       .then_inc(loops_added, 1)

                def add_bias(u):
                    dve.wait_ge(loops_added, first + u + 1)
                    row = spread(bias).unsqueeze(1).to_broadcast([P, len(packs(4)[u]), D])
                    dve.tensor_tensor(y_sb[:, of_pack(u), :], y_sb[:, of_pack(u), :], row, ALU.add)\
                       .then_inc(attended, 1)
                return weigh_edges, weigh_loop, add_loop, add_bias

            dve.wait_ge(read_by["act"], fills_read(FIRST_FILL["invT"], "act"))
            split_terms("gat1")

            def positive_side(u):
                dve.wait_ge(g_low, u + 1)
                dve.tensor_scalar(y_sb[:, of_pack(u), :], y_sb[:, of_pack(u), :], 0.0, None, ALU.max)\
                   .then_inc(positive_ready, 1)

            def join_elu(u):
                dve.wait_ge(positive_ready, u + 1)
                dve.scalar_tensor_tensor(y_sb[:, of_pack(u), :],
                                         spare.rearrange("p (t f) -> p t f", t=NT)[:, of_pack(u), :], -1.0,
                                         y_sb[:, of_pack(u), :], ALU.add, ALU.add).then_inc(g1_ready, 1)

            in_packs(*attention_output("gat1", softmax_pass("gat1"), "gb1"), pause, pause, positive_side, join_elu)
            dve.wait_ge(read_by["act"], fills_read(FIRST_FILL["x2T"], "act"))
            split_terms("gat2")

            def join_attention(u):
                dve.wait_ge(attended, NPACK + u + 1)
                dve.tensor_tensor(y_sb[:, of_pack(u), :], y_sb[:, of_pack(u), :], x_sb[:, of_pack(u), :], ALU.add)\
                   .then_inc(y_made, 1)

            norm(2, *attention_output("gat2", softmax_pass("gat2"), "gb2"), join_attention)

            def sum_pass(k, by_row):
                all_at = base[k]
                chunks = ROW[k] // P
                rows_acc = sum_rows(k) if by_row else None
                zero(k, rows_acc if by_row else big[:, 0:chunks, :])

                def slot(g, b, tiles=None):
                    if has(g):
                        if not early(g, 2):
                            dve.wait_ge(summed, all_at + g - 1)
                        make_onehot(k, g, b, dst_rel)
                    if has(g, 1):
                        q = 1 - b
                        dve.wait_ge(summed, all_at + g)
                        if by_row:
                            accumulate(k, g - 1, tiles, lambda j: ps[:, 4 + 2 * q + j // 2, (j % 2) * 256:(j % 2) * 256 + P]
                                       .unsqueeze(1), lambda t: rows_acc[:, bass.ds(t, 1), :])
                        else:
                            accumulate(k, g - 1, tiles, lambda j: ps[:, 4 + 2 * q + j // 2,
                                                              (j % 2) * 256:(j % 2) * 256 + chunks * P]
                                       .rearrange("p (c n) -> p c n", c=chunks),
                                       lambda t: big[:, 0:chunks, bass.ds(t * P, P)])
                slots(dve, slot, 1, tiles_of=(mybir.EngineType.DVE, 1))
                dve.wait_ge(accumulated, G * (all_at + NG))

            sum_pass("sage0", False)
            dve.tensor_tensor(big[:, 0, :], big[:, 0, :], inv_T[:, :], ALU.mult).then_inc(agg_scaled, 1)
            dve.wait_ge(table_written, 16 * 5 * TABLE_PARTS)
            sum_pass("sage1", False)
            dve.tensor_tensor(big[:, 0, :], big[:, 0, :], inv_T[:, :], ALU.mult)
            link(dve.tensor_tensor(big[:, 1, :], big[:, 1, :], inv_T[:, :], ALU.mult))
            dve.sem_inc(agg_scaled, 1)
            dve.wait_ge(read_by["act"], fills_read(FIRST_FILL["out2"], "act"))
            sum_pass("sage2", True)
            by_node = sum_rows("sage2")

            def scale_sums(u):
                dve.tensor_tensor(by_node[:, of_pack(u), :], by_node[:, of_pack(u), :],
                                  per_node(inv_row[:, of_pack(u)]), ALU.mult).then_inc(sums_scaled, 1)

            def join_sage(u):
                dve.wait_ge(sums_scaled, u + 1)
                dve.tensor_tensor(y_sb[:, of_pack(u), :], bank_rows("out2", u), by_node[:, of_pack(u), :], ALU.add)\
                   .then_inc(read_by["dve"], 1)

            def add_residual(u):
                dve.wait_ge(read_by["dve"], fills_read(FIRST_FILL["out2"] + u + 1, "dve"))
                dve.scalar_tensor_tensor(y_sb[:, of_pack(u), :], y_sb[:, of_pack(u), :], 0.0, x_sb[:, of_pack(u), :],
                                         ALU.max, ALU.add).then_inc(y_made, 1)

            norm(3, scale_sums, join_sage, add_residual)
            acc = softmax_pass("pool")
            def totals(u):
                return acc[:, of_pack(u), D:2 * D]

            def bound_totals(u):
                dve.tensor_scalar(totals(u), totals(u), 1.0, None, ALU.max).then_inc(totals_bounded, 1)

            def invert_totals(u):
                dve.wait_ge(totals_bounded, u + 1)
                dve.reciprocal(totals(u), totals(u)).then_inc(totals_inverted, 1)

            def divide(u):
                dve.wait_ge(totals_inverted, u + 1)
                dve.tensor_tensor(y_sb[:, of_pack(u), :], acc[:, of_pack(u), 0:D], totals(u), ALU.mult)\
                   .then_inc(agg3_ready, 1)

            def scale_output(u):
                dve.wait_ge(read_by["act"], fills_read(FIRST_FILL["last"] + 2 * u + 2, "act"))
                row = spread("scale").unsqueeze(1).to_broadcast([P, len(packs(4)[u]), D])
                dve.tensor_tensor(y_sb[:, of_pack(u), :], y_sb[:, of_pack(u), :], row, ALU.mult).then_inc(y_half, 1)

            def add_both_residuals(u):
                dve.wait_ge(y_half, u + 1)
                dve.scalar_tensor_tensor(y_sb[:, of_pack(u), :], x_sb[:, of_pack(u), :], 2.0, y_sb[:, of_pack(u), :],
                                         ALU.mult, ALU.add).then_inc(y_made, 1)

            dve.wait_ge(table_written, 16 * 7 * TABLE_PARTS)
            norm(4, bound_totals, invert_totals, divide, pause, scale_output, add_both_residuals)


def lay_out(inputs):
    import numpy as np

    a = {k: np.asarray(v) for k, v in inputs.items()}
    n = NCH * CH * P
    src = np.zeros(n, np.int32)
    src[:N_EDGES] = a["src"]
    dst = np.full(n + 2, PAD_NODE, np.int32)
    dst[0] = -1
    dst[1:1 + N_EDGES] = a["dst"]
    dst[-1] = -1
    tables = [src, dst[1:-1], dst[:-2], dst[2:]]
    edges_i = np.ascontiguousarray(np.stack(tables).reshape(4, NCH, CH, P).transpose(2, 0, 1, 3)).reshape(CH, -1)
    ea = np.zeros((NB * P, D), np.float32)
    ea[:N_EDGES] = a["edge_attr_128"]
    ea_blocks = np.ascontiguousarray(ea.reshape(NB, P, D).transpose(0, 2, 1))
    x_rows = np.zeros((NODES, D), np.float32)
    x_rows[:N_NODES] = a["x"]

    def head_last(w, axis):
        shape = list(w.shape)
        if w.shape == (HEADS, D // HEADS):
            return w.T
        cut_shape = shape[:axis] + [HEADS, D // HEADS] + shape[axis + 1:]
        return np.swapaxes(w.reshape(cut_shape), axis, axis + 1).reshape(shape)

    gW1, gW2 = head_last(a["L1_gnn_W1"], 1), head_last(a["L1_gnn_W2"], 0)
    weights = {"W1a": a["L0_gnn_W1a"], "W1bT": a["L0_gnn_W1b"].T, "W2a": a["L0_gnn_W2a"], "W2b": a["L0_gnn_W2b"],
               "gW1": gW1, "gW2": gW2, "gW1T": gW1.T, "gW2T": gW2.T, "b1b": a["L0_gnn_b1b"].reshape(2, P).T,
               "att1": np.stack([head_last(a["L1_gnn_att_src1"], 0).reshape(P),
                                 head_last(a["L1_gnn_att_dst1"], 0).reshape(P)], axis=1),
               "att2": np.stack([a["L1_gnn_att_src2"].reshape(P), a["L1_gnn_att_dst2"].reshape(P)], axis=1),
               "Ws0": a["L2_gnn_Ws0"], "Wn0": a["L2_gnn_Wn0"],
               "Ws1": a["L2_gnn_Ws1"], "Wn1": a["L2_gnn_Wn1"], "Ws2": a["L2_gnn_Ws2"], "Wn2": a["L2_gnn_Wn2"],
               "mlpT": a["L3_gnn_mlp_w"].T, "b2a": a["L0_gnn_b2a"].reshape(2, P).T,
               "sb0": a["L2_gnn_b0"].reshape(2, P).T, "sb1": a["L2_gnn_b1"].reshape(2, P).T}
    cols = []
    for name, (c, m) in WEIGHTS.items():
        cols.append(weights[name].reshape(c, P, m).transpose(1, 0, 2).reshape(P, c * m))
    bias = {"sb2": a["L2_gnn_b2"],
            "mlp_b": a["L3_gnn_mlp_b"]}
    spread = {"b1a": a["L0_gnn_b1a"], "b2b": a["L0_gnn_b2b"], "gb1": head_last(a["L1_gnn_b1"], 0), "gb2": a["L1_gnn_b2"], "scale": a["L3_gnn_scale"]}
    return {
        "edges_i": edges_i, "ea_blocks": ea_blocks, "x_rows": x_rows, "xT_in": np.ascontiguousarray(x_rows.T),
        "wpack": np.ascontiguousarray(np.concatenate(cols, axis=1)),
        "bpack": np.concatenate([bias[k].reshape(-1) for k in BIAS_ROWS]).reshape(1, -1),
        "rpack": np.concatenate([spread[k].reshape(-1) for k in SPREAD_ROWS]).reshape(1, -1),
    }


def kernel(**inputs):
    import concourse.bacc as _bacc
    from concourse import mybir as _mybir
    from concourse.bass_utils import run_bass_kernel_spmd as _run

    nc = _bacc.Bacc("TRN2", target_bir_lowering=False, num_devices=1)
    arrays, args = {}, []
    for name, a in lay_out(inputs).items():
        arrays[f"in_{name}"] = a
        args.append(nc.dram_tensor(f"in_{name}", a.shape, _mybir.dt.from_np(a.dtype), kind="ExternalInput").ap())
    args.append(nc.dram_tensor("out_0", (N_NODES, D), F32, kind="ExternalOutput").ap())
    program(nc, *args)
    r = _run(nc, [arrays], core_ids=[0])
    return r.results[0]["out_0"]
```
